# Optimizing a Trainium2 kernel written in Bass

```python
import numpy as np
import jax
import jax.numpy as jnp

def _softmax(x, axis=-1):
    return jax.nn.softmax(x, axis=axis)

def _gelu(x):
    return jax.nn.gelu(x, approximate=True)

def _silu(x):
    return jax.nn.silu(x)

def _sigmoid(x):
    return jax.nn.sigmoid(x)

def _layernorm(x, axis=-1, eps=1e-05):
    m = jnp.mean(x, axis=axis, keepdims=True)
    v = jnp.var(x, axis=axis, keepdims=True)
    return (x - m) / jnp.sqrt(v + eps)

def _scatter_add(tgt, idx, src, axis=0):
    return tgt.at[idx].add(src)

def _segment_sum(src, seg, n):
    return jax.ops.segment_sum(src, seg, n)
kernel_name = 'mk_xattn_ffn_d2_seqx_r4_a46ce4'

def setup_inputs(seed: int=0):
    np.random.seed(seed)
    _w = jnp.asarray

    def _rec_inputs():
        import jax
        import jax.numpy as jnp
        _rk = jax.random.key(seed)
        x = -0.0002928 + 1 * jax.random.normal(jax.random.fold_in(_rk, 1), (4, 512, 256), jnp.float32)
        _lenS = 512 - jax.random.randint(jax.random.fold_in(_rk, 7), (4,), 0, max(1, 512 // 4) + 1, jnp.int32)
        _lenS2 = 1601 - jax.random.randint(jax.random.fold_in(_rk, 8), (4,), 0, max(1, 1601 // 4) + 1, jnp.int32)
        _ctx_1024P = jax.random.normal(jax.random.fold_in(_rk, 11), (4, 16, 256), jnp.float32)
        _ctx_1024c = jax.random.dirichlet(jax.random.fold_in(_rk, 511), 0.3 * jnp.ones((16,), jnp.float32), (4, 1601))
        _ctx_1024t = jnp.einsum('bsk,bkd->bsd', _ctx_1024c, _ctx_1024P)
        _ctx_1024t = _ctx_1024t * jax.lax.rsqrt(jnp.mean(jnp.square(_ctx_1024t)) + 1e-12) * 0.953939
        ctx_1024 = 4.13588e-05 + 0.999923 * (_ctx_1024t + 0.3 * jax.random.normal(jax.random.fold_in(_rk, 611), (4, 1601, 256), jnp.float32))
        _validS = jnp.arange(512)[None, :] < _lenS[:, None]
        _validS2 = jnp.arange(1601)[None, :] < _lenS2[:, None]
        _causal = jnp.tril(jnp.ones((512, 512), dtype=bool))
        mask_BxS2_bf1 = jnp.ones((4, 1601), dtype=bool)
        return (x, ctx_1024, mask_BxS2_bf1)
    x, ctx_1024, mask_BxS2_bf1 = _rec_inputs()

    def _L0_xattn_setup():
        import jax, jax.numpy as jnp
        import numpy as np
        B, TQ, TK, D, H = (4, 256, 512, 256, 16)
        HD = D // H

        def _to_heads(t):
            Bx, T, _ = t.shape
            return t.reshape(Bx, T, H, HD).transpose(0, 2, 1, 3)
        key = jax.random.key(seed)
        ks = jax.random.split(key, 8)

        def xavier(k, shape):
            fan_in, fan_out = (shape[0], shape[1])
            limit = float(np.sqrt(6.0 / (fan_in + fan_out)))
            return jax.random.uniform(k, shape, jnp.float32, -limit, limit)
        return {'x': jax.random.normal(ks[0], (B, TQ, D), jnp.float32), 'memory': jax.random.normal(ks[1], (B, TK, D), jnp.float32), 'memory_padding_mask': jnp.ones((B, TK), dtype=bool), 'W_q': xavier(ks[2], (D, D)), 'b_q': jnp.zeros((D,), jnp.float32), 'W_kv': xavier(ks[3], (D, 2 * D)), 'b_kv': jnp.zeros((2 * D,), jnp.float32), 'W_o': xavier(ks[4], (D, D)), 'b_o': jnp.zeros((D,), jnp.float32)}
    _L0_xattn_all = _L0_xattn_setup()
    _L0_xattn_in = {k: v for k, v in _L0_xattn_all.items() if k in ('W_q', 'b_q', 'W_kv', 'b_kv', 'W_o', 'b_o')}
    del _L0_xattn_all

    def _L0_ffn_setup():
        import jax, jax.numpy as jnp
        import numpy as np
        DIM = 256
        HIDDEN = 768
        SCALE = 1.0 / 127.0

        def _dequant(w_int, dtype):
            return w_int.astype(dtype) * jnp.asarray(SCALE, dtype)
        key = jax.random.key(seed)
        k_x, k_g, k_u, k_d = jax.random.split(key, 4)
        x = jax.random.normal(k_x, (4, 512, DIM), dtype=jnp.float32)
        w_gate = jax.random.randint(k_g, (HIDDEN, DIM), -127, 128, dtype=jnp.int32)
        w_up = jax.random.randint(k_u, (HIDDEN, DIM), -127, 128, dtype=jnp.int32)
        w_down = jax.random.randint(k_d, (DIM, HIDDEN), -127, 128, dtype=jnp.int32)
        return {'x': x, 'w_gate': w_gate, 'w_up': w_up, 'w_down': w_down}
    _L0_ffn_all = _L0_ffn_setup()
    _L0_ffn_in = {k: v for k, v in _L0_ffn_all.items() if k in ('w_gate', 'w_up', 'w_down')}
    del _L0_ffn_all

    def _L1_xattn_setup():
        import jax, jax.numpy as jnp
        import numpy as np
        D_MODEL = 256
        N_HEADS = 16
        D_K = D_MODEL // N_HEADS
        key = jax.random.key(seed)
        ks = jax.random.split(key, 7)
        B, S = (4, 512)
        scale = 1.0 / np.sqrt(D_MODEL)
        return {'query': jax.random.normal(ks[0], (B, S, D_MODEL), dtype=jnp.float32), 'key': jax.random.normal(ks[1], (B, S, D_MODEL), dtype=jnp.float32), 'value': jax.random.normal(ks[2], (B, S, D_MODEL), dtype=jnp.float32), 'W_q': jax.random.normal(ks[3], (D_MODEL, D_MODEL), dtype=jnp.float32) * scale, 'W_k': jax.random.normal(ks[4], (D_MODEL, D_MODEL), dtype=jnp.float32) * scale, 'W_v': jax.random.normal(ks[5], (D_MODEL, D_MODEL), dtype=jnp.float32) * scale, 'W_o': jax.random.normal(ks[6], (D_MODEL, D_MODEL), dtype=jnp.float32) * scale}
    _L1_xattn_all = _L1_xattn_setup()
    _L1_xattn_in = {k: v for k, v in _L1_xattn_all.items() if k in ('W_q', 'W_k', 'W_v', 'W_o')}
    del _L1_xattn_all

    def _L1_ffn_setup():
        import jax, jax.numpy as jnp
        import numpy as np
        B, T, D = (2, 512, 256)
        E, K, FF = (8, 2, 1024)

        def _reference_tuple_inner(x, gate_w, gate_b, w1, b1, w2, b2):
            n_experts = w1.shape[0]
            gate_logits = x @ gate_w + gate_b
            topk_vals, topk_idx = jax.lax.top_k(gate_logits, K)
            topk_w = jax.nn.softmax(topk_vals, axis=-1)
            onehot = jax.nn.one_hot(topk_idx, n_experts, dtype=x.dtype)
            comb = jnp.sum(onehot * topk_w[..., None], axis=2)
            h = jax.nn.gelu(jnp.einsum('btd,edf->ebtf', x, w1) + b1[:, None, None, :], approximate=False)
            y = jnp.einsum('ebtf,efd->ebtd', h, w2) + b2[:, None, None, :]
            output = jnp.einsum('ebtd,bte->btd', y, comb)
            expert_counts = jnp.sum(onehot, axis=(0, 1, 2)).astype(jnp.float32)
            return (output, gate_logits, topk_idx, expert_counts)
        key = jax.random.key(seed)
        ks = jax.random.split(key, 4)
        scale = 0.02
        return {'x': jax.random.normal(ks[0], (B, T, D), jnp.float32), 'gate_w': jax.random.normal(ks[1], (D, E), jnp.float32) * scale, 'gate_b': jnp.zeros((E,), jnp.float32), 'w1': jax.random.normal(ks[2], (E, D, FF), jnp.float32) * scale, 'b1': jnp.zeros((E, FF), jnp.float32), 'w2': jax.random.normal(ks[3], (E, FF, D), jnp.float32) * scale, 'b2': jnp.zeros((E, D), jnp.float32)}
    _L1_ffn_all = _L1_ffn_setup()
    _L1_ffn_in = {k: v for k, v in _L1_ffn_all.items() if k in ('gate_w', 'gate_b', 'w1', 'b1', 'w2', 'b2')}
    del _L1_ffn_all
    return {'x': x, 'ctx_1024': ctx_1024, 'mask_BxS2_bf1': mask_BxS2_bf1, 'L0_xattn_W_q': _L0_xattn_in['W_q'], 'L0_xattn_b_q': _L0_xattn_in['b_q'], 'L0_xattn_W_kv': _L0_xattn_in['W_kv'], 'L0_xattn_b_kv': _L0_xattn_in['b_kv'], 'L0_xattn_W_o': _L0_xattn_in['W_o'], 'L0_xattn_b_o': _L0_xattn_in['b_o'], 'L0_ffn_w_gate': _L0_ffn_in['w_gate'], 'L0_ffn_w_up': _L0_ffn_in['w_up'], 'L0_ffn_w_down': _L0_ffn_in['w_down'], 'L1_xattn_W_q': _L1_xattn_in['W_q'], 'L1_xattn_W_k': _L1_xattn_in['W_k'], 'L1_xattn_W_v': _L1_xattn_in['W_v'], 'L1_xattn_W_o': _L1_xattn_in['W_o'], 'L1_ffn_gate_w': _L1_ffn_in['gate_w'], 'L1_ffn_gate_b': _L1_ffn_in['gate_b'], 'L1_ffn_w1': _L1_ffn_in['w1'], 'L1_ffn_b1': _L1_ffn_in['b1'], 'L1_ffn_w2': _L1_ffn_in['w2'], 'L1_ffn_b2': _L1_ffn_in['b2']}

def reference(x, ctx_1024, mask_BxS2_bf1, L0_xattn_W_q, L0_xattn_b_q, L0_xattn_W_kv, L0_xattn_b_kv, L0_xattn_W_o, L0_xattn_b_o, L0_ffn_w_gate, L0_ffn_w_up, L0_ffn_w_down, L1_xattn_W_q, L1_xattn_W_k, L1_xattn_W_v, L1_xattn_W_o, L1_ffn_gate_w, L1_ffn_gate_b, L1_ffn_w1, L1_ffn_b1, L1_ffn_w2, L1_ffn_b2):
    import jax
    import jax.numpy as jnp

    def _L0_xattn_ref(x, memory, memory_padding_mask, W_q, b_q, W_kv, b_kv, W_o, b_o):
        import jax, jax.numpy as jnp
        import numpy as np
        B, TQ, TK, D, H = (4, 256, 512, 256, 16)
        HD = D // H

        def _to_heads(t):
            Bx, T, _ = t.shape
            return t.reshape(Bx, T, H, HD).transpose(0, 2, 1, 3)
        q = x @ W_q + b_q
        kv = memory @ W_kv + b_kv
        k, v = (kv[..., :D], kv[..., D:])
        q = _to_heads(q)
        k = _to_heads(k)
        v = _to_heads(v)
        scores = jnp.einsum('bhqd,bhkd->bhqk', q, k) * (1.0 / np.sqrt(HD))
        pad = ~memory_padding_mask
        scores = jnp.where(pad[:, None, None, :], -jnp.inf, scores)
        A = jax.nn.softmax(scores, axis=-1)
        ctx = jnp.einsum('bhqk,bhkd->bhqd', A, v)
        y = ctx.transpose(0, 2, 1, 3).reshape(x.shape[0], x.shape[1], D)
        return y @ W_o + b_o

    def _L0_ffn_ref(x, w_gate, w_up, w_down):
        import jax, jax.numpy as jnp
        import numpy as np
        DIM = 256
        HIDDEN = 768
        SCALE = 1.0 / 127.0

        def _dequant(w_int, dtype):
            return w_int.astype(dtype) * jnp.asarray(SCALE, dtype)
        wg = _dequant(w_gate, x.dtype)
        wu = _dequant(w_up, x.dtype)
        wd = _dequant(w_down, x.dtype)
        gate = jnp.einsum('bsd,hd->bsh', x, wg)
        up = jnp.einsum('bsd,hd->bsh', x, wu)
        h = jax.nn.silu(gate) * up
        return jnp.einsum('bsh,dh->bsd', h, wd)

    def _L1_xattn_ref(query, key, value, W_q, W_k, W_v, W_o):
        import jax, jax.numpy as jnp
        import numpy as np
        D_MODEL = 256
        N_HEADS = 16
        D_K = D_MODEL // N_HEADS
        B, S, _ = query.shape
        Q = query @ W_q.T
        K = key @ W_k.T
        V = value @ W_v.T
        Q = Q.reshape(B, S, N_HEADS, D_K).transpose(0, 2, 1, 3)
        K = K.reshape(B, -1, N_HEADS, D_K).transpose(0, 2, 1, 3)
        V = V.reshape(B, -1, N_HEADS, D_K).transpose(0, 2, 1, 3)
        scores = jnp.einsum('bhqd,bhkd->bhqk', Q, K) / jnp.sqrt(jnp.float32(D_K))
        weights = jax.nn.softmax(scores, axis=-1)
        attn = jnp.einsum('bhqk,bhkd->bhqd', weights, V)
        attn = attn.transpose(0, 2, 1, 3).reshape(B, S, D_MODEL)
        return attn @ W_o.T

    def _L1_ffn_ref(x, gate_w, gate_b, w1, b1, w2, b2):
        import jax, jax.numpy as jnp
        import numpy as np
        B, T, D = (2, 512, 256)
        E, K, FF = (8, 2, 1024)

        def _reference_tuple_inner(x, gate_w, gate_b, w1, b1, w2, b2):
            n_experts = w1.shape[0]
            gate_logits = x @ gate_w + gate_b
            topk_vals, topk_idx = jax.lax.top_k(gate_logits, K)
            topk_w = jax.nn.softmax(topk_vals, axis=-1)
            onehot = jax.nn.one_hot(topk_idx, n_experts, dtype=x.dtype)
            comb = jnp.sum(onehot * topk_w[..., None], axis=2)
            h = jax.nn.gelu(jnp.einsum('btd,edf->ebtf', x, w1) + b1[:, None, None, :], approximate=False)
            y = jnp.einsum('ebtf,efd->ebtd', h, w2) + b2[:, None, None, :]
            output = jnp.einsum('ebtd,bte->btd', y, comb)
            expert_counts = jnp.sum(onehot, axis=(0, 1, 2)).astype(jnp.float32)
            return (output, gate_logits, topk_idx, expert_counts)
        return _reference_tuple_inner(x, gate_w, gate_b, w1, b1, w2, b2)[0]
    x = x + _L0_xattn_ref(_layernorm(x, axis=-1), ctx_1024, mask_BxS2_bf1, L0_xattn_W_q, L0_xattn_b_q, L0_xattn_W_kv, L0_xattn_b_kv, L0_xattn_W_o, L0_xattn_b_o)
    x = x + _L0_ffn_ref(_layernorm(x, axis=-1), L0_ffn_w_gate, L0_ffn_w_up, L0_ffn_w_down)
    x = x + _L1_xattn_ref(_layernorm(x, axis=-1), ctx_1024, ctx_1024, L1_xattn_W_q, L1_xattn_W_k, L1_xattn_W_v, L1_xattn_W_o)
    x = x + _L1_ffn_ref(_layernorm(x, axis=-1), L1_ffn_gate_w, L1_ffn_gate_b, L1_ffn_w1, L1_ffn_b1, L1_ffn_w2, L1_ffn_b2)
    return x

_drawn_inputs = setup_inputs


def setup_inputs(seed=0):
    import zlib

    import numpy as np

    out = dict(_drawn_inputs(seed))
    spreads = {'L0_xattn_b_q': (0.0, 0.462),
     'L0_xattn_b_kv': (0.0, 0.1),
     'L0_xattn_b_o': (0.0, 0.1),
     'L1_ffn_gate_b': (0.0, 2.0),
     'L1_ffn_b1': (0.0, 2.0),
     'L1_ffn_b2': (0.0, 2.0)}
    factors = {'L1_xattn_W_q': 8.0,
     'L1_xattn_W_k': 8.0,
     'L1_xattn_W_v': 8.0,
     'L1_xattn_W_o': 8.0,
     'L1_ffn_gate_w': 63.512,
     'L1_ffn_w1': 64.0,
     'L1_ffn_w2': 56.85}
    for name, (base, spread) in spreads.items():
        noise = np.random.default_rng([zlib.crc32(name.encode()), seed]).standard_normal(out[name].shape)
        drawn = base * np.exp(spread * noise) if base else spread * noise
        out[name] = jnp.asarray(drawn.astype(out[name].dtype))
    for name, factor in factors.items():
        out[name] = (out[name] * factor).astype(out[name].dtype)
    return out
```

```python
from contextlib import ExitStack

import concourse.bass as bass
from concourse import mybir

ALU = mybir.AluOpType
ACT = mybir.ActivationFunctionType
AX = mybir.AxisListType
F32 = mybir.dt.float32
BF16 = mybir.dt.bfloat16
I32 = mybir.dt.int32
U32 = mybir.dt.uint32
U8 = mybir.dt.uint8

P = 128
B, S, D = 4, 512, 256
H, HD = 16, 16
KV = 1601
KVP = KV + 1
KT = -(-KV // P)
LAST = KV - (KT - 1) * P
DK = D // P
NT = B * S // P
QT = S // P
HG = 4
NG = H // HG
TERMS = 6
ROW_MASK = TERMS * HD
ROW_C = ROW_MASK + 1
ROWS = ROW_C + 2
MASKED = -1.0e30
CLAMP = -1.0e20
EPS = 1e-5
FF0 = 768
E, FF = 8, 1024
INV127 = 1.0 / 127.0

CHUNK = 401
CHUNK_AT = [0, 400, 800, 1200]
NCHUNK = HG * QT * len(CHUNK_AT)
LEAD = 20
NS = KT * HG
KCH = [(0, 401), (401, 400), (801, 400), (1201, 400)]
VPART = [(0, 7), (7, 13)]

JOBS = [
    (0, 1, "v", (3, 0)), (0, 2, "norm", 0), (0, 3, "v", (3, 1)), (0, 4, "ot", 0), (0, 5, "ot", 1),
    (0, 6, "out", 0), (0, 7, "out", 1), (0, 8, "xt", 0), (0, 9, "xt", 1), (0, 10, "mx", 0), (0, 11, "q", 0),
    (0, 12, "q", 1),
    (1, 2, "norm", 1), (1, 3, "k", (0, 0)), (1, 5, "k", (0, 1)), (1, 6, "k", (0, 2)), (1, 7, "k", (0, 3)),
    (1, 8, "v", (0, 0)), (1, 10, "mx", 1), (1, 11, "v", (0, 1)),
    (2, 2, "norm", 2), (2, 4, "v", (1, 0)), (2, 7, "v", (1, 1)), (2, 10, "mx", 2),
    (3, 2, "norm", 3), (3, 3, "v", (2, 0)), (3, 4, "v", (2, 1)), (3, 5, "k", (1, 0)), (3, 6, "k", (1, 1)),
    (3, 7, "k", (1, 2)), (3, 8, "k", (1, 3)), (3, 10, "mx", 3),
]
PROLOGUE = (
    [("xt", 0), ("xt", 1), ("q", 0), ("q", 1)]
    + [("k", (0, c)) for c in range(4)] + [("k", (1, c)) for c in range(4)]
    + [("v", (s, p)) for s in range(3) for p in range(2)] + [("mx", -1)]
)
TAIL = [("norm", 4), ("ot", 0), ("ot", 1), ("out", 0), ("out", 1)]
BEHIND = ("ot", "out")
ON_ACT = ("xt", "q", "k", "ot")
AHEAD = ("xt", "q", "k")


def jobs_of(first, last):
    out = []
    for g, kt, job, arg in JOBS:
        if first and ((job == "norm" and g == 0) or job in BEHIND):
            continue
        if last and (job in AHEAD or (job == "v" and arg[0] < 3) or (job == "mx" and g == 3)):
            continue
        out.append((g, kt, job, arg))
    return out


def jobs_before(b, first):
    return len(PROLOGUE) + (0 if first else b * len(JOBS) - 5)


def chunks_at(g, kt, last):
    lo, hi = LEAD + 5 * kt, LEAD + min(5 * kt + 5, NCHUNK)
    out = [(g + 1 + r // NCHUNK, r % NCHUNK) for r in range(lo, hi)]
    return [(t, i) for t, i in out if not (last and t >= NG)]


def attention(nc, name, x, ident, k_rows, q_rows, ctxT, w_q, w_k, w_v, w_o, b_q, b_k, b_v, b_o, mask):
    with ExitStack() as ctx:
        sb = lambda n, s, d=F32: ctx.enter_context(nc.sbuf_tensor(f"{name}_{n}", s, d))
        ps = lambda n, s: ctx.enter_context(nc.psum_tensor(f"{name}_{n}", s, F32))
        sem = lambda n: nc.alloc_semaphore(f"{name}_{n}")

        sc, mxp = ps("sc", [P, 3, 512]), ps("mxp", [P, 3, 512])
        avp, misc = ps("avp", [P, 512]), ps("misc", [P, 512])

        KS = sb("KS", [ROWS, NG, HG, KVP], BF16)
        QS = sb("QS", [ROWS, NG, HG, S], BF16)
        V = sb("V", [P, NG, KT, HG, 32])
        pr = sb("pr", [P, 3, HG, S])
        ctx_sb = sb("ctx", [P, DK, KV])
        wq, wk, wv = (sb(n, [P, DK, D]) for n in ("wq", "wk", "wv"))
        wo = sb("wo", [P, DK, D])
        bq, bk = sb("bq", [P, 2]), sb("bk", [P, 2])
        bv = sb("bv", [P, D])
        kf, idle = sb("kf", [P, KV]), sb("idle", [P, 5])
        kparts = sb("kparts", [P, 3, KVP], BF16)
        qf = sb("qf", [P, 2, S])
        qparts = sb("qparts", [P, 3, 2, S], BF16)
        xn, xnT = sb("xn", [P, QT, D]), sb("xnT", [P, DK, S])
        mx, mxr = sb("mx", [P, 2, NCHUNK]), sb("mxr", [P, 2, HG * QT])
        cneg, chi, clo = sb("cneg", [16, P]), sb("chi", [16, P], BF16), sb("clo", [16, P], BF16)
        osb, rden = sb("osb", [P, S]), sb("rden", [P, QT, HG])
        on = sb("on", [P, QT, D])
        oT = sb("oT", [P, DK, S])
        bo = sb("bo", [P, D])
        st, mv = sb("st", [P, NT, 6]), sb("mv", [P, NT, 2])
        eps, ve, rs, tmp = sb("eps", [P, 1]), sb("ve", [P, NT]), sb("rs", [P, NT]), sb("tmp", [P, 2, NT])
        nmask = 0
        if mask is not None:
            nmask = 16
            mrow = sb("mrow", [B, KVP], U8)
            mbias = kparts[0:B, 0, :]
            mbias_dram = nc.dram_tensor(f"{name}_mbias", [B, HG, KVP], BF16, kind="Internal").ap()

        weights_in, mask_in, mask_out = sem("weights_in"), sem("mask_in"), sem("mask_out")
        ctx_in = sem("ctx_in")
        setup_v, rows_in = sem("setup_v"), sem("rows_in")
        ln_v, ln_s = sem("ln_v"), sem("ln_s")
        xn_done = sem("xn_done")
        misc_full, misc_free = sem("misc_full"), sem("misc_free")
        split_step, gated, restack_go = sem("split_step"), sem("gated"), sem("restack_go")
        k_in = [sem(f"k_in{s}") for s in range(NG)]
        q_in = [sem(f"q_in{s}") for s in range(NG)]
        c_in = [sem(f"c_in{s}") for s in range(NG)]
        max_ready, max_done, rowmax_done, c_step = sem("max_ready"), sem("max_done"), sem("rowmax_done"), sem("c_step")
        score_ready, exp_done, av_done = sem("score_ready"), sem("exp_done"), sem("av_done")
        osb_done, rden_done, bias_done = sem("osb_done"), sem("rden_done"), sem("bias_done")
        WEIGHTS_IN = 16 * (4 if b_o is None else 8)
        K_IN, Q_IN, C_IN = 16 * TERMS + nmask, 16 * TERMS, 32
        SPLITS = {("q", 0): 0, ("q", 1): 1, ("k", 0): 2, ("k", 1): 3}

        def split_count(n, kind, half):
            return 16 * n + 4 * (SPLITS[kind, half] + 1)

        block = ctx.enter_context(nc.Block())

        @block.sync
        def _(sp):
            sp.dma_start(KS[ROW_MASK:ROWS, :, :, :].bitcast(U32).rearrange("r g h n -> r (g h n)"), k_rows).then_inc(rows_in, 16)
            sp.dma_start(QS[ROW_MASK:ROWS, :, :, :].bitcast(U32).rearrange("r g h n -> r (g h n)"), q_rows).then_inc(rows_in, 16)
            if b_o is not None:
                sp.dma_start(bq[:, :], b_q).then_inc(weights_in, 16)
                sp.dma_start(bk[:, :], b_k).then_inc(weights_in, 16)
                sp.dma_start(bv[:, :], b_v.partition_broadcast(P)).then_inc(weights_in, 16)
                sp.dma_start(bo[:, :], b_o.partition_broadcast(P)).then_inc(weights_in, 16)
            for w, src in ((wq, w_q), (wk, w_k), (wv, w_v), (wo, w_o)):
                sp.dma_start(w[:, :, :], src.rearrange("(k p) n -> p k n", p=P)).then_inc(weights_in, 16)

            def load_context(n):
                sp.dma_start(ctx_sb[:, :, :], ctxT[n].rearrange("(k p) n -> p k n", p=P)
                             if isinstance(n, int) else ctxT[bass.ds(n, 1)].rearrange("o (k p) n -> p (o k) n", p=P)
                             ).then_inc(ctx_in, 16)

            load_context(0)
            if mask is not None:
                sp.dma_start(mrow[:, 0:KV], mask).then_inc(mask_in, 16)
                sp.wait_ge(setup_v, 4)
                for h in range(HG):
                    sp.dma_start(mbias_dram[:, h, :], mbias).then_inc(mask_out, 16)
                sp.wait_ge(mask_out, 16 * HG)

            def restack(n, s):
                sp.wait_ge(restack_go, NG * n + s + 1)
                for t, part in enumerate((0, 1, 2, 0, 1, 0)):
                    sp.dma_start(QS[HD * t:HD * t + HD, s, :, :],
                                 qparts[64 * (s % 2):64 * (s % 2) + 64, part, s // 2, :]).then_inc(q_in[s], 16)
                for t, part in enumerate((0, 0, 0, 1, 1, 2)):
                    sp.dma_start(KS[HD * t:HD * t + HD, s, :, 0:KV],
                                 kparts[64 * (s % 2):64 * (s % 2) + 64, part, 0:KV]).then_inc(k_in[s], 16)
                if mask is not None:
                    src = mbias_dram[n:n + 1] if isinstance(n, int) else mbias_dram[bass.ds(n, 1)]
                    sp.dma_start(KS[ROW_MASK:ROW_MASK + 1, s, :, :], src).then_inc(k_in[s], 16)

            def shifts(G, s):
                sp.wait_ge(c_step, 2 * (G + 1))
                row = QS[ROW_C:ROW_C + 1, s, :, :].rearrange("o h (t n) -> o (h t) n", n=P)
                sp.dma_start(row, chi[:, :]).then_inc(c_in[s], 16)
                row = QS[ROW_C + 1:ROW_C + 2, s, :, :].rearrange("o h (t n) -> o (h t) n", n=P)
                sp.dma_start(row, clo[:, :]).then_inc(c_in[s], 16)

            sp.wait_ge(rows_in, 32)
            for s in range(3):
                restack(0, s)
            shifts(0, 0)

            def body(b, first, last):
                restack(b, 3)
                shifts(NG * b + 1, 1)
                if not last:
                    load_context(b + 1)
                shifts(NG * b + 2, 2)
                if not last:
                    restack(b + 1, 0)
                    restack(b + 1, 1)
                shifts(NG * b + 3, 3)
                if not last:
                    shifts(NG * b + 4, 0)
                    restack(b + 1, 2)

            body(0, True, False)
            with sp.Fori(1, B - 1) as b:
                body(b, False, False)
            body(B - 1, False, True)

        @block.gpsimd
        def _(pool):
            nc.gpsimd.memset(idle[:, :], 0.0).then_inc(gated, 1)

            def gate(i):
                return nc.gpsimd.tensor_tensor(idle[:, i:i + 1], idle[:, 0:1], idle[:, 0:1], ALU.mult)

            def split(n, kind, half, rest, parts):
                done = split_count(n, kind, half) - 4
                gate(1)
                nc.gpsimd.tensor_copy(parts[0], rest).then_inc(split_step, 1)
                pool.wait_ge(split_step, done + 1)
                nc.gpsimd.tensor_tensor(rest, rest, parts[0], ALU.subtract).then_inc(split_step, 1)
                pool.wait_ge(split_step, done + 2)
                gate(2)
                nc.gpsimd.tensor_copy(parts[1], rest).then_inc(split_step, 1)
                pool.wait_ge(split_step, done + 3)
                nc.gpsimd.tensor_tensor(parts[2], rest, parts[1], ALU.subtract).then_inc(split_step, 1)

            def split_q(n, half, job, fresh):
                pool.wait_ge(misc_free, job + 1)
                if not fresh:
                    for s in (2 * half, 2 * half + 1):
                        pool.wait_ge(q_in[s], Q_IN * n)
                split(n, "q", half, qf[:, half, :], [qparts[:, i, half, :] for i in range(3)])

            def split_k(n, half, job, fresh):
                pool.wait_ge(misc_free, job + 1)
                if half == 1:
                    for s in (0, 1):
                        pool.wait_ge(k_in[s], K_IN * (n + 1))
                elif not fresh:
                    for s in (2, 3):
                        pool.wait_ge(k_in[s], K_IN * n)
                split(n, "k", half, kf[:, :], [kparts[:, i, 0:KV] for i in range(3)])

            def go(n, s, fresh):
                if not fresh:
                    pool.wait_ge(score_ready, NS * (NG * n - NG + s + 1))
                pool.wait_ge(split_step, split_count(n, "k", s // 2))
                gate(4).then_inc(restack_go, 1)
                pool.wait_ge(restack_go, NG * n + s + 1)

            def add_bias(n):
                pool.wait_ge(xn_done, QT * (n + 1))
                gate(3)
                xs = x[:, QT * n:QT * n + QT, :] if isinstance(n, int) else x[:, bass.ds(QT * n, QT), :]
                nc.gpsimd.tensor_tensor(xs, xs, bo[:, :].rearrange("p (o d) -> p o d", o=1).broadcast_to([P, QT, D]),
                                        ALU.add).then_inc(bias_done, 1)

            pool.wait_ge(gated, 1)
            at = {j: i for i, j in enumerate(PROLOGUE)}
            if b_o is not None:
                pool.wait_ge(weights_in, WEIGHTS_IN)
                add_bias(0)
            split_q(0, 0, at["q", 0], True)
            split_q(0, 1, at["q", 1], True)
            if mask is not None:
                pool.wait_ge(mask_out, 16 * HG)
            split_k(0, 0, at["k", (0, 3)], True)
            go(0, 0, True)
            go(0, 1, True)
            split_k(0, 1, at["k", (1, 3)], True)
            go(0, 2, True)
            go(0, 3, True)

            def body(b, first, last):
                before = jobs_before(b, first)
                for i, (g, kt, job, arg) in enumerate(jobs_of(first, last)):
                    if job == "q" and arg == 0 and b_o is not None:
                        add_bias(b + 1)
                    if job == "q":
                        split_q(b + 1, arg, before + i, False)
                    if job == "k" and arg[1] == 3:
                        split_k(b + 1, arg[0], before + i, False)
                        for s in (2 * arg[0], 2 * arg[0] + 1):
                            go(b + 1, s, False)

            body(0, True, False)
            with pool.Fori(1, B - 1) as b:
                body(b, False, False)
            body(B - 1, False, True)

        @block.scalar
        def _(act):
            act.wait_ge(ln_v, 2)
            nc.scalar.activation(tmp[:, 0, :], ve[:, :], ACT.Sqrt).then_inc(ln_s, 1)

            def take(n, job, kind, arg, fresh):
                act.wait_ge(misc_full, job + 1)
                if kind == "xt":
                    nc.scalar.copy(xnT[:, arg, :], misc[:, :]).then_inc(misc_free, 1)
                if kind == "ot":
                    nc.scalar.copy(oT[:, arg, :], misc[:, :]).then_inc(misc_free, 1)
                if kind == "q":
                    if not fresh:
                        act.wait_ge(split_step, split_count(n - 1, "q", arg))
                    nc.scalar.activation(qf[:, arg, :], misc[:, :], ACT.Identity, bias=bq[:, arg:arg + 1],
                                         scale=HD ** -0.5).then_inc(misc_free, 1)
                if kind == "k":
                    half, c = arg
                    if half == 1:
                        act.wait_ge(split_step, split_count(n, "k", 0))
                    elif not fresh:
                        act.wait_ge(split_step, split_count(n - 1, "k", 1))
                    o, w = KCH[c]
                    nc.scalar.activation(kf[:, o:o + w], misc[:, 0:w], ACT.Identity,
                                         bias=bk[:, half:half + 1]).then_inc(misc_free, 1)

            def take_out(G):
                act.wait_ge(av_done, KT * (G + 1))
                nc.scalar.copy(osb[:, :], avp[:, :]).then_inc(osb_done, 1)

            act.wait_ge(setup_v, 3)
            for i, (job, arg) in enumerate(PROLOGUE):
                if job in ON_ACT:
                    take(0, i, job, arg, True)

            def body(b, first, last):
                before = jobs_before(b, first)
                jobs = {(g, kt): (i, job, arg) for i, (g, kt, job, arg) in enumerate(jobs_of(first, last))}
                for g in range(NG):
                    G = NG * b + g
                    for kt in range(KT):
                        rows = P if kt < KT - 1 else LAST
                        slot = kt % 2 if kt < KT - 1 else 2
                        if kt == 1 and not (first and g == 0):
                            take_out(G - 1)
                        if kt in (0, 1, KT - 1):
                            if not (first and g == 0):
                                act.wait_ge(av_done, KT * G - (2 - kt if kt < 2 else 0))
                        else:
                            act.wait_ge(av_done, KT * G + kt - 1)
                        for h in range(HG):
                            j = HG * kt + h
                            act.wait_ge(score_ready, NS * G + j + 1)
                            nc.scalar.activation(pr[0:rows, slot, h, :], sc[0:rows, j % 3, :],
                                                 ACT.Exp).then_inc(exp_done, 1)
                            i, job, arg = jobs.get((g, kt), (0, "", 0))
                            if h == 1 and job in ON_ACT:
                                take(b + 1, before + i, job, arg, False)

            body(0, True, False)
            with act.Fori(1, B - 1) as b:
                body(b, False, False)
            body(B - 1, False, True)
            take_out(NG * B - 1)
            tail = jobs_before(B - 1, False) + len(jobs_of(False, True))
            for i, (job, arg) in enumerate(TAIL):
                if job in ON_ACT:
                    take(B, tail + i, job, arg, False)

        @block.vector
        def _(dve):
            nc.vector.memset(V[:, :, :, :, :], 0.0).then_inc(setup_v, 1)
            dve.wait_ge(setup_v, 1)
            nc.vector.memset(V[:, :, :, :, HD:HD + 1], 1.0).then_inc(setup_v, 1)
            if b_q is None:
                nc.vector.memset(bq[:, :], 0.0)
                nc.vector.memset(bv[:, :], 0.0)
                nc.vector.memset(bk[:, :], 0.0).then_inc(setup_v, 1)
            else:
                dve.wait_ge(weights_in, WEIGHTS_IN)
                nc.vector.tensor_scalar(bq[:, :], bq[:, :], HD ** -0.5, None, ALU.mult).then_inc(setup_v, 1)
            if mask is not None:
                dve.wait_ge(mask_in, 16)
                nc.vector.memset(mbias[:, KV:KVP], 0.0)
                nc.vector.tensor_scalar(mbias[:, 0:KV], mrow[:, 0:KV], -MASKED, MASKED, ALU.mult, ALU.add).then_inc(setup_v, 1)

            for t in range(NT):
                last = nc.vector.bn_stats(st[:, t, :], x[:, t, :])
            last.then_inc(ln_v, 1)
            dve.wait_ge(ln_v, 1)
            for t in range(NT):
                last = nc.vector.bn_aggr(mv[:, t, :], st[:, t, :])
            last.then_inc(ln_s, 1)
            dve.wait_ge(ln_s, 1)
            nc.vector.tensor_scalar(ve[:, :], mv[:, :, 1], EPS, None, ALU.add).then_inc(ln_v, 1)
            dve.wait_ge(ln_s, 2)
            rsqrt_steps(nc, dve, ln_v, 2, ve, tmp, rs)

            def normalize_tokens(n, t):
                i = QT * n + t
                ds = (lambda a: a[:, i, :]) if isinstance(n, int) else (lambda a: a[:, bass.ds(i, 1), :])
                col = (lambda a: a[:, i:i + 1]) if isinstance(n, int) else (lambda a: a[:, bass.ds(i, 1)])
                mean = mv[:, i, 0:1] if isinstance(n, int) else mv[:, bass.ds(i, 1), 0]
                dst = xn[:, t, :] if isinstance(n, int) else xn[:, t:t + 1, :]
                nc.vector.tensor_scalar(dst, ds(x), mean, col(rs), ALU.subtract, ALU.mult).then_inc(xn_done, 1)

            def take(b, job, kind, arg, first):
                if kind == "mx":
                    G = NG * b + arg + 1
                    dve.wait_ge(misc_full, job + 1)
                    if not (isinstance(G, int) and G == 0):
                        dve.wait_ge(c_in[(arg) % NG], C_IN * ((b + 1) if arg >= 0 else b))
                    nc.vector.tensor_scalar(cneg[:, :], misc[0:16, 0:P], CLAMP, -1.0, ALU.max, ALU.mult).then_inc(misc_free, 1)
                    dve.wait_ge(misc_free, job + 1)
                    nc.vector.tensor_copy(chi[:, :], cneg[:, :]).then_inc(c_step, 1)
                    dve.wait_ge(c_step, 2 * G + 1)
                    nc.vector.tensor_tensor(clo[:, :], cneg[:, :], chi[:, :], ALU.subtract).then_inc(c_step, 1)
                    return
                dve.wait_ge(misc_full, job + 1)
                if kind == "norm":
                    g, G = (arg - 1) % NG, NG * b + arg - 1
                    src = misc[:, :].rearrange("p (t j d) -> p t j d", j=HG, d=32)
                    nc.vector.reciprocal(rden[:, :, :], src[:, :, :, HD]).then_inc(rden_done, 1)
                    dve.wait_ge(rden_done, G + 1)
                    ont = on[:, :, 64 * g:64 * g + 64].rearrange("p t (j d) -> p t j d", j=HG)
                    ins = None
                    for t in range(QT):
                        r = rden[:, t, :].rearrange("p (j o) -> p j o", o=1).broadcast_to([P, HG, HD])
                        ins = nc.vector.tensor_tensor(ont[:, t], src[:, t, :, 0:HD], r, ALU.mult)
                    ins.then_inc(misc_free, 1)
                if kind == "out":
                    i = QT * (b - 1) + 2 * arg
                    xs = x[:, i:i + 2, :] if isinstance(b, int) else x[:, bass.ds(i, 2), :]
                    if b_o is not None:
                        dve.wait_ge(bias_done, b)
                    nc.vector.tensor_tensor(xs, misc[:, :].rearrange("p (t n) -> p t n", t=2), xs,
                                            ALU.add).then_inc(misc_free, 1)
                if kind == "v":
                    s, part = arg
                    if not (first and (b == 0 if isinstance(b, int) else False)):
                        dve.wait_ge(av_done, KT * (NG * (b - 1) + s + 1))
                    k0, k1 = VPART[part]
                    src = misc[:, :].rearrange("p (k j d) -> p k j d", j=HG, d=HD)
                    bias = bv[:, 64 * s:64 * s + 64].rearrange("p (o j d) -> p o j d", o=1, d=HD)
                    full = min(k1, KT - 1) - k0
                    ins = nc.vector.tensor_tensor(V[:, s, k0:k0 + full, :, 0:HD], src[:, 0:full],
                                                  bias.broadcast_to([P, full, HG, HD]), ALU.add)
                    if k1 == KT:
                        ins = nc.vector.tensor_tensor(V[0:LAST, s, KT - 1, :, 0:HD], src[0:LAST, full],
                                                      bias[0:LAST, 0], ALU.add)
                    ins.then_inc(misc_free, 1)

            def row_maxima(G, par):
                dve.wait_ge(max_done, NCHUNK * (G + 1))
                nc.vector.tensor_reduce(mxr[:, par, :], mx[:, par, :].rearrange("p (i c) -> p i c", c=4),
                                        AX.X, ALU.max).then_inc(rowmax_done, 1)

            def reduce_chunk(G, par, i):
                dve.wait_ge(max_ready, NCHUNK * G + i + 1)
                nc.vector.tensor_reduce(mx[:, par, i:i + 1], mxp[:, i % 3, 0:CHUNK], AX.X, ALU.max).then_inc(max_done, 1)

            for t in range(QT):
                normalize_tokens(0, t)
            for i, (job, arg) in enumerate(PROLOGUE):
                if job == "v":
                    take(0, i, job, arg, True)
            for i in range(NCHUNK):
                reduce_chunk(0, 0, i)
            row_maxima(0, 0)
            take(0, len(PROLOGUE) - 1, "mx", -1, True)
            for i in range(LEAD):
                reduce_chunk(1, 1, i)

            def body(b, first, last):
                before = jobs_before(b, first)
                jobs = {(g, kt): (i, job, arg) for i, (g, kt, job, arg) in enumerate(jobs_of(first, last))}
                for g in range(NG):
                    for kt in range(KT):
                        if jobs.get((g, kt), (0, ""))[1] == "mx":
                            row_maxima(NG * b + g + 1, (g + 1) % 2)
                        chunks = chunks_at(g, kt, last)
                        for tg, c in chunks[:2]:
                            reduce_chunk(NG * b + tg, tg % 2, c)
                        i, job, arg = jobs.get((g, kt), (0, "", 0))
                        if job and job not in ON_ACT:
                            n = b if job != "v" or arg[0] == 3 else b + 1
                            take(n, before + i, job, arg, first and n is b)
                        for tg, c in chunks[2:]:
                            reduce_chunk(NG * b + tg, tg % 2, c)
                        if g == 0 and 3 <= kt < 3 + QT and not last:
                            normalize_tokens(b + 1, kt - 3)

            body(0, True, False)
            with dve.Fori(1, B - 1) as b:
                body(b, False, False)
            body(B - 1, False, True)
            tail = jobs_before(B - 1, False) + len(jobs_of(False, True))
            for i, (job, arg) in enumerate(TAIL):
                if job not in ON_ACT:
                    take(B - (job == "norm"), tail + i, job, arg, False)

        @block.tensor
        def _(pe):
            pe.wait_ge(weights_in, WEIGHTS_IN)
            pe.wait_ge(rows_in, 32)
            pe.wait_ge(setup_v, 3)

            def start(n, job, kind, arg, parts=(0, 1)):
                if 0 in parts and not (isinstance(job, int) and job == 0):
                    pe.wait_ge(misc_free, job)
                mm = None
                if kind == "xt" and 0 in parts:
                    pe.wait_ge(xn_done, QT * (n + 1))
                if kind == "k" and 0 in parts:
                    pe.wait_ge(ctx_in, 16 * (n + 1))
                if kind == "norm" and 0 in parts:
                    pe.wait_ge(osb_done, NG * n + arg)
                if kind == "mx" and 0 in parts:
                    pe.wait_ge(rowmax_done, NG * n + arg + 2)
                for part in parts:
                    if kind in ("xt", "ot", "norm"):
                        for t in (2 * part, 2 * part + 1):
                            src = {"xt": xn[:, t, P * arg:P * arg + P] if arg < DK else None,
                                   "ot": on[:, t, P * arg:P * arg + P] if arg < DK else None,
                                   "norm": osb[:, P * t:P * t + P]}[kind]
                            mm = nc.tensor.transpose(misc[:, P * t:P * t + P], src, ident[:, :])
                    if kind == "mx" and part == 0:
                        mm = nc.tensor.transpose(misc[0:16, 0:P], mxr[:, (arg + 1) % 2, :], ident[:, :])
                    if kind == "q":
                        mm = nc.tensor.matmul(misc[:, :], wq[:, part, P * arg:P * arg + P], xnT[:, part, :],
                                              start=part == 0, stop=part == DK - 1)
                    if kind == "k":
                        half, c = arg
                        o, w = KCH[c]
                        mm = nc.tensor.matmul(misc[:, 0:w], wk[:, part, P * half:P * half + P],
                                              ctx_sb[:, part, o:o + w], start=part == 0, stop=part == DK - 1)
                    if kind == "v":
                        s, i = arg
                        k0, k1 = VPART[i]
                        mid = (k0 + k1) // 2
                        for kt in (range(k0, mid) if part == 0 else range(mid, k1)):
                            rows = P if kt < KT - 1 else LAST
                            for k in range(DK):
                                mm = nc.tensor.matmul(misc[0:rows, 64 * (kt - k0):64 * (kt - k0) + 64],
                                                      ctx_sb[:, k, P * kt:P * kt + rows], wv[:, k, 64 * s:64 * s + 64],
                                                      start=k == 0, stop=k == DK - 1)
                    if kind == "out":
                        for k in range(DK):
                            a = P * (2 * arg + part)
                            mm = nc.tensor.matmul(misc[:, D * part:D * part + D], oT[:, k, a:a + P], wo[:, k, :],
                                                  start=k == 0, stop=k == DK - 1)
                if (1 if kind != "mx" else 0) in parts:
                    mm.then_inc(misc_full, 1)

            def max_chunk(G, s, i, n):
                h, t, c = i // (QT * 4), i // 4 % QT, i % 4
                if i == 0:
                    pe.wait_ge(q_in[s], Q_IN * (n + 1))
                    pe.wait_ge(k_in[s], K_IN * (n + 1))
                if i >= 3:
                    pe.wait_ge(max_done, NCHUNK * G + i - 2)
                elif not (isinstance(G, int) and G == 0):
                    pe.wait_ge(max_done, NCHUNK * G - (0, 2, 1)[i])
                nc.tensor.matmul(mxp[:, i % 3, 0:CHUNK], QS[0:ROW_MASK + 1, s, h, P * t:P * t + P],
                                 KS[0:ROW_MASK + 1, s, h, CHUNK_AT[c]:CHUNK_AT[c] + CHUNK],
                                 start=True, stop=True).then_inc(max_ready, 1)

            def score(G, s, kt, h, first):
                j = HG * kt + h
                rows = P if kt < KT - 1 else LAST
                if j >= 3:
                    pe.wait_ge(exp_done, NS * G + j - 2)
                elif not first:
                    pe.wait_ge(exp_done, NS * G - (0, 2, 1)[j])
                nc.tensor.matmul(sc[0:rows, j % 3, :], KS[:, s, h, P * kt:P * kt + rows], QS[:, s, h, :],
                                 start=True, stop=True).then_inc(score_ready, 1)

            def pv(G, s, kt, first):
                rows = P if kt < KT - 1 else LAST
                slot = kt % 2 if kt < KT - 1 else 2
                pe.wait_ge(exp_done, NS * G + HG * kt + HG)
                if kt == 0 and not first:
                    pe.wait_ge(osb_done, G)
                for j in range(HG):
                    mm = nc.tensor.matmul(avp[32 * j:32 * j + 32, :], V[0:rows, s, kt, j, :], pr[0:rows, slot, j, :],
                                          start=kt == 0, stop=kt == KT - 1)
                mm.then_inc(av_done, 1)

            for i, (job, arg) in enumerate(PROLOGUE[:-1]):
                start(0, i, job, arg)
            for i in range(NCHUNK):
                max_chunk(0, 0, i, 0)
            start(0, len(PROLOGUE) - 1, "mx", -1)
            for i in range(LEAD):
                max_chunk(1, 1, i, 0)

            def body(b, first, last):
                before = jobs_before(b, first)
                jobs = {(g, kt): (i, job, arg) for i, (g, kt, job, arg) in enumerate(jobs_of(first, last))}
                for g in range(NG):
                    G = NG * b + g
                    none_before = first and g == 0
                    for kt in range(KT):
                        if kt == 0:
                            pe.wait_ge(c_in[g], C_IN * (b + 1))
                        chunks = chunks_at(g, kt, last)
                        i, job, arg = jobs.get((g, kt), (0, "", 0))
                        n = b + 1 if job in AHEAD or (job == "v" and arg[0] < 3) else b
                        for h in range(HG):
                            score(G, g, kt, h, none_before)
                            for tg, c in (chunks[h:h + 1] if h < HG - 1 else chunks[h:]):
                                max_chunk(NG * b + tg, tg % NG, c, b + tg // NG)
                            if h < 2 and job:
                                start(n, before + i, job, arg, (h,))
                            if h == 2 and kt > 0:
                                pv(G, g, kt - 1, none_before)
                            elif h == 2 and not none_before:
                                pv(G - 1, (g - 1) % NG, KT - 1, False)

            body(0, True, False)
            with pe.Fori(1, B - 1) as b:
                body(b, False, False)
            body(B - 1, False, True)
            pv(NG * B - 1, NG - 1, KT - 1, False)
            tail = jobs_before(B - 1, False) + len(jobs_of(False, True))
            for i, (job, arg) in enumerate(TAIL):
                start(B - 1, tail + i, job, arg)


def rsqrt_steps(nc, dve, done, n, ve, tmp, rs):
    y, h = tmp[:, 0, :], tmp[:, 1, :]
    nc.vector.reciprocal(rs[:, :], y).then_inc(done, 1)
    dve.wait_ge(done, n + 1)
    nc.vector.tensor_tensor(h, rs[:, :], rs[:, :], ALU.mult).then_inc(done, 1)
    dve.wait_ge(done, n + 2)
    nc.vector.tensor_tensor(h, h, ve[:, :], ALU.mult).then_inc(done, 1)
    dve.wait_ge(done, n + 3)
    nc.vector.tensor_scalar(h, h, -0.5, 1.5, ALU.mult, ALU.add).then_inc(done, 1)
    dve.wait_ge(done, n + 4)
    nc.vector.tensor_tensor(rs[:, :], rs[:, :], h, ALU.mult).then_inc(done, 1)
    dve.wait_ge(done, n + 5)


def normalized_transposed(nc, name, ctx, x, ident):
    sb = lambda n, s, d=F32: ctx.enter_context(nc.sbuf_tensor(f"{name}_{n}", s, d))
    sem = lambda n: nc.alloc_semaphore(f"{name}_{n}")
    tp = ctx.enter_context(nc.psum_tensor(f"{name}_tp", [P, 2, 2, DK, P], F32))
    xn, xnT = sb("xn", [P, 4, D]), sb("xnT", [P, DK, B * S])
    st, mv = sb("st", [P, NT, 6]), sb("mv", [P, NT, 2])
    ve, rs, tmp = sb("ve", [P, NT]), sb("rs", [P, NT]), sb("tmp", [P, 2, NT])
    ln_v, ln_s, xn_done = sem("ln_v"), sem("ln_s"), sem("xn_done")
    tp_ready, xnT_done = sem("tp_ready"), sem("xnT_done")
    PAIRS = NT // 2

    def vector(dve):
        for t in range(NT):
            last = nc.vector.bn_stats(st[:, t, :], x[:, t, :])
        last.then_inc(ln_v, 1)
        dve.wait_ge(ln_v, 1)
        for t in range(NT):
            last = nc.vector.bn_aggr(mv[:, t, :], st[:, t, :])
        last.then_inc(ln_s, 1)
        dve.wait_ge(ln_s, 1)
        nc.vector.tensor_scalar(ve[:, :], mv[:, :, 1], EPS, None, ALU.add).then_inc(ln_v, 1)
        dve.wait_ge(ln_s, 2)
        rsqrt_steps(nc, dve, ln_v, 2, ve, tmp, rs)
        for t in range(NT):
            if t >= 4:
                dve.wait_ge(tp_ready, (t - 4) // 2 + 1)
            nc.vector.tensor_scalar(xn[:, t % 4, :], x[:, t, :], mv[:, t, 0:1], rs[:, t:t + 1],
                                    ALU.subtract, ALU.mult).then_inc(xn_done, 1)

    def tensor(pe):
        for p in range(PAIRS):
            pe.wait_ge(xn_done, 2 * p + 2)
            if p >= 2:
                pe.wait_ge(xnT_done, p - 1)
            for i in range(2):
                for k in range(DK):
                    mm = nc.tensor.transpose(tp[:, p % 2, i, k, :], xn[:, (2 * p + i) % 4, P * k:P * k + P], ident[:, :])
            mm.then_inc(tp_ready, 1)

    def scalar(act):
        act.wait_ge(ln_v, 2)
        nc.scalar.activation(tmp[:, 0, :], ve[:, :], ACT.Sqrt).then_inc(ln_s, 1)
        for p in range(PAIRS):
            act.wait_ge(tp_ready, p + 1)
            dst = xnT[:, :, 2 * P * p:2 * P * p + 2 * P].rearrange("p k (i n) -> p i k n", i=2)
            nc.scalar.copy(dst, tp[:, p % 2]).then_inc(xnT_done, 1)

    return xnT, xnT_done, PAIRS, vector, tensor, scalar


def swiglu(nc, x, ident, w_gate, w_up, w_down):
    MT = FF0 // P
    NC = B
    with ExitStack() as ctx:
        sb = lambda n, s, d=F32: ctx.enter_context(nc.sbuf_tensor(f"ffn_{n}", s, d))
        sem = lambda n: nc.alloc_semaphore(f"ffn_{n}")
        xnT, xnT_done, PAIRS, ln_vector, ln_tensor, ln_scalar = normalized_transposed(nc, "ffn", ctx, x, ident)
        gp = ctx.enter_context(nc.psum_tensor("ffn_gate", [P, 2, S], F32))
        up = ctx.enter_context(nc.psum_tensor("ffn_up", [P, 2, S], F32))
        yp = ctx.enter_context(nc.psum_tensor("ffn_y", [P, QT, D], F32))
        wi = sb("wi", [P, 3, DK * FF0], I32)
        wf = sb("wf", [P, 3, DK * FF0])
        wg, wu = (wf[:, i, :].rearrange("p (k n) -> p k n", k=DK) for i in range(2))
        wd = wf[:, 2, :].rearrange("p (m n) -> p m n", m=MT)
        sg, hT = sb("sg", [P, 2, S]), sb("hT", [P, MT, S])
        w_in = [sem(f"w_in{i}") for i in range(3)]
        w_cast = sem("w_cast")
        gate_ready, up_ready, silu_done, h_done = sem("gate_ready"), sem("up_ready"), sem("silu_done"), sem("h_done")
        down_done, y_taken = sem("down_done"), sem("y_taken")
        block = ctx.enter_context(nc.Block())

        @block.sync
        def _(sp):
            for i, w in enumerate((w_gate, w_up)):
                sp.dma_start(wi[:, i, :].rearrange("p (k n) -> p k n", k=DK),
                             w.rearrange("(k p) n -> p k n", p=P)).then_inc(w_in[i], 16)
            sp.dma_start(wi[:, 2, :].rearrange("p (m n) -> p m n", m=MT),
                         w_down.rearrange("(m p) n -> p m n", p=P)).then_inc(w_in[2], 16)

        @block.gpsimd
        def _(pool):
            for i in range(3):
                pool.wait_ge(w_in[i], 16)
                nc.gpsimd.tensor_copy(wf[:, i, :], wi[:, i, :]).then_inc(w_cast, 1)

        def chunks(engine, body):
            body(0)
            with engine.Fori(1, NC) as c:
                body(c)

        @block.scalar
        def _(act):
            ln_scalar(act)

            def body(c):
                for m in range(MT):
                    q = MT * c + m
                    act.wait_ge(gate_ready, q + 1)
                    if not (isinstance(q, int) and q < 2):
                        act.wait_ge(h_done, q - 1)
                    nc.scalar.activation(sg[:, m % 2, :], gp[:, m % 2, :], ACT.Silu, scale=INV127).then_inc(silu_done, 1)

            chunks(act, body)

        @block.vector
        def _(dve):
            ln_vector(dve)

            def take_y(c):
                dve.wait_ge(down_done, MT * (c + 1))
                for i in range(2):
                    t = QT * c + 2 * i
                    xs = x[:, t:t + 2, :] if isinstance(c, int) else x[:, bass.ds(t, 2), :]
                    ins = nc.vector.scalar_tensor_tensor(out=xs, in0=yp[:, 2 * i:2 * i + 2, :], scalar=INV127, in1=xs,
                                                         op0=ALU.mult, op1=ALU.add)
                ins.then_inc(y_taken, 1)

            def body(c):
                for m in range(MT):
                    if m == 1 and not (isinstance(c, int) and c == 0):
                        take_y(c - 1)
                    q = MT * c + m
                    dve.wait_ge(silu_done, q + 1)
                    dve.wait_ge(up_ready, q + 1)
                    if not isinstance(c, int):
                        dve.wait_ge(down_done, q - MT + 1)
                    nc.vector.scalar_tensor_tensor(out=hT[:, m, :], in0=up[:, m % 2, :], scalar=INV127,
                                                   in1=sg[:, m % 2, :], op0=ALU.mult, op1=ALU.mult).then_inc(h_done, 1)

            chunks(dve, body)
            take_y(NC - 1)

        @block.tensor
        def _(pe):
            ln_tensor(pe)
            pe.wait_ge(xnT_done, PAIRS)
            pe.wait_ge(w_cast, 3)

            def down(q, m, c):
                pe.wait_ge(h_done, q + 1)
                if m == 0 and not (isinstance(c, int) and c == 0):
                    pe.wait_ge(y_taken, c)
                for t in range(QT):
                    mm = nc.tensor.matmul(yp[:, t, :], hT[:, m, P * t:P * t + P], wd[:, m, :],
                                          start=m == 0 and t % 2 == 0, stop=m == MT - 1, skip_group_check=True)
                mm.then_inc(down_done, 1)

            def body(c):
                tokens = slice(S * c, S * c + S) if isinstance(c, int) else bass.ds(S * c, S)
                for m in range(MT):
                    q = MT * c + m
                    for w, bank, ready, free in ((wg, gp, gate_ready, silu_done), (wu, up, up_ready, h_done)):
                        if not (isinstance(q, int) and q < 2):
                            pe.wait_ge(free, q - 1)
                        for k in range(DK):
                            mm = nc.tensor.matmul(bank[:, m % 2, :], w[:, k, P * m:P * m + P], xnT[:, k, tokens],
                                                  start=k == 0, stop=k == DK - 1)
                        mm.then_inc(ready, 1)
                    if not (isinstance(q, int) and q == 0):
                        down(q - 1, (m - 1) % MT, c if m > 0 else c - 1)

            chunks(pe, body)
            down(MT * NC - 1, MT - 1, NC - 1)


def route(nc, ctx, sb, sem, x, iota, xnT, gw, gb, w_in, w_in_n, lp):
    lg, m8, i8 = sb("lg", [P, NT, E]), sb("m8", [P, NT, 8]), sb("i8", [P, NT, 8], U32)
    top = sb("top", [P, 2, NT])
    wt = sb("wt", [P, 2, NT])
    ex, den = sb("ex", [P, NT]), sb("den", [P, NT])
    hot = sb("hot", [P, 2, NT, E])
    comb = sb("comb", [P, NT, E])
    lg_ready, gate_v, gate_s = sem("lg_ready"), sem("gate_v"), sem("gate_s")

    def tensor(pe):
        pe.wait_ge(w_in, w_in_n)
        for t in range(NT):
            for k in range(DK):
                mm = nc.tensor.matmul(lp[:, E * t:E * t + E], xnT[:, k, P * t:P * t + P], gw[:, k, :],
                                      start=k == 0, stop=k == DK - 1)
        mm.then_inc(lg_ready, 1)

    def scalar(act):
        act.wait_ge(gate_v, 4)
        nc.scalar.activation(ex[:, :], den[:, :], ACT.Exp).then_inc(gate_s, 1)

    def vector(dve):
        n = [0]

        def step(ins):
            n[0] += 1
            ins.then_inc(gate_v, 1)
            dve.wait_ge(gate_v, n[0])

        dve.wait_ge(lg_ready, 1)
        dve.wait_ge(w_in, w_in_n)
        gbb = gb[:, :].rearrange("p (o e) -> p o e", o=1).broadcast_to([P, NT, E])
        step(nc.vector.tensor_tensor(lg[:, :, :], lp[:, 0:NT * E].rearrange("p (t e) -> p t e", e=E), gbb, ALU.add))
        for t in range(NT):
            last = nc.vector.max(m8[:, t, :], lg[:, t, :])
        step(last)
        for t in range(NT):
            last = nc.vector.max_index(i8[:, t, :], m8[:, t, :], lg[:, t, :])
        step(last)
        step(nc.vector.tensor_tensor(den[:, :], m8[:, :, 1], m8[:, :, 0], ALU.subtract))
        dve.wait_ge(gate_s, 1)
        step(nc.vector.tensor_scalar(den[:, :], ex[:, :], 1.0, None, ALU.add))
        step(nc.vector.reciprocal(wt[:, 0, :], den[:, :]))
        step(nc.vector.tensor_tensor(wt[:, 1, :], ex[:, :], wt[:, 0, :], ALU.mult))
        step(nc.vector.tensor_copy(top[:, :, :], i8[:, :, 0:2].rearrange("p t i -> p i t")))
        iot = iota[:, 0:E].rearrange("p (o e) -> p o e", o=1).broadcast_to([P, NT, E])
        for i in range(2):
            def each(a):
                return a[:, i, :].rearrange("p (t o) -> p t o", o=1).broadcast_to([P, NT, E])
            step(nc.vector.tensor_tensor(hot[:, i], iot, each(top), ALU.is_equal))
            step(nc.vector.tensor_tensor(hot[:, i], hot[:, i], each(wt), ALU.mult))
        step(nc.vector.tensor_tensor(comb[:, :, :], hot[:, 0], hot[:, 1], ALU.add))

    return comb, gate_v, 13, vector, tensor, scalar


def experts(nc, x, ident, iota, gate_w, gate_b, w1, b1, w2, b2):
    MT = FF // P
    NC = B
    with ExitStack() as ctx:
        sb = lambda n, s, d=F32: ctx.enter_context(nc.sbuf_tensor(f"moe_{n}", s, d))
        sem = lambda n: nc.alloc_semaphore(f"moe_{n}")
        xnT, xnT_done, PAIRS, ln_vector, ln_tensor, ln_scalar = normalized_transposed(nc, "moe", ctx, x, ident)
        hp = ctx.enter_context(nc.psum_tensor("moe_h", [P, 2, S], F32))
        yp = ctx.enter_context(nc.psum_tensor("moe_y", [P, QT, D], F32))
        lp = ctx.enter_context(nc.psum_tensor("moe_l", [P, 512], F32))
        gw, gb = sb("gw", [P, DK, E]), sb("gb", [P, E])
        b1c, b2r = sb("b1", [P, E, MT]), sb("b2", [E, D])
        b1e = sb("b1e", [P, 2, MT])
        w1s, w2s = sb("w1", [P, 2, DK, FF]), sb("w2", [P, 2, MT, D])
        hT, cT = sb("hT", [P, MT, S]), sb("cT", [E, S])
        w_in, b1_done = sem("w_in"), sem("b1_done")
        comb, comb_done, comb_n, gate_vector, gate_tensor, gate_scalar = route(
            nc, ctx, sb, sem, x, iota, xnT, gw, gb, w_in, 64, lp)
        e_in = [sem("e_in0"), sem("e_in1")]
        h_ready, h_done, down_done, y_taken = sem("h_ready"), sem("h_done"), sem("down_done"), sem("y_taken")
        cT_ready, cT_done, b2_ready, b2_done = sem("cT_ready"), sem("cT_done"), sem("b2_ready"), sem("b2_done")
        block = ctx.enter_context(nc.Block())
        PER = NC * MT

        def pairs(engine, body):
            body(0)
            with engine.Fori(1, E // 2 - 1) as i:
                body(i)
            body(E // 2 - 1)

        @block.sync
        def _(sp):
            sp.dma_start(gw[:, :, :], gate_w.rearrange("(k p) n -> p k n", p=P)).then_inc(w_in, 16)
            sp.dma_start(gb[:, :], gate_b.partition_broadcast(P)).then_inc(w_in, 16)
            sp.dma_start(b1c[:, :, :], b1).then_inc(w_in, 16)
            sp.dma_start(b2r[:, :], b2).then_inc(w_in, 16)

            for e in range(2):
                sp.dma_start(w1s[:, e], w1[e].rearrange("(k p) n -> p k n", p=P)).then_inc(e_in[e], 16)
                sp.dma_start(w2s[:, e], w2[e].rearrange("(k p) n -> p k n", p=P)).then_inc(e_in[e], 16)

        @block.scalar
        def _(act):
            ln_scalar(act)
            gate_scalar(act)

            act.wait_ge(w_in, 64)

            def body(i):
                for par in range(2):
                    e = 2 * i + par
                    nc.scalar.copy(b1e[:, par, :], b1c[:, e, :] if isinstance(e, int) else b1c[:, bass.ds(e, 1), :]).then_inc(b1_done, 1)
                    act.wait_ge(b1_done, e + 1)
                    for c in range(NC):
                        for m in range(MT):
                            q = PER * e + MT * c + m
                            act.wait_ge(h_ready, q + 1)
                            if not (isinstance(q, int) and q < MT):
                                act.wait_ge(down_done, q - MT + 1)
                            if c == 1 and m == 0 and not (isinstance(e, int) and e in (0, E - 1)):
                                n, o = e + 1, 1 - par
                                ws = (w1[n:n + 1], w2[n:n + 1]) if isinstance(n, int) else (w1[bass.ds(n, 1)], w2[bass.ds(n, 1)])
                                act.dma_start(w1s[:, o], ws[0].rearrange("o (k p) n -> p (o k) n", p=P)).then_inc(e_in[o], 16)
                                act.dma_start(w2s[:, o], ws[1].rearrange("o (k p) n -> p (o k) n", p=P)).then_inc(e_in[o], 16)
                            nc.scalar.activation(hT[:, m, :], hp[:, m % 2, :], ACT.Gelu,
                                                 bias=b1e[:, par, m:m + 1]).then_inc(h_done, 1)

            pairs(act, body)

        @block.vector
        def _(dve):
            ln_vector(dve)
            gate_vector(dve)
            for c in range(NC):
                dve.wait_ge(cT_ready, c + 1)
                if c:
                    dve.wait_ge(b2_ready, c)
                nc.vector.tensor_copy(cT[:, :], lp[0:E, :]).then_inc(cT_done, 1)
                dve.wait_ge(b2_ready, c + 1)
                nc.vector.tensor_tensor(x[:, QT * c:QT * c + QT, :], yp[:, :, :], x[:, QT * c:QT * c + QT, :],
                                        ALU.add).then_inc(b2_done, 1)

            def body(i):
                for par in range(2):
                    for c in range(NC):
                        n = NC * (2 * i + par) + c
                        dve.wait_ge(down_done, MT * (n + 1))
                        for t in range(QT):
                            e = 2 * i + par
                            w = comb[:, QT * c + t, e:e + 1] if isinstance(e, int) else comb[:, QT * c + t, bass.ds(e, 1)]
                            xs = x[:, QT * c + t, :]
                            last = nc.vector.scalar_tensor_tensor(out=xs, in0=yp[:, t, :], scalar=w, in1=xs,
                                                                  op0=ALU.mult, op1=ALU.add)
                        last.then_inc(y_taken, 1)

            pairs(dve, body)

        @block.tensor
        def _(pe):
            ln_tensor(pe)
            pe.wait_ge(xnT_done, PAIRS)
            gate_tensor(pe)
            pe.wait_ge(comb_done, comb_n)
            for c in range(NC):
                if c:
                    pe.wait_ge(cT_done, c)
                for t in range(QT):
                    mm = nc.tensor.transpose(lp[0:E, P * t:P * t + P], comb[:, QT * c + t, :], ident[:, :])
                mm.then_inc(cT_ready, 1)
                pe.wait_ge(cT_done, c + 1)
                if c:
                    pe.wait_ge(b2_done, c)
                for t in range(QT):
                    mm = nc.tensor.matmul(yp[:, t, :], cT[:, P * t:P * t + P], b2r[:, :], start=True, stop=True)
                mm.then_inc(b2_ready, 1)
            pe.wait_ge(b2_done, NC)

            def down(q, m, par, n):
                pe.wait_ge(h_done, q + 1)
                if m == 0 and not (isinstance(n, int) and n == 0):
                    pe.wait_ge(y_taken, n)
                for t in range(QT):
                    mm = nc.tensor.matmul(yp[:, t, :], hT[:, m, P * t:P * t + P], w2s[:, par, m, :],
                                          start=m == 0 and t % 2 == 0, stop=m == MT - 1, skip_group_check=True)
                mm.then_inc(down_done, 1)

            def body(i):
                for par in range(2):
                    pe.wait_ge(e_in[par], 32 * (i + 1))
                    for c in range(NC):
                        n = NC * (2 * i + par) + c
                        for m in range(MT):
                            q = MT * n + m
                            if not (isinstance(q, int) and q < 2):
                                pe.wait_ge(h_done, q - 1)
                            for k in range(DK):
                                mm = nc.tensor.matmul(hp[:, m % 2, :], w1s[:, par, k, P * m:P * m + P],
                                                      xnT[:, k, S * c:S * c + S], start=k == 0, stop=k == DK - 1)
                            mm.then_inc(h_ready, 1)
                            if not (isinstance(q, int) and q == 0):
                                down(q - 1, (m - 1) % MT, par if c or m else 1 - par, n if m > 0 else n - 1)

            pairs(pe, body)
            down(PER * E - 1, MT - 1, 1, NC * E - 1)


def xattn_ffn_2(nc, ins, out):
    with ExitStack() as ctx:
        x = ctx.enter_context(nc.sbuf_tensor("x_sb", [P, NT, D], F32))
        ident = ctx.enter_context(nc.sbuf_tensor("ident_sb", [P, P], F32))
        iota = ctx.enter_context(nc.sbuf_tensor("iota_sb", [P, E], F32))
        x_in, x_out = nc.alloc_semaphore("x_in"), nc.alloc_semaphore("x_out")
        with nc.Block() as block:
            @block.sync
            def _(sp):
                sp.dma_start(x[:, :, :], ins["x"].rearrange("(t p) d -> p t d", p=P)).then_inc(x_in, 16)
                sp.dma_start(ident[:, :], ins["ident"]).then_inc(x_in, 16)
                sp.dma_start(iota[:, :], ins["iota"]).then_inc(x_in, 16)
                sp.wait_ge(x_in, 48)
        stacks = ins["k_rows"], ins["q_rows"], ins["ctxT"]
        attention(nc, "L0", x, ident, *stacks, ins["L0_wq"], ins["L0_wk"], ins["L0_wv"], ins["L0_wo"],
                  ins["L0_bq"], ins["L0_bk"], ins["L0_bv"], ins["L0_bo"], ins["mask"])
        swiglu(nc, x, ident, ins["w_gate"], ins["w_up"], ins["w_down"])
        attention(nc, "L1", x, ident, *stacks, ins["L1_wq"], ins["L1_wk"], ins["L1_wv"], ins["L1_wo"],
                  None, None, None, None, None)
        experts(nc, x, ident, iota, ins["gate_w"], ins["gate_b"], ins["w1"], ins["b1"], ins["w2"], ins["b2"])
        with nc.Block() as block:
            @block.sync
            def _(sp):
                sp.dma_start(out.rearrange("(t p) d -> p t d", p=P), x[:, :, :]).then_inc(x_out, 16)
                sp.wait_ge(x_out, 16)




def kernel(**inputs):
    import numpy as _np
    import concourse.bacc as _bacc
    from concourse import mybir as _mybir
    from concourse.bass_utils import run_bass_kernel_spmd as _run

    a = {n: _np.asarray(v) for n, v in inputs.items()}
    order = _np.array([HD * (HG * g + j) + d for g in range(NG) for d in range(HD) for j in range(HG)])
    wkv, bkv = a["L0_xattn_W_kv"], a["L0_xattn_b_kv"]
    ones = 0x3F803F80
    k_rows = _np.full((3, NG * HG * KVP // 2), ones, _np.uint32)
    k_rows[0] = 0
    arrays = {
        "x": a["x"].reshape(B * S, D),
        "ident": _np.eye(P, dtype=_np.float32),
        "iota": _np.tile(_np.arange(E, dtype=_np.float32), (P, 1)),
        "k_rows": k_rows,
        "q_rows": _np.full((3, NG * HG * S // 2), ones, _np.uint32),
        "ctxT": a["ctx_1024"].transpose(0, 2, 1),
        "mask": a["mask_BxS2_bf1"].view(_np.uint8),
        "L0_wq": a["L0_xattn_W_q"][:, order], "L0_wk": wkv[:, :D][:, order], "L0_wv": wkv[:, D:],
        "L0_wo": a["L0_xattn_W_o"],
        "L0_bq": a["L0_xattn_b_q"][order].reshape(2, P).T, "L0_bk": bkv[:D][order].reshape(2, P).T,
        "L0_bv": bkv[D:], "L0_bo": a["L0_xattn_b_o"],
        "w_gate": a["L0_ffn_w_gate"].T, "w_up": a["L0_ffn_w_up"].T, "w_down": a["L0_ffn_w_down"].T,
        "L1_wq": a["L1_xattn_W_q"].T[:, order], "L1_wk": a["L1_xattn_W_k"].T[:, order],
        "L1_wv": a["L1_xattn_W_v"].T, "L1_wo": a["L1_xattn_W_o"].T,
        "gate_w": a["L1_ffn_gate_w"], "gate_b": a["L1_ffn_gate_b"],
        "w1": a["L1_ffn_w1"], "b1": a["L1_ffn_b1"].reshape(E, FF // P, P).transpose(2, 0, 1),
        "w2": a["L1_ffn_w2"], "b2": a["L1_ffn_b2"],
    }
    arrays = {n: _np.ascontiguousarray(v) for n, v in arrays.items()}
    nc = _bacc.Bacc("TRN2", target_bir_lowering=False, num_devices=1)
    ins = {n: nc.dram_tensor(f"in_{n}", v.shape, _mybir.dt.from_np(v.dtype), kind="ExternalInput").ap()
           for n, v in arrays.items()}
    out = nc.dram_tensor("out", (B * S, D), F32, kind="ExternalOutput").ap()
    xattn_ffn_2(nc, ins, out)
    r = _run(nc, [{f"in_{n}": v for n, v in arrays.items()}], core_ids=[0])
    return _np.asarray(r.results[0]["out"]).reshape(B, S, D)
```

```python
from contextlib import ExitStack

import concourse.bass as bass
from concourse import mybir

ALU = mybir.AluOpType
ACT = mybir.ActivationFunctionType
AX = mybir.AxisListType
F32 = mybir.dt.float32
BF16 = mybir.dt.bfloat16
I32 = mybir.dt.int32
U32 = mybir.dt.uint32
U8 = mybir.dt.uint8

P = 128
B, S, D = 4, 512, 256
H, HD = 16, 16
KV = 1601
KVP = KV + 1
KT = -(-KV // P)
LAST = KV - (KT - 1) * P
DK = D // P
NT = B * S // P
QT = S // P
HG = 4
NG = H // HG
TERMS = 6
ROW_MASK = TERMS * HD
ROW_C = ROW_MASK + 1
ROWS = ROW_C + 2
MASKED = -1.0e30
CLAMP = -1.0e20
EPS = 1e-5
FF0 = 768
E, FF = 8, 1024
INV127 = 1.0 / 127.0
TOP = 2
SLOT_TILES = (TOP * B * S + E * (P - 1)) // P
ROUTE_CONST = 2 * P + 2 * NT + 1

CHUNK = 401
CHUNK_AT = [0, 400, 800, 1200]
NCHUNK = HG * QT * len(CHUNK_AT)
LEAD = 20
NS = KT * HG
KCH = [(0, 401), (401, 400), (801, 400), (1201, 400)]
VPART = [(0, 4), (4, 7), (7, 10), (10, 13)]

JOBS = [
    (0, 1, "v", (1, 0)), (0, 2, "norm", 0), (0, 3, "v", (1, 1)), (0, 4, "v", (1, 2)), (0, 5, "v", (1, 3)),
    (0, 6, "ot", 0), (0, 7, "ot", 1), (0, 8, "out", 0), (0, 9, "out", 1), (0, 10, "mx", 0), (0, 11, "xt", 0),
    (0, 12, "xt", 1),
    (1, 0, "q", 0), (1, 1, "q", 1), (1, 2, "norm", 1), (1, 3, "k", (0, 0)), (1, 5, "k", (0, 1)),
    (1, 6, "k", (0, 2)), (1, 7, "k", (0, 3)), (1, 10, "mx", 1),
    (2, 2, "norm", 2), (2, 4, "v", (0, 0)), (2, 5, "v", (0, 1)), (2, 6, "v", (0, 2)), (2, 7, "v", (0, 3)),
    (2, 10, "mx", 2),
    (3, 2, "norm", 3), (3, 4, "k", (1, 0)), (3, 5, "k", (1, 1)), (3, 6, "k", (1, 2)), (3, 7, "k", (1, 3)),
    (3, 10, "mx", 3),
]
FIRST = ([("xt", 0), ("xt", 1), ("q", 0)] + [("k", (0, c)) for c in range(4)] + [("v", (0, i)) for i in range(4)])
BESIDE = [("q", 1)] + [("k", (1, c)) for c in range(4)]
PROLOGUE = FIRST + BESIDE + [("mx", -1)]
TAIL = [("norm", 4), ("ot", 0), ("ot", 1), ("out", 0), ("out", 1)]
BEHIND = ("ot", "out")
ON_ACT = ("xt", "q", "k", "ot")
AHEAD = ("xt", "q", "k")


def jobs_of(first, last):
    out = []
    for g, kt, job, arg in JOBS:
        if first and ((job == "norm" and g == 0) or job in BEHIND):
            continue
        if last and (job in AHEAD or (job == "v" and arg[0] == 0) or (job == "mx" and g == 3)):
            continue
        out.append((g, kt, job, arg))
    return out


def jobs_before(b, first):
    return len(PROLOGUE) + (0 if first else b * len(JOBS) - 5)


def chunks_at(g, kt, last):
    lo, hi = LEAD + 5 * kt, LEAD + min(5 * kt + 5, NCHUNK)
    out = [(g + 1 + r // NCHUNK, r % NCHUNK) for r in range(lo, hi)]
    return [(t, i) for t, i in out if not (last and t >= NG)]


def attention(nc, name, x, ident, k_rows, q_rows, ctxT, w_q, w_k, w_v, w_o, b_q, b_k, b_v, b_o, mask):
    with ExitStack() as ctx:
        sb = lambda n, s, d=F32: ctx.enter_context(nc.sbuf_tensor(f"{name}_{n}", s, d))
        ps = lambda n, s: ctx.enter_context(nc.psum_tensor(f"{name}_{n}", s, F32))
        sem = lambda n: nc.alloc_semaphore(f"{name}_{n}")

        sc, mxp = ps("sc", [P, 3, 512]), ps("mxp", [P, 3, 512])
        avp, misc = ps("avp", [P, 512]), ps("misc", [P, 512])

        KS = sb("KS", [ROWS, NG, HG, KVP], BF16)
        QS = sb("QS", [ROWS, NG, HG, S], BF16)
        V = sb("V", [P, NG, KT, HG, 32])
        pr = sb("pr", [P, 3, HG, S])
        ctx_sb = sb("ctx", [P, DK, KV])
        wq, wk, wv = (sb(n, [P, DK, D]) for n in ("wq", "wk", "wv"))
        wo = sb("wo", [P, DK, D])
        bq, bk = sb("bq", [P, 2]), sb("bk", [P, 2])
        bv = sb("bv", [P, D])
        kf, idle = sb("kf", [P, KV]), sb("idle", [P, 5])
        kparts = sb("kparts", [P, 3, KVP], BF16)
        qf = sb("qf", [P, 2, S])
        qparts = sb("qparts", [P, 3, 2, S], BF16)
        xn, xnT = sb("xn", [P, QT, D]), sb("xnT", [P, DK, S])
        mx, mxr = sb("mx", [P, 2, NCHUNK]), sb("mxr", [P, 2, HG * QT])
        cneg, chi, clo = sb("cneg", [16, P]), sb("chi", [16, P], BF16), sb("clo", [16, P], BF16)
        osb, rden = sb("osb", [P, S]), sb("rden", [P, QT, HG])
        on = sb("on", [P, QT, D])
        oT = sb("oT", [P, DK, S])
        bo = sb("bo", [P, D])
        st, mv = sb("st", [P, NT, 6]), sb("mv", [P, NT, 2])
        eps, ve, rs, tmp = sb("eps", [P, 1]), sb("ve", [P, NT]), sb("rs", [P, NT]), sb("tmp", [P, 2, NT])
        nmask = 0
        if mask is not None:
            nmask = 16
            mrow = sb("mrow", [B, KVP], U8)
            mbias = kparts[0:B, 0, :]
            mbias_dram = nc.dram_tensor(f"{name}_mbias", [B, HG, KVP], BF16, kind="Internal").ap()

        first_in, weights_in, v_clear = sem("first_in"), sem("weights_in"), sem("v_clear")
        mask_in, mask_out = sem("mask_in"), sem("mask_out")
        ctx_in = sem("ctx_in")
        setup_v, rows_in = sem("setup_v"), sem("rows_in")
        ln_v, ln_s = sem("ln_v"), sem("ln_s")
        xn_done = sem("xn_done")
        misc_full, misc_free = sem("misc_full"), sem("misc_free")
        split_step, gated, restack_go = sem("split_step"), sem("gated"), sem("restack_go")
        k_in = [sem(f"k_in{s}") for s in range(NG)]
        q_in = [sem(f"q_in{s}") for s in range(NG)]
        c_in = [sem(f"c_in{s}") for s in range(NG)]
        max_ready, max_done, rowmax_done, c_step = sem("max_ready"), sem("max_done"), sem("rowmax_done"), sem("c_step")
        score_ready, exp_done, av_done = sem("score_ready"), sem("exp_done"), sem("av_done")
        osb_done, rden_done, bias_done = sem("osb_done"), sem("rden_done"), sem("bias_done")
        FIRST_IN, WEIGHTS_IN = (32, 32) if b_o is None else (64, 64)
        K_IN, Q_IN, C_IN = 16 * TERMS + nmask, 16 * TERMS, 32
        SPLITS = [("q", 0), ("q", 1), ("k", 0), ("k", 1)]
        FIRST_SPLITS = [("q", 0), ("k", 0), ("q", 1), ("k", 1)]

        def split_count(n, kind, half):
            order = FIRST_SPLITS if isinstance(n, int) and n == 0 else SPLITS
            return 16 * n + 4 * (order.index((kind, half)) + 1)

        block = ctx.enter_context(nc.Block())

        @block.sync
        def _(sp):
            def load_context(n):
                sp.dma_start(ctx_sb[:, :, :], ctxT[n].rearrange("(k p) n -> p k n", p=P)
                             if isinstance(n, int) else ctxT[bass.ds(n, 1)].rearrange("o (k p) n -> p (o k) n", p=P)
                             ).then_inc(ctx_in, 16)

            def load_weights(w, src, done):
                sp.dma_start(w[:, :, :], src.rearrange("(k p) n -> p k n", p=P)).then_inc(done, 16)

            load_weights(wq, w_q, first_in)
            if b_o is not None:
                sp.dma_start(bq[:, :], b_q).then_inc(first_in, 16)
                sp.dma_start(bk[:, :], b_k).then_inc(first_in, 16)
            load_weights(wk, w_k, first_in)
            if mask is not None:
                sp.dma_start(mrow[:, 0:KV], mask).then_inc(mask_in, 16)
            load_context(0)
            sp.dma_start(KS[ROW_MASK:ROWS, :, :, :].bitcast(U32).rearrange("r g h n -> r (g h n)"), k_rows).then_inc(rows_in, 16)
            sp.dma_start(QS[ROW_MASK:ROWS, :, :, :].bitcast(U32).rearrange("r g h n -> r (g h n)"), q_rows).then_inc(rows_in, 16)
            load_weights(wv, w_v, weights_in)
            if b_o is not None:
                sp.dma_start(bv[:, :], b_v.partition_broadcast(P)).then_inc(weights_in, 16)
                sp.dma_start(bo[:, :], b_o.partition_broadcast(P)).then_inc(weights_in, 16)
            load_weights(wo, w_o, weights_in)
            if mask is not None:
                sp.wait_ge(setup_v, 2)
                for h in range(HG):
                    sp.dma_start(mbias_dram[:, h, :], mbias).then_inc(mask_out, 16)
                sp.wait_ge(mask_out, 16 * HG)

            def restack(n, s):
                sp.wait_ge(restack_go, NG * n + s + 1)
                for t, part in enumerate((0, 1, 2, 0, 1, 0)):
                    sp.dma_start(QS[HD * t:HD * t + HD, s, :, :],
                                 qparts[64 * (s % 2):64 * (s % 2) + 64, part, s // 2, :]).then_inc(q_in[s], 16)
                for t, part in enumerate((0, 0, 0, 1, 1, 2)):
                    sp.dma_start(KS[HD * t:HD * t + HD, s, :, 0:KV],
                                 kparts[64 * (s % 2):64 * (s % 2) + 64, part, 0:KV]).then_inc(k_in[s], 16)
                if mask is not None:
                    src = mbias_dram[n:n + 1] if isinstance(n, int) else mbias_dram[bass.ds(n, 1)]
                    sp.dma_start(KS[ROW_MASK:ROW_MASK + 1, s, :, :], src).then_inc(k_in[s], 16)

            def shifts(G, s):
                sp.wait_ge(c_step, 2 * (G + 1))
                row = QS[ROW_C:ROW_C + 1, s, :, :].rearrange("o h (t n) -> o (h t) n", n=P)
                sp.dma_start(row, chi[:, :]).then_inc(c_in[s], 16)
                row = QS[ROW_C + 1:ROW_C + 2, s, :, :].rearrange("o h (t n) -> o (h t) n", n=P)
                sp.dma_start(row, clo[:, :]).then_inc(c_in[s], 16)

            sp.wait_ge(rows_in, 32)
            restack(0, 0)
            restack(0, 1)
            shifts(0, 0)
            restack(0, 2)

            def body(b, first, last):
                restack(b, 3)
                shifts(NG * b + 1, 1)
                if not last:
                    load_context(b + 1)
                shifts(NG * b + 2, 2)
                if not last:
                    restack(b + 1, 0)
                    restack(b + 1, 1)
                shifts(NG * b + 3, 3)
                if not last:
                    shifts(NG * b + 4, 0)
                    restack(b + 1, 2)

            body(0, True, False)
            with sp.Fori(1, B - 1) as b:
                body(b, False, False)
            body(B - 1, False, True)

        @block.gpsimd
        def _(pool):
            nc.gpsimd.memset(idle[:, :], 0.0).then_inc(gated, 1)
            nc.gpsimd.memset(V[:, :, :, :, :], 0.0).then_inc(v_clear, 1)
            pool.wait_ge(v_clear, 1)
            nc.gpsimd.memset(V[:, :, :, :, HD:HD + 1], 1.0).then_inc(v_clear, 1)

            def gate(i):
                return nc.gpsimd.tensor_tensor(idle[:, i:i + 1], idle[:, 0:1], idle[:, 0:1], ALU.mult)

            def split(n, kind, half, rest, parts):
                done = split_count(n, kind, half) - 4
                gate(1)
                nc.gpsimd.tensor_copy(parts[0], rest).then_inc(split_step, 1)
                pool.wait_ge(split_step, done + 1)
                nc.gpsimd.tensor_tensor(rest, rest, parts[0], ALU.subtract).then_inc(split_step, 1)
                pool.wait_ge(split_step, done + 2)
                gate(2)
                nc.gpsimd.tensor_copy(parts[1], rest).then_inc(split_step, 1)
                pool.wait_ge(split_step, done + 3)
                nc.gpsimd.tensor_tensor(parts[2], rest, parts[1], ALU.subtract).then_inc(split_step, 1)

            def split_q(n, half, job, fresh):
                pool.wait_ge(misc_free, job + 1)
                if not fresh:
                    for s in (2 * half, 2 * half + 1):
                        pool.wait_ge(q_in[s], Q_IN * n)
                split(n, "q", half, qf[:, half, :], [qparts[:, i, half, :] for i in range(3)])

            def split_k(n, half, job, fresh):
                pool.wait_ge(misc_free, job + 1)
                if half == 1:
                    for s in (0, 1):
                        pool.wait_ge(k_in[s], K_IN * (n + 1))
                elif not fresh:
                    for s in (2, 3):
                        pool.wait_ge(k_in[s], K_IN * n)
                split(n, "k", half, kf[:, :], [kparts[:, i, 0:KV] for i in range(3)])

            def go(n, s, fresh):
                if not fresh:
                    pool.wait_ge(score_ready, NS * (NG * n - NG + s + 1))
                pool.wait_ge(split_step, split_count(n, "k", s // 2))
                gate(4).then_inc(restack_go, 1)
                pool.wait_ge(restack_go, NG * n + s + 1)

            def add_bias(n):
                pool.wait_ge(xn_done, QT * (n + 1))
                gate(3)
                xs = x[:, QT * n:QT * n + QT, :] if isinstance(n, int) else x[:, bass.ds(QT * n, QT), :]
                nc.gpsimd.tensor_tensor(xs, xs, bo[:, :].rearrange("p (o d) -> p o d", o=1).broadcast_to([P, QT, D]),
                                        ALU.add).then_inc(bias_done, 1)

            pool.wait_ge(gated, 1)
            at = {j: i for i, j in enumerate(PROLOGUE)}
            if b_o is not None:
                pool.wait_ge(weights_in, WEIGHTS_IN)
                add_bias(0)
            go(0, 0, True)
            go(0, 1, True)
            split_q(0, 1, at["q", 1], True)
            split_k(0, 1, at["k", (1, 3)], True)
            go(0, 2, True)
            go(0, 3, True)

            def body(b, first, last):
                before = jobs_before(b, first)
                for i, (g, kt, job, arg) in enumerate(jobs_of(first, last)):
                    if job == "q" and arg == 0 and b_o is not None:
                        add_bias(b + 1)
                    if job == "q":
                        split_q(b + 1, arg, before + i, False)
                    if job == "k" and arg[1] == 3:
                        split_k(b + 1, arg[0], before + i, False)
                        for s in (2 * arg[0], 2 * arg[0] + 1):
                            go(b + 1, s, False)

            body(0, True, False)
            with pool.Fori(1, B - 1) as b:
                body(b, False, False)
            body(B - 1, False, True)

        @block.scalar
        def _(act):
            def root(lo, hi, n):
                act.wait_ge(ln_v, n)
                nc.scalar.activation(tmp[:, 0, lo:hi], ve[:, lo:hi], ACT.Sqrt).then_inc(ln_s, 1)

            def take(n, job, kind, arg, fresh):
                act.wait_ge(misc_full, job + 1)
                if kind == "xt":
                    nc.scalar.copy(xnT[:, arg, :], misc[:, :]).then_inc(misc_free, 1)
                if kind == "ot":
                    nc.scalar.copy(oT[:, arg, :], misc[:, :]).then_inc(misc_free, 1)
                if kind == "q":
                    if not fresh:
                        act.wait_ge(split_step, split_count(n - 1, "q", arg))
                    nc.scalar.activation(qf[:, arg, :], misc[:, :], ACT.Identity, bias=bq[:, arg:arg + 1],
                                         scale=HD ** -0.5).then_inc(misc_free, 1)
                if kind == "k":
                    half, c = arg
                    if half == 1:
                        act.wait_ge(split_step, split_count(n, "k", 0))
                    elif not fresh:
                        act.wait_ge(split_step, split_count(n - 1, "k", 1))
                    o, w = KCH[c]
                    nc.scalar.activation(kf[:, o:o + w], misc[:, 0:w], ACT.Identity,
                                         bias=bk[:, half:half + 1]).then_inc(misc_free, 1)

            def take_out(G):
                act.wait_ge(av_done, KT * (G + 1))
                nc.scalar.copy(osb[:, :], avp[:, :]).then_inc(osb_done, 1)

            root(0, QT, 2)
            act.wait_ge(setup_v, 1)
            for i, (job, arg) in enumerate(PROLOGUE):
                if job == "q" and arg == 0:
                    root(QT, NT, 9)
                if job in ON_ACT:
                    take(0, i, job, arg, True)

            def body(b, first, last):
                before = jobs_before(b, first)
                jobs = {(g, kt): (i, job, arg) for i, (g, kt, job, arg) in enumerate(jobs_of(first, last))}
                for g in range(NG):
                    G = NG * b + g
                    for kt in range(KT):
                        rows = P if kt < KT - 1 else LAST
                        slot = kt % 2 if kt < KT - 1 else 2
                        if kt == 1 and not (first and g == 0):
                            take_out(G - 1)
                        if kt in (0, 1, KT - 1):
                            if not (first and g == 0):
                                act.wait_ge(av_done, KT * G - (2 - kt if kt < 2 else 0))
                        else:
                            act.wait_ge(av_done, KT * G + kt - 1)
                        for h in range(HG):
                            j = HG * kt + h
                            act.wait_ge(score_ready, NS * G + j + 1)
                            nc.scalar.activation(pr[0:rows, slot, h, :], sc[0:rows, (j + g) % 3, :],
                                                 ACT.Exp).then_inc(exp_done, 1)
                            i, job, arg = jobs.get((g, kt), (0, "", 0))
                            if h == 1 and job in ON_ACT:
                                take(b + 1, before + i, job, arg, False)

            body(0, True, False)
            with act.Fori(1, B - 1) as b:
                body(b, False, False)
            body(B - 1, False, True)
            take_out(NG * B - 1)
            tail = jobs_before(B - 1, False) + len(jobs_of(False, True))
            for i, (job, arg) in enumerate(TAIL):
                if job in ON_ACT:
                    take(B, tail + i, job, arg, False)

        @block.vector
        def _(dve):
            if b_q is None:
                nc.vector.memset(bq[:, :], 0.0)
                nc.vector.memset(bv[:, :], 0.0)
                nc.vector.memset(bk[:, :], 0.0).then_inc(setup_v, 1)
            else:
                dve.wait_ge(first_in, FIRST_IN)
                nc.vector.tensor_scalar(bq[:, :], bq[:, :], HD ** -0.5, None, ALU.mult).then_inc(setup_v, 1)
            if mask is not None:
                dve.wait_ge(mask_in, 16)
                nc.vector.memset(mbias[:, KV:KVP], 0.0)
                nc.vector.tensor_scalar(mbias[:, 0:KV], mrow[:, 0:KV], -MASKED, MASKED, ALU.mult, ALU.add).then_inc(setup_v, 1)

            def statistics(lo, hi):
                v, a = (0, 0) if lo == 0 else (7, 2)
                for t in range(lo, hi):
                    last = nc.vector.bn_stats(st[:, t, :], x[:, t, :])
                last.then_inc(ln_v, 1)
                dve.wait_ge(ln_v, v + 1)
                for t in range(lo, hi):
                    last = nc.vector.bn_aggr(mv[:, t, :], st[:, t, :])
                last.then_inc(ln_s, 1)
                dve.wait_ge(ln_s, a + 1)
                nc.vector.tensor_scalar(ve[:, lo:hi], mv[:, lo:hi, 1], EPS, None, ALU.add).then_inc(ln_v, 1)
                dve.wait_ge(ln_s, a + 2)
                rsqrt_steps(nc, dve, ln_v, v + 2, ve[:, lo:hi], tmp[:, :, lo:hi], rs[:, lo:hi])

            def normalize_tokens(n, t):
                i = QT * n + t
                ds = (lambda a: a[:, i, :]) if isinstance(n, int) else (lambda a: a[:, bass.ds(i, 1), :])
                col = (lambda a: a[:, i:i + 1]) if isinstance(n, int) else (lambda a: a[:, bass.ds(i, 1)])
                mean = mv[:, i, 0:1] if isinstance(n, int) else mv[:, bass.ds(i, 1), 0]
                dst = xn[:, t, :] if isinstance(n, int) else xn[:, t:t + 1, :]
                nc.vector.tensor_scalar(dst, ds(x), mean, col(rs), ALU.subtract, ALU.mult).then_inc(xn_done, 1)

            def take(b, job, kind, arg, first):
                if kind == "mx":
                    G = NG * b + arg + 1
                    dve.wait_ge(misc_full, job + 1)
                    if not (isinstance(G, int) and G == 0):
                        dve.wait_ge(c_in[(arg) % NG], C_IN * ((b + 1) if arg >= 0 else b))
                    nc.vector.tensor_scalar(cneg[:, :], misc[0:16, 0:P], CLAMP, -1.0, ALU.max, ALU.mult).then_inc(misc_free, 1)
                    dve.wait_ge(misc_free, job + 1)
                    nc.vector.tensor_copy(chi[:, :], cneg[:, :]).then_inc(c_step, 1)
                    dve.wait_ge(c_step, 2 * G + 1)
                    nc.vector.tensor_tensor(clo[:, :], cneg[:, :], chi[:, :], ALU.subtract).then_inc(c_step, 1)
                    return
                dve.wait_ge(misc_full, job + 1)
                if kind == "norm":
                    g, G = (arg - 1) % NG, NG * b + arg - 1
                    src = misc[:, :].rearrange("p (t j d) -> p t j d", j=HG, d=32)
                    nc.vector.reciprocal(rden[:, :, :], src[:, :, :, HD]).then_inc(rden_done, 1)
                    dve.wait_ge(rden_done, G + 1)
                    ont = on[:, :, 64 * g:64 * g + 64].rearrange("p t (j d) -> p t j d", j=HG)
                    ins = None
                    for t in range(QT):
                        r = rden[:, t, :].rearrange("p (j o) -> p j o", o=1).broadcast_to([P, HG, HD])
                        ins = nc.vector.tensor_tensor(ont[:, t], src[:, t, :, 0:HD], r, ALU.mult)
                    ins.then_inc(misc_free, 1)
                if kind == "out":
                    i = QT * (b - 1) + 2 * arg
                    xs = x[:, i:i + 2, :] if isinstance(b, int) else x[:, bass.ds(i, 2), :]
                    if b_o is not None:
                        dve.wait_ge(bias_done, b)
                    nc.vector.tensor_tensor(xs, misc[:, :].rearrange("p (t n) -> p t n", t=2), xs,
                                            ALU.add).then_inc(misc_free, 1)
                if kind == "v":
                    half, part = arg
                    if not (first and (b == 0 if isinstance(b, int) else False)):
                        dve.wait_ge(av_done, KT * (NG * (b - 1) + 2 * half + 2))
                    k0, k1 = VPART[part]
                    src = misc[:, :].rearrange("p (k s j d) -> p k s j d", s=2, j=HG, d=HD)
                    full = min(k1, KT - 1) - k0
                    for i in range(2):
                        s = 2 * half + i
                        bias = bv[:, 64 * s:64 * s + 64].rearrange("p (o j d) -> p o j d", o=1, d=HD)
                        ins = nc.vector.tensor_tensor(V[:, s, k0:k0 + full, :, 0:HD], src[:, 0:full, i],
                                                      bias.broadcast_to([P, full, HG, HD]), ALU.add)
                        if k1 == KT:
                            ins = nc.vector.tensor_tensor(V[0:LAST, s, KT - 1, :, 0:HD], src[0:LAST, full, i],
                                                          bias[0:LAST, 0], ALU.add)
                    ins.then_inc(misc_free, 1)

            def row_maxima(G, par):
                dve.wait_ge(max_done, NCHUNK * (G + 1))
                nc.vector.tensor_reduce(mxr[:, par, :], mx[:, par, :].rearrange("p (i c) -> p i c", c=4),
                                        AX.X, ALU.max).then_inc(rowmax_done, 1)

            def reduce_chunk(G, s, i):
                dve.wait_ge(max_ready, NCHUNK * G + i + 1)
                nc.vector.tensor_reduce(mx[:, s % 2, i:i + 1], mxp[:, (i + s) % 3, 0:CHUNK], AX.X, ALU.max).then_inc(max_done, 1)
                if i == NCHUNK - 1:
                    row_maxima(G, s % 2)

            def split_steps(n, kind, rest, parts):
                done = split_count(n, kind, 0) - 4
                nc.vector.tensor_copy(parts[0], rest).then_inc(split_step, 1)
                yield
                dve.wait_ge(split_step, done + 1)
                nc.vector.tensor_tensor(rest, rest, parts[0], ALU.subtract).then_inc(split_step, 1)
                yield
                dve.wait_ge(split_step, done + 2)
                nc.vector.tensor_copy(parts[1], rest).then_inc(split_step, 1)
                yield
                dve.wait_ge(split_step, done + 3)
                nc.vector.tensor_tensor(parts[2], rest, parts[1], ALU.subtract).then_inc(split_step, 1)
                yield

            statistics(0, QT)
            for t in range(QT):
                normalize_tokens(0, t)
            statistics(QT, NT)
            at = {j: i for i, j in enumerate(PROLOGUE)}
            dve.wait_ge(misc_free, at["q", 0] + 1)
            for _ in split_steps(0, "q", qf[:, 0, :], [qparts[:, i, 0, :] for i in range(3)]):
                pass
            if mask is not None:
                dve.wait_ge(mask_out, 16 * HG)
            dve.wait_ge(misc_free, at["k", (0, 3)] + 1)
            dve.wait_ge(v_clear, 2)
            for i, _ in enumerate(split_steps(0, "k", kf[:, :], [kparts[:, i, 0:KV] for i in range(3)])):
                take(0, at["v", (0, i)], "v", (0, i), True)
            for i in range(NCHUNK):
                reduce_chunk(0, 0, i)
            take(0, len(PROLOGUE) - 1, "mx", -1, True)
            for i in range(LEAD):
                reduce_chunk(1, 1, i)

            def body(b, first, last):
                before = jobs_before(b, first)
                jobs = {(g, kt): (i, job, arg) for i, (g, kt, job, arg) in enumerate(jobs_of(first, last))}
                for g in range(NG):
                    for kt in range(KT):
                        chunks = chunks_at(g, kt, last)
                        for tg, c in chunks[:2]:
                            reduce_chunk(NG * b + tg, tg % NG, c)
                        i, job, arg = jobs.get((g, kt), (0, "", 0))
                        if job and job not in ON_ACT:
                            n = b if job != "v" or arg[0] == 1 else b + 1
                            take(n, before + i, job, arg, first and n is b)
                        for tg, c in chunks[2:]:
                            reduce_chunk(NG * b + tg, tg % NG, c)
                        if g == 0 and 3 <= kt < 3 + QT and not last:
                            normalize_tokens(b + 1, kt - 3)

            body(0, True, False)
            with dve.Fori(1, B - 1) as b:
                body(b, False, False)
            body(B - 1, False, True)
            tail = jobs_before(B - 1, False) + len(jobs_of(False, True))
            for i, (job, arg) in enumerate(TAIL):
                if job not in ON_ACT:
                    take(B - (job == "norm"), tail + i, job, arg, False)

        @block.tensor
        def _(pe):
            pe.wait_ge(first_in, FIRST_IN)

            def start(n, job, kind, arg, parts=(0, 1)):
                if 0 in parts and not (isinstance(job, int) and job == 0):
                    pe.wait_ge(misc_free, job)
                mm = None
                if kind == "xt" and 0 in parts:
                    pe.wait_ge(xn_done, QT * (n + 1))
                if kind == "k" and 0 in parts:
                    pe.wait_ge(ctx_in, 16 * (n + 1))
                if kind == "norm" and 0 in parts:
                    pe.wait_ge(osb_done, NG * n + arg)
                if kind == "mx" and 0 in parts:
                    pe.wait_ge(rowmax_done, NG * n + arg + 2)
                for part in parts:
                    if kind in ("xt", "ot", "norm"):
                        for t in (2 * part, 2 * part + 1):
                            src = {"xt": xn[:, t, P * arg:P * arg + P] if arg < DK else None,
                                   "ot": on[:, t, P * arg:P * arg + P] if arg < DK else None,
                                   "norm": osb[:, P * t:P * t + P]}[kind]
                            mm = nc.tensor.transpose(misc[:, P * t:P * t + P], src, ident[:, :])
                    if kind == "mx" and part == 0:
                        mm = nc.tensor.transpose(misc[0:16, 0:P], mxr[:, (arg + 1) % 2, :], ident[:, :])
                    if kind == "q":
                        mm = nc.tensor.matmul(misc[:, :], wq[:, part, P * arg:P * arg + P], xnT[:, part, :],
                                              start=part == 0, stop=part == DK - 1)
                    if kind == "k":
                        half, c = arg
                        o, w = KCH[c]
                        mm = nc.tensor.matmul(misc[:, 0:w], wk[:, part, P * half:P * half + P],
                                              ctx_sb[:, part, o:o + w], start=part == 0, stop=part == DK - 1)
                    if kind == "v":
                        half, i = arg
                        k0, k1 = VPART[i]
                        mid = (k0 + k1) // 2
                        for kt in (range(k0, mid) if part == 0 else range(mid, k1)):
                            rows = P if kt < KT - 1 else LAST
                            for k in range(DK):
                                mm = nc.tensor.matmul(misc[0:rows, P * (kt - k0):P * (kt - k0) + P],
                                                      ctx_sb[:, k, P * kt:P * kt + rows], wv[:, k, P * half:P * half + P],
                                                      start=k == 0, stop=k == DK - 1)
                    if kind == "out":
                        for k in range(DK):
                            a = P * (2 * arg + part)
                            mm = nc.tensor.matmul(misc[:, D * part:D * part + D], oT[:, k, a:a + P], wo[:, k, :],
                                                  start=k == 0, stop=k == DK - 1)
                if (1 if kind != "mx" else 0) in parts:
                    mm.then_inc(misc_full, 1)

            def max_chunk(G, s, i, n):
                h, t, c = i // (QT * 4), i // 4 % QT, i % 4
                if i == 0:
                    pe.wait_ge(q_in[s], Q_IN * (n + 1))
                    pe.wait_ge(k_in[s], K_IN * (n + 1))
                if i >= 3:
                    pe.wait_ge(max_done, NCHUNK * G + i - 2)
                elif not (isinstance(G, int) and G == 0):
                    pe.wait_ge(max_done, NCHUNK * G - ((0, 2, 1) if s == 0 else (2, 1, 0))[i])
                nc.tensor.matmul(mxp[:, (i + s) % 3, 0:CHUNK], QS[0:ROW_MASK + 1, s, h, P * t:P * t + P],
                                 KS[0:ROW_MASK + 1, s, h, CHUNK_AT[c]:CHUNK_AT[c] + CHUNK],
                                 start=True, stop=True).then_inc(max_ready, 1)

            def score(G, s, kt, h, first):
                j = HG * kt + h
                rows = P if kt < KT - 1 else LAST
                if j >= 3:
                    pe.wait_ge(exp_done, NS * G + j - 2)
                elif not first:
                    pe.wait_ge(exp_done, NS * G - ((0, 2, 1) if s == 0 else (2, 1, 0))[j])
                nc.tensor.matmul(sc[0:rows, (j + s) % 3, :], KS[:, s, h, P * kt:P * kt + rows], QS[:, s, h, :],
                                 start=True, stop=True).then_inc(score_ready, 1)

            def pv(G, s, kt, first):
                rows = P if kt < KT - 1 else LAST
                slot = kt % 2 if kt < KT - 1 else 2
                pe.wait_ge(exp_done, NS * G + HG * kt + HG)
                if kt == 0 and not first:
                    pe.wait_ge(osb_done, G)
                for j in range(HG):
                    mm = nc.tensor.matmul(avp[32 * j:32 * j + 32, :], V[0:rows, s, kt, j, :], pr[0:rows, slot, j, :],
                                          start=kt == 0, stop=kt == KT - 1)
                mm.then_inc(av_done, 1)

            for i, (job, arg) in enumerate(FIRST):
                if job == "v" and arg == (0, 0):
                    pe.wait_ge(weights_in, WEIGHTS_IN)
                start(0, i, job, arg)
            pe.wait_ge(rows_in, 32)
            for i in range(NCHUNK):
                max_chunk(0, 0, i, 0)
                if i % 8 == 7 and i // 8 < len(BESIDE):
                    start(0, len(FIRST) + i // 8, *BESIDE[i // 8])
            start(0, len(PROLOGUE) - 1, "mx", -1)
            for i in range(LEAD):
                max_chunk(1, 1, i, 0)
            pe.wait_ge(v_clear, 2)

            def body(b, first, last):
                before = jobs_before(b, first)
                jobs = {(g, kt): (i, job, arg) for i, (g, kt, job, arg) in enumerate(jobs_of(first, last))}
                for g in range(NG):
                    G = NG * b + g
                    none_before = first and g == 0
                    for kt in range(KT):
                        if kt == 0:
                            pe.wait_ge(c_in[g], C_IN * (b + 1))
                        chunks = chunks_at(g, kt, last)
                        i, job, arg = jobs.get((g, kt), (0, "", 0))
                        n = b + 1 if job in AHEAD or (job == "v" and arg[0] == 0) else b
                        for h in range(HG):
                            score(G, g, kt, h, none_before)
                            for tg, c in (chunks[h:h + 1] if h < HG - 1 else chunks[h:]):
                                max_chunk(NG * b + tg, tg % NG, c, b + tg // NG)
                            if h < 2 and job:
                                start(n, before + i, job, arg, (h,))
                            if h == 2 and kt > 0:
                                pv(G, g, kt - 1, none_before)
                            elif h == 2 and not none_before:
                                pv(G - 1, (g - 1) % NG, KT - 1, False)

            body(0, True, False)
            with pe.Fori(1, B - 1) as b:
                body(b, False, False)
            body(B - 1, False, True)
            pv(NG * B - 1, NG - 1, KT - 1, False)
            tail = jobs_before(B - 1, False) + len(jobs_of(False, True))
            for i, (job, arg) in enumerate(TAIL):
                start(B - 1, tail + i, job, arg)


def rsqrt_steps(nc, dve, done, n, ve, tmp, rs):
    y, h = tmp[:, 0, :], tmp[:, 1, :]
    nc.vector.reciprocal(rs[:, :], y).then_inc(done, 1)
    dve.wait_ge(done, n + 1)
    nc.vector.tensor_tensor(h, rs[:, :], rs[:, :], ALU.mult).then_inc(done, 1)
    dve.wait_ge(done, n + 2)
    nc.vector.tensor_tensor(h, h, ve[:, :], ALU.mult).then_inc(done, 1)
    dve.wait_ge(done, n + 3)
    nc.vector.tensor_scalar(h, h, -0.5, 1.5, ALU.mult, ALU.add).then_inc(done, 1)
    dve.wait_ge(done, n + 4)
    nc.vector.tensor_tensor(rs[:, :], rs[:, :], h, ALU.mult).then_inc(done, 1)
    dve.wait_ge(done, n + 5)


def normalized_transposed(nc, name, ctx, x, ident, kept):
    sb = lambda n, s, d=F32: ctx.enter_context(nc.sbuf_tensor(f"{name}_{n}", s, d))
    sem = lambda n: nc.alloc_semaphore(f"{name}_{n}")
    tp = ctx.enter_context(nc.psum_tensor(f"{name}_tp", [P, 2, 2, DK, P], F32))
    xn, xnT = sb("xn", [P, kept, D]), sb("xnT", [P, DK, B * S])
    st, mv = sb("st", [P, NT, 6]), sb("mv", [P, NT, 2])
    ve, rs, tmp = sb("ve", [P, NT]), sb("rs", [P, NT]), sb("tmp", [P, 2, NT])
    ln_v, ln_s, xn_done = sem("ln_v"), sem("ln_s"), sem("xn_done")
    tp_ready, xnT_done = sem("tp_ready"), sem("xnT_done")
    PAIRS = NT // 2

    def vector(dve):
        for t in range(NT):
            last = nc.vector.bn_stats(st[:, t, :], x[:, t, :])
        last.then_inc(ln_v, 1)
        dve.wait_ge(ln_v, 1)
        for t in range(NT):
            last = nc.vector.bn_aggr(mv[:, t, :], st[:, t, :])
        last.then_inc(ln_s, 1)
        dve.wait_ge(ln_s, 1)
        nc.vector.tensor_scalar(ve[:, :], mv[:, :, 1], EPS, None, ALU.add).then_inc(ln_v, 1)
        dve.wait_ge(ln_s, 2)
        rsqrt_steps(nc, dve, ln_v, 2, ve, tmp, rs)
        for t in range(NT):
            if t >= kept:
                dve.wait_ge(tp_ready, (t - kept) // 2 + 1)
            nc.vector.tensor_scalar(xn[:, t % kept, :], x[:, t, :], mv[:, t, 0:1], rs[:, t:t + 1],
                                    ALU.subtract, ALU.mult).then_inc(xn_done, 1)

    def tensor(pe):
        for p in range(PAIRS):
            pe.wait_ge(xn_done, 2 * p + 2)
            if p >= 2:
                pe.wait_ge(xnT_done, p - 1)
            for i in range(2):
                for k in range(DK):
                    mm = nc.tensor.transpose(tp[:, p % 2, i, k, :], xn[:, (2 * p + i) % kept, P * k:P * k + P], ident[:, :])
            mm.then_inc(tp_ready, 1)

    def scalar(act):
        act.wait_ge(ln_v, 2)
        nc.scalar.activation(tmp[:, 0, :], ve[:, :], ACT.Sqrt).then_inc(ln_s, 1)
        for p in range(PAIRS):
            act.wait_ge(tp_ready, p + 1)
            dst = xnT[:, :, 2 * P * p:2 * P * p + 2 * P].rearrange("p k (i n) -> p i k n", i=2)
            nc.scalar.copy(dst, tp[:, p % 2]).then_inc(xnT_done, 1)

    return xn, xn_done, xnT, xnT_done, PAIRS, vector, tensor, scalar


def swiglu(nc, x, ident, w_gate, w_up, w_down):
    MT = FF0 // P
    NC = B
    with ExitStack() as ctx:
        sb = lambda n, s, d=F32: ctx.enter_context(nc.sbuf_tensor(f"ffn_{n}", s, d))
        sem = lambda n: nc.alloc_semaphore(f"ffn_{n}")
        _, _, xnT, xnT_done, PAIRS, ln_vector, ln_tensor, ln_scalar = normalized_transposed(nc, "ffn", ctx, x, ident, 4)
        gp = ctx.enter_context(nc.psum_tensor("ffn_gate", [P, 2, S], F32))
        up = ctx.enter_context(nc.psum_tensor("ffn_up", [P, 2, S], F32))
        yp = ctx.enter_context(nc.psum_tensor("ffn_y", [P, QT, D], F32))
        wi = sb("wi", [P, 3, DK * FF0], I32)
        wf = sb("wf", [P, 3, DK * FF0])
        wg, wu = (wf[:, i, :].rearrange("p (k n) -> p k n", k=DK) for i in range(2))
        wd = wf[:, 2, :].rearrange("p (m n) -> p m n", m=MT)
        sg, hT = sb("sg", [P, 2, S]), sb("hT", [P, MT, S])
        w_in = [sem(f"w_in{i}") for i in range(3)]
        w_cast = sem("w_cast")
        gate_ready, up_ready, silu_done, h_done = sem("gate_ready"), sem("up_ready"), sem("silu_done"), sem("h_done")
        down_done, y_taken = sem("down_done"), sem("y_taken")
        block = ctx.enter_context(nc.Block())

        @block.sync
        def _(sp):
            for i, w in enumerate((w_gate, w_up)):
                sp.dma_start(wi[:, i, :].rearrange("p (k n) -> p k n", k=DK),
                             w.rearrange("(k p) n -> p k n", p=P)).then_inc(w_in[i], 16)
            sp.dma_start(wi[:, 2, :].rearrange("p (m n) -> p m n", m=MT),
                         w_down.rearrange("(m p) n -> p m n", p=P)).then_inc(w_in[2], 16)

        @block.gpsimd
        def _(pool):
            for i in range(3):
                pool.wait_ge(w_in[i], 16)
                nc.gpsimd.tensor_copy(wf[:, i, :], wi[:, i, :]).then_inc(w_cast, 1)

        def chunks(engine, body):
            body(0)
            with engine.Fori(1, NC) as c:
                body(c)

        @block.scalar
        def _(act):
            ln_scalar(act)

            def body(c):
                for m in range(MT):
                    q = MT * c + m
                    act.wait_ge(gate_ready, q + 1)
                    if not (isinstance(q, int) and q < 2):
                        act.wait_ge(h_done, q - 1)
                    nc.scalar.activation(sg[:, m % 2, :], gp[:, m % 2, :], ACT.Silu, scale=INV127).then_inc(silu_done, 1)

            chunks(act, body)

        @block.vector
        def _(dve):
            ln_vector(dve)

            def take_y(c):
                dve.wait_ge(down_done, MT * (c + 1))
                for i in range(2):
                    t = QT * c + 2 * i
                    xs = x[:, t:t + 2, :] if isinstance(c, int) else x[:, bass.ds(t, 2), :]
                    ins = nc.vector.scalar_tensor_tensor(out=xs, in0=yp[:, 2 * i:2 * i + 2, :], scalar=INV127, in1=xs,
                                                         op0=ALU.mult, op1=ALU.add)
                ins.then_inc(y_taken, 1)

            def body(c):
                for m in range(MT):
                    if m == 1 and not (isinstance(c, int) and c == 0):
                        take_y(c - 1)
                    q = MT * c + m
                    dve.wait_ge(silu_done, q + 1)
                    dve.wait_ge(up_ready, q + 1)
                    if not isinstance(c, int):
                        dve.wait_ge(down_done, q - MT + 1)
                    nc.vector.scalar_tensor_tensor(out=hT[:, m, :], in0=up[:, m % 2, :], scalar=INV127,
                                                   in1=sg[:, m % 2, :], op0=ALU.mult, op1=ALU.mult).then_inc(h_done, 1)

            chunks(dve, body)
            take_y(NC - 1)

        @block.tensor
        def _(pe):
            ln_tensor(pe)
            pe.wait_ge(xnT_done, PAIRS)
            pe.wait_ge(w_cast, 3)

            def down(q, m, c):
                pe.wait_ge(h_done, q + 1)
                if m == 0 and not (isinstance(c, int) and c == 0):
                    pe.wait_ge(y_taken, c)
                for t in range(QT):
                    mm = nc.tensor.matmul(yp[:, t, :], hT[:, m, P * t:P * t + P], wd[:, m, :],
                                          start=m == 0 and t % 2 == 0, stop=m == MT - 1, skip_group_check=True)
                mm.then_inc(down_done, 1)

            def body(c):
                tokens = slice(S * c, S * c + S) if isinstance(c, int) else bass.ds(S * c, S)
                for m in range(MT):
                    q = MT * c + m
                    for w, bank, ready, free in ((wg, gp, gate_ready, silu_done), (wu, up, up_ready, h_done)):
                        if not (isinstance(q, int) and q < 2):
                            pe.wait_ge(free, q - 1)
                        for k in range(DK):
                            mm = nc.tensor.matmul(bank[:, m % 2, :], w[:, k, P * m:P * m + P], xnT[:, k, tokens],
                                                  start=k == 0, stop=k == DK - 1)
                        mm.then_inc(ready, 1)
                    if not (isinstance(q, int) and q == 0):
                        down(q - 1, (m - 1) % MT, c if m > 0 else c - 1)

            chunks(pe, body)
            down(MT * NC - 1, MT - 1, NC - 1)


def route(nc, ctx, sb, sem, const, xnT, gw, gb, w_in, w_in_n, plan):
    gather_row, scatter_row, weight, tile_expert = plan
    iota, before, token, slot_no = const
    lg, m8, i8 = sb("lg", [P, NT, E]), sb("m8", [P, NT, 8]), sb("i8", [P, NT, 8], U32)
    top, wt = sb("top", [P, 2, NT]), sb("wt", [P, 2, NT])
    ex, den = sb("ex", [P, NT]), sb("den", [P, NT])
    hot = sb("hot", [P, 2 * NT, E])
    chosen = sb("chosen", [P, NT * E])
    ones = sb("ones", [P, P])
    run = sb("run", [P, 2, NT, E])
    tiles_i, tiles = sb("tiles_i", [P, 2, E], I32), sb("tiles", [P, E])
    ends = sb("ends", [P, 2, E])
    slot, hi, lo = sb("slot", [P, 2 * NT]), sb("hi", [P, 2 * NT]), sb("lo", [P, 2 * NT])
    slot_i = sb("slot_i", [P, 2, 2 * NT], I32)
    at = sb("at", [P, NT, E])
    picked = sb("picked", [P, 2 * NT, E])
    entry = xnT[:, :, :].rearrange("p k n -> p (k n)")[:, 0:6 * NT * SLOT_TILES].rearrange(
        "p (q n w) -> p q n w", q=3, n=2 * NT)
    place = sb("place", [P, 2, 8, P])
    rows, pad = sb("rows", [P, SLOT_TILES]), sb("pad", [P, SLOT_TILES])
    past = sb("past", [P, SLOT_TILES, E])
    past_n = sb("past_n", [P, SLOT_TILES])
    lp = ctx.enter_context(nc.psum_tensor("moe_l", [P, 512], F32))
    cp = ctx.enter_context(nc.psum_tensor("moe_c", [P, 2, NT * E], F32))
    tbl = ctx.enter_context(nc.psum_tensor("moe_tbl", [P, 2, SLOT_TILES], F32))
    lg_ready, step_v, ex_done = sem("lg_ready"), sem("step_v"), sem("ex_done")
    diff_done, chosen_done, counts_ready = sem("diff_done"), sem("chosen_done"), sem("counts_ready")
    entry_done, place_done, place_used, tbl_ready = sem("entry_done"), sem("place_done"), sem("place_used"), sem("tbl_ready")
    GROUPS = 2 * NT // 8

    def tensor(pe):
        pe.wait_ge(w_in, w_in_n)
        for t in range(NT):
            for k in range(DK):
                mm = nc.tensor.matmul(lp[:, E * t:E * t + E], xnT[:, k, P * t:P * t + P], gw[:, k, :],
                                      start=k == 0, stop=k == DK - 1)
        mm.then_inc(lg_ready, 1)
        pe.wait_ge(chosen_done, 1)
        nc.tensor.matmul(cp[:, 0, :], before, chosen[:, :], start=True, stop=True)
        nc.tensor.matmul(cp[:, 1, :], ones[:, :], chosen[:, :], start=True, stop=True).then_inc(counts_ready, 1)
        pe.wait_ge(entry_done, 1)
        for g in range(GROUPS):
            pe.wait_ge(place_done, g + 1)
            for i in range(8):
                n = 8 * g + i
                mm = nc.tensor.matmul(tbl[:, :, :], place[:, g % 2, i, :], entry[:, 1:3, n, :],
                                      start=n == 0, stop=n == 2 * NT - 1)
            mm.then_inc(place_used, 1)

    def scalar(act):
        act.wait_ge(diff_done, 1)
        nc.scalar.activation(ex[:, :], den[:, :], ACT.Exp).then_inc(ex_done, 1)

    def vector(dve):
        n = [0]

        def step(ins):
            n[0] += 1
            ins.then_inc(step_v, 1)
            dve.wait_ge(step_v, n[0])

        def each(a, width):
            m = a.shape[-1]
            return a.rearrange("p (n o) -> p n o", o=1).broadcast_to([P, m, width])

        def over(a, count):
            return a.rearrange("p (o w) -> p o w", o=1).broadcast_to([P, count, a.shape[-1]])

        nc.vector.memset(ones[:, :], 1.0)
        dve.wait_ge(lg_ready, 1)
        dve.wait_ge(w_in, w_in_n)
        step(nc.vector.tensor_tensor(lg[:, :, :], lp[:, 0:NT * E].rearrange("p (t e) -> p t e", e=E),
                                     over(gb[:, :], NT), ALU.add))
        for t in range(NT):
            last = nc.vector.max(m8[:, t, :], lg[:, t, :])
        step(last)
        for t in range(NT):
            last = nc.vector.max_index(i8[:, t, :], m8[:, t, :], lg[:, t, :])
        step(last)
        nc.vector.tensor_tensor(den[:, :], m8[:, :, 1], m8[:, :, 0], ALU.subtract).then_inc(diff_done, 1)
        step(nc.vector.tensor_copy(top[:, :, :], i8[:, :, 0:2].rearrange("p t i -> p i t")))
        step(nc.vector.tensor_tensor(hot[:, :, :], over(iota[:, 0:E], 2 * NT),
                                     each(top[:, :, :].rearrange("p i t -> p (i t)"), E), ALU.is_equal))
        step(nc.vector.tensor_tensor(chosen[:, :], hot[:, 0:NT, :].rearrange("p t e -> p (t e)"),
                                     hot[:, NT:2 * NT, :].rearrange("p t e -> p (t e)"), ALU.add))
        nc.vector.sem_inc(chosen_done, 1)
        dve.wait_ge(ex_done, 1)
        step(nc.vector.tensor_scalar(den[:, :], ex[:, :], 1.0, None, ALU.add))
        step(nc.vector.reciprocal(wt[:, 0, :], den[:, :]))
        step(nc.vector.tensor_tensor(wt[:, 1, :], ex[:, :], wt[:, 0, :], ALU.mult))
        dve.wait_ge(counts_ready, 1)
        step(nc.vector.tensor_copy(run[:, 0], cp[:, 1, :].rearrange("p (t e) -> p t e", e=E)))
        a, s = 0, 1
        while s < NT:
            nc.vector.tensor_copy(run[:, 1 - a, 0:s, :], run[:, a, 0:s, :])
            step(nc.vector.tensor_tensor(run[:, 1 - a, s:NT, :], run[:, a, s:NT, :], run[:, a, 0:NT - s, :], ALU.add))
            a, s = 1 - a, 2 * s
        step(nc.vector.tensor_scalar(tiles_i[:, 0, :], run[:, a, NT - 1, :], float(P - 1), None, ALU.add))
        step(nc.vector.tensor_scalar(tiles_i[:, 1, :], tiles_i[:, 0, :], 7, None, ALU.logical_shift_right))
        nc.vector.tensor_copy(ends[:, 0, :], tiles_i[:, 1, :])
        step(nc.vector.tensor_copy(tiles[:, :], tiles_i[:, 1, :]))
        b, s = 0, 1
        while s < E:
            nc.vector.tensor_copy(ends[:, 1 - b, 0:s], ends[:, b, 0:s])
            step(nc.vector.tensor_tensor(ends[:, 1 - b, s:E], ends[:, b, s:E], ends[:, b, 0:E - s], ALU.add))
            b, s = 1 - b, 2 * s
        step(nc.vector.tensor_tensor(tiles[:, :], ends[:, b, :], tiles[:, :], ALU.subtract))
        step(nc.vector.tensor_tensor(at[:, :, :], run[:, a], cp[:, 1, :].rearrange("p (t e) -> p t e", e=E), ALU.subtract))
        step(nc.vector.tensor_tensor(at[:, :, :], at[:, :, :], cp[:, 0, :].rearrange("p (t e) -> p t e", e=E), ALU.add))
        step(nc.vector.scalar_tensor_tensor(out=at[:, :, :], in0=over(tiles[:, :], NT), scalar=float(P), in1=at[:, :, :],
                                            op0=ALU.mult, op1=ALU.add))
        nc.vector.tensor_tensor(picked[:, 0:NT, :], hot[:, 0:NT, :], at[:, :, :], ALU.mult)
        step(nc.vector.tensor_tensor(picked[:, NT:2 * NT, :], hot[:, NT:2 * NT, :], at[:, :, :], ALU.mult))
        step(nc.vector.tensor_reduce(slot[:, :], picked[:, :, :], AX.X, ALU.add))
        step(nc.vector.tensor_copy(slot_i[:, 0, :], slot[:, :]))
        step(nc.vector.tensor_scalar(slot_i[:, 1, :], slot_i[:, 0, :], 7, None, ALU.logical_shift_right))
        step(nc.vector.tensor_copy(hi[:, :], slot_i[:, 1, :]))
        step(nc.vector.scalar_tensor_tensor(out=lo[:, :], in0=hi[:, :], scalar=-float(P), in1=slot[:, :],
                                            op0=ALU.mult, op1=ALU.add))
        step(nc.vector.tensor_tensor(entry[:, 0], over(iota[:, 0:SLOT_TILES], 2 * NT), each(hi[:, :], SLOT_TILES),
                                     ALU.is_equal))
        nc.vector.tensor_tensor(entry[:, 1], entry[:, 0], each(token, SLOT_TILES), ALU.mult)
        nc.vector.tensor_tensor(entry[:, 2], entry[:, 0], each(wt[:, :, :].rearrange("p i t -> p (i t)"), SLOT_TILES),
                                ALU.mult).then_inc(entry_done, 1)
        for g in range(GROUPS):
            if g >= 2:
                dve.wait_ge(place_used, g - 1)
            nc.vector.tensor_tensor(place[:, g % 2], over(iota, 8), each(lo[:, 8 * g:8 * g + 8], P),
                                    ALU.is_equal).then_inc(place_done, 1)
        step(nc.vector.tensor_tensor(past[:, :, :], each(iota[:, 0:SLOT_TILES], E), over(ends[:, b, :], SLOT_TILES),
                                     ALU.is_ge))
        step(nc.vector.tensor_reduce(past_n[:, :], past[:, :, :], AX.X, ALU.add))
        step(nc.vector.tensor_scalar(tile_expert, past_n[:, :], float(E - 1), None, ALU.min))
        dve.wait_ge(place_used, GROUPS)
        nc.vector.tensor_copy(weight, tbl[:, 1, :])
        step(nc.vector.tensor_scalar(rows[:, :], tbl[:, 0, :], float(B * S), None, ALU.add))
        step(nc.vector.tensor_scalar(pad[:, :], rows[:, :], float(B * S), slot_no, ALU.is_equal, ALU.mult))
        step(nc.vector.tensor_tensor(pad[:, :], pad[:, :], rows[:, :], ALU.add))
        nc.vector.tensor_copy(scatter_row, pad[:, :])
        step(nc.vector.tensor_scalar(gather_row, pad[:, :], float(B * S - 1), None, ALU.min))

    return vector, tensor, scalar


def experts(nc, x, ident, route_const, gate_w, gate_b, w1, b1, w2, b2, out):
    MT = FF // P
    HALF = FF // 2
    sem = lambda n: nc.alloc_semaphore(f"moe_{n}")
    xn_rows = nc.dram_tensor("moe_xn_rows", (B * S, D), F32).ap()
    xn_out, x_out = sem("xn_out"), sem("x_out")
    w_in = sem("w_in")
    e_in = [sem(f"e_in{e}") for e in range(E)]
    with ExitStack() as outer:
        keep = lambda n, s, d=F32: outer.enter_context(nc.sbuf_tensor(f"moe_{n}", s, d))
        w1s, w2s = keep("w1", [P, E, DK, FF]), keep("w2", [P, E, MT, D])
        b1c, b2b = keep("b1", [P, E, MT]), keep("b2", [P, E, D])
        gather_row, scatter_row = keep("gather_row", [P, SLOT_TILES], U32), keep("scatter_row", [P, SLOT_TILES], U32)
        weight, tile_expert = keep("weight", [P, SLOT_TILES]), keep("tile_expert", [P, SLOT_TILES], I32)

        with ExitStack() as ctx:
            sb = lambda n, s, d=F32: ctx.enter_context(nc.sbuf_tensor(f"route_{n}", s, d))
            xn, xn_done, xnT, xnT_done, PAIRS, ln_vector, ln_tensor, ln_scalar = normalized_transposed(
                nc, "moe", ctx, x, ident, NT)
            gw, gb = sb("gw", [P, DK, E]), sb("gb", [P, E])
            rc = sb("const", [P, ROUTE_CONST])
            const = rc[:, 0:P], rc[:, P:2 * P], rc[:, 2 * P:2 * P + 2 * NT], rc[:, 2 * P + 2 * NT:]
            plan = gather_row[:, :], scatter_row[:, :], weight[:, :], tile_expert[:, :]
            route_vector, route_tensor, route_scalar = route(nc, ctx, sb, sem, const, xnT, gw, gb, w_in, 80, plan)
            block = ctx.enter_context(nc.Block())

            @block.sync
            def _(sp):
                sp.dma_start(gw[:, :, :], gate_w.rearrange("(k p) n -> p k n", p=P)).then_inc(w_in, 16)
                sp.dma_start(gb[:, :], gate_b.partition_broadcast(P)).then_inc(w_in, 16)
                sp.dma_start(rc[:, :], route_const).then_inc(w_in, 16)
                sp.dma_start(b1c[:, :, :], b1).then_inc(w_in, 16)
                sp.dma_start(b2b[:, :, :], b2.partition_broadcast(P)).then_inc(w_in, 16)
                for e in range(E):
                    if e == 1:
                        for i in range(4):
                            sp.wait_ge(xn_done, 4 * i + 4)
                            sp.dma_start(xn_rows[4 * P * i:4 * P * i + 4 * P, :].rearrange("(t p) d -> p t d", p=P),
                                         xn[:, 4 * i:4 * i + 4, :]).then_inc(xn_out, 16)
                        sp.dma_start(out[0:B * S, :].rearrange("(t p) d -> p t d", p=P), x[:, :, :]).then_inc(x_out, 16)
                        sp.dma_start(out[B * S:, :], x[:, 0, :]).then_inc(x_out, 16)
                    sp.dma_start(w1s[:, e], w1[e].rearrange("(k p) n -> p k n", p=P)).then_inc(e_in[e], 16)
                    sp.dma_start(w2s[:, e], w2[e].rearrange("(k p) n -> p k n", p=P)).then_inc(e_in[e], 16)
                sp.wait_ge(xn_out, 64)

            @block.scalar
            def _(act):
                ln_scalar(act)
                route_scalar(act)

            @block.vector
            def _(dve):
                ln_vector(dve)
                route_vector(dve)

            @block.tensor
            def _(pe):
                ln_tensor(pe)
                pe.wait_ge(xnT_done, PAIRS)
                route_tensor(pe)

        with ExitStack() as ctx:
            sb = lambda n, s, d=F32: ctx.enter_context(nc.sbuf_tensor(f"moe_{n}", s, d))
            ps = lambda n, s: ctx.enter_context(nc.psum_tensor(f"tile_{n}", s, F32))
            xg, xT = sb("xg", [P, 2, D]), sb("xT", [P, DK, P])
            g_row, s_row = [sb(f"g_row{i}", [P, 1], U32) for i in range(2)], sb("s_row", [P, 1], U32)
            idle = sb("idle", [P, 8])
            h_in, hT = sb("h_in", [P, FF]), sb("hT", [P, MT, P])
            b1e = sb("b1e", [P, 2, MT])
            y_sum, y_out = sb("y_sum", [P, 2, D]), sb("y_out", [P, 2, D])
            xp, hp, tp, yp = ps("xp", [P, 4, P]), ps("hp", [P, 2, HALF]), ps("tp", [P, MT, P]), ps("yp", [P, D])
            g_in = [sem("g_in0"), sem("g_in1")]
            added = [sem("added0"), sem("added1")]
            row_step, idle_done = sem("row_step"), sem("idle_done")
            xT_ready, xT_done, h_ready, h_taken = sem("xT_ready"), sem("xT_done"), sem("h_ready"), sem("h_taken")
            hT_ready, hT_done, b1_done = sem("hT_ready"), sem("hT_done"), sem("b1_done")
            y_ready, y_step, y_done = sem("y_ready"), sem("y_step"), sem("y_done")
            block = ctx.enter_context(nc.Block())
            LAST_TILE = SLOT_TILES - 1

            def tiles(engine, body):
                for j in range(3):
                    body(j, j % 2, j // 2)
                with engine.Fori(1, (SLOT_TILES - 5) // 2) as i:
                    body(2 * i + 1, 1, i)
                    body(2 * i + 2, 0, i + 1)
                for j in range(SLOT_TILES - 4, SLOT_TILES):
                    body(j, j % 2, j // 2)

            def col(a, j):
                return a[:, j:j + 1] if isinstance(j, int) else a[:, bass.ds(j, 1)]

            def expert_of(engine, j):
                at = slice(j, j + 1) if isinstance(j, int) else bass.ds(j, 1)
                return engine.value_load(tile_expert[0:1, at], min_val=0, max_val=E - 1)

            @block.gpsimd
            def _(pool):
                def gate(i):
                    return nc.gpsimd.tensor_tensor(idle[:, i:i + 1], idle[:, 0:1], idle[:, 0:1], ALU.mult)

                def gather(j, par):
                    nc.gpsimd.tensor_copy(g_row[par][:, :], col(gather_row, j)).then_inc(row_step, 1)
                    pool.wait_ge(row_step, j + 1 if isinstance(j, int) and j <= 3 else 2 * j - 2)
                    gate(2)
                    nc.gpsimd.indirect_dma_start(xg[:, par, :], None, xn_rows,
                                                 bass.IndirectOffsetOnAxis(ap=g_row[par][:, :], axis=0)).then_inc(g_in[par], 16)

                nc.gpsimd.memset(idle[:, :], 0.0).then_inc(idle_done, 1)
                pool.wait_ge(idle_done, 1)
                for j in range(3):
                    if j == 2:
                        pool.wait_ge(xT_ready, 1)
                        gate(5)
                    gather(j, j % 2)
                pool.wait_ge(x_out, 32)

                def body(j, par, pair):
                    if not isinstance(j, int) or j + 3 < SLOT_TILES:
                        pool.wait_ge(xT_ready, j + 2)
                        gate(1)
                        gather(j + 3, 1 - par)
                    pool.wait_ge(y_done, j + 1)
                    if not isinstance(j, int) or j > 0:
                        pool.wait_ge(added[1 - par], 16 * (pair + par))
                    gate(3)
                    nc.gpsimd.tensor_copy(s_row[:, :], col(scatter_row, j)).then_inc(row_step, 1)
                    pool.wait_ge(row_step, j + 1 + (j + 4 if not isinstance(j, int) or j + 3 < SLOT_TILES else SLOT_TILES))
                    gate(4)
                    nc.gpsimd.indirect_dma_start(out, bass.IndirectOffsetOnAxis(ap=s_row[:, :], axis=0), y_out[:, par, :], None,
                                                 compute_op=ALU.add).then_inc(added[par], 16)

                tiles(pool, body)
                pool.wait_ge(added[0], 16 * ((SLOT_TILES + 1) // 2))
                pool.wait_ge(added[1], 16 * (SLOT_TILES // 2))

            @block.scalar
            def _(act):
                def take_xT(j):
                    act.wait_ge(xT_ready, j + 1)
                    if not (isinstance(j, int) and j == 0):
                        act.wait_ge(h_ready, 2 * j)
                    nc.scalar.copy(xT[:, :, :], xp[:, 0:DK, :]).then_inc(xT_done, 1)

                take_xT(0)

                def body(j, par, pair):
                    e = expert_of(act, j)
                    nc.scalar.copy(b1e[:, par, :], b1c[:, bass.ds(e, 1), :]).then_inc(b1_done, 1)
                    if not isinstance(j, int) or j < LAST_TILE:
                        take_xT(j + 1)
                    act.wait_ge(b1_done, j + 1)
                    if not (isinstance(j, int) and j == 0):
                        act.wait_ge(y_ready, j)
                    for m in range(MT):
                        if m % (MT // 2) == 0:
                            act.wait_ge(hT_ready, 2 * j + 1 + m // (MT // 2))
                        last = nc.scalar.activation(hT[:, m, :], tp[:, m, :], ACT.Gelu, bias=b1e[:, par, m:m + 1])
                        if m % (MT // 2) == MT // 2 - 1:
                            last.then_inc(hT_done, 1)

                tiles(act, body)

            @block.vector
            def _(dve):
                def take_y(j, par, pair):
                    e = expert_of(dve, j)
                    if not (isinstance(j, int) and j < 2):
                        dve.wait_ge(added[par], 16 * pair)
                    dve.wait_ge(y_ready, j + 1)
                    nc.vector.tensor_tensor(y_sum[:, par, :], yp[:, :], b2b[:, bass.ds(e, 1), :].rearrange("p o d -> p (o d)"),
                                            ALU.add).then_inc(y_step, 1)
                    dve.wait_ge(y_step, j + 1)
                    nc.vector.tensor_scalar(y_out[:, par, :], y_sum[:, par, :], col(weight, j), None, ALU.mult).then_inc(y_done, 1)

                def body(j, par, pair):
                    for h in range(2):
                        dve.wait_ge(h_ready, 2 * j + h + 1)
                        if not (isinstance(j, int) and j == 0):
                            dve.wait_ge(hT_ready, 2 * j + h - 1)
                        nc.vector.tensor_copy(h_in[:, HALF * h:HALF * h + HALF], hp[:, h, :]).then_inc(h_taken, 1)
                    if not (isinstance(j, int) and j == 0):
                        take_y(j - 1, 1 - par, pair + par - 1)

                tiles(dve, body)
                take_y(LAST_TILE, LAST_TILE % 2, LAST_TILE // 2)

            @block.tensor
            def _(pe):
                def transpose_x(j, par, pair):
                    pe.wait_ge(g_in[par], 16 * (pair + 1))
                    if not (isinstance(j, int) and j == 0):
                        pe.wait_ge(xT_done, j)
                    for k in range(DK):
                        mm = nc.tensor.transpose(xp[:, k, :], xg[:, par, P * k:P * k + P], ident[:, :])
                    mm.then_inc(xT_ready, 1)

                def down(j, e):
                    pe.wait_ge(hT_done, 2 * j + 2)
                    if not (isinstance(j, int) and j == 0):
                        pe.wait_ge(y_done, j)
                    for m in range(MT):
                        mm = nc.tensor.matmul(yp[:, :], hT[:, m, :], w2s[:, bass.ds(e, 1), m, :],
                                              start=m == 0, stop=m == MT - 1)
                    mm.then_inc(y_ready, 1)

                transpose_x(0, 0, 0)
                for e in range(E):
                    pe.wait_ge(e_in[e], 32)

                def body(j, par, pair):
                    e = expert_of(pe, j)
                    pe.wait_ge(xT_done, j + 1)
                    for h in range(2):
                        if not (isinstance(j, int) and j == 0):
                            pe.wait_ge(h_taken, 2 * j + h - 1)
                        for k in range(DK):
                            mm = nc.tensor.matmul(hp[:, h, :], xT[:, k, :], w1s[:, bass.ds(e, 1), k, HALF * h:HALF * h + HALF],
                                                  start=k == 0, stop=k == DK - 1)
                        mm.then_inc(h_ready, 1)
                    if not isinstance(j, int) or j < LAST_TILE:
                        transpose_x(j + 1, 1 - par, pair + par)
                    if not (isinstance(j, int) and j == 0):
                        down(j - 1, expert_of(pe, j - 1))
                    for h in range(2):
                        pe.wait_ge(h_taken, 2 * j + h + 1)
                        if not (isinstance(j, int) and j == 0):
                            pe.wait_ge(hT_done, 2 * j + h - 1)
                        for m in range(MT // 2 * h, MT // 2 * (h + 1)):
                            mm = nc.tensor.transpose(tp[:, m, :], h_in[:, P * m:P * m + P], ident[:, :])
                        mm.then_inc(hT_ready, 1)

                tiles(pe, body)
                down(LAST_TILE, expert_of(pe, LAST_TILE))


def xattn_ffn_2(nc, ins, out):
    with ExitStack() as ctx:
        x = ctx.enter_context(nc.sbuf_tensor("x_sb", [P, NT, D], F32))
        ident = ctx.enter_context(nc.sbuf_tensor("ident_sb", [P, P], F32))
        x_in = nc.alloc_semaphore("x_in")
        with nc.Block() as block:
            @block.sync
            def _(sp):
                sp.dma_start(x[:, :, :], ins["x"].rearrange("(t p) d -> p t d", p=P)).then_inc(x_in, 16)
                sp.dma_start(ident[:, :], ins["ident"]).then_inc(x_in, 16)
                sp.wait_ge(x_in, 32)
        stacks = ins["k_rows"], ins["q_rows"], ins["ctxT"]
        attention(nc, "L0", x, ident, *stacks, ins["L0_wq"], ins["L0_wk"], ins["L0_wv"], ins["L0_wo"],
                  ins["L0_bq"], ins["L0_bk"], ins["L0_bv"], ins["L0_bo"], ins["mask"])
        swiglu(nc, x, ident, ins["w_gate"], ins["w_up"], ins["w_down"])
        attention(nc, "L1", x, ident, *stacks, ins["L1_wq"], ins["L1_wk"], ins["L1_wv"], ins["L1_wo"],
                  None, None, None, None, None)
        experts(nc, x, ident, ins["route_const"], ins["gate_w"], ins["gate_b"], ins["w1"], ins["b1"], ins["w2"], ins["b2"], out)




def route_constants(np):
    p = np.arange(P, dtype=np.float32)
    rows = p[:, None] + P * np.tile(np.arange(NT, dtype=np.float32), TOP) - B * S
    return np.concatenate([np.tile(p, (P, 1)), np.triu(np.ones((P, P), np.float32), 1), rows, p[:, None]], axis=1)


def kernel(**inputs):
    import numpy as _np
    import concourse.bacc as _bacc
    from concourse import mybir as _mybir
    from concourse.bass_utils import run_bass_kernel_spmd as _run

    a = {n: _np.asarray(v) for n, v in inputs.items()}
    order = _np.array([HD * (HG * g + j) + d for g in range(NG) for d in range(HD) for j in range(HG)])
    wkv, bkv = a["L0_xattn_W_kv"], a["L0_xattn_b_kv"]
    ones = 0x3F803F80
    k_rows = _np.full((3, NG * HG * KVP // 2), ones, _np.uint32)
    k_rows[0] = 0
    arrays = {
        "x": a["x"].reshape(B * S, D),
        "ident": _np.eye(P, dtype=_np.float32),
        "route_const": route_constants(_np),
        "k_rows": k_rows,
        "q_rows": _np.full((3, NG * HG * S // 2), ones, _np.uint32),
        "ctxT": a["ctx_1024"].transpose(0, 2, 1),
        "mask": a["mask_BxS2_bf1"].view(_np.uint8),
        "L0_wq": a["L0_xattn_W_q"][:, order], "L0_wk": wkv[:, :D][:, order], "L0_wv": wkv[:, D:],
        "L0_wo": a["L0_xattn_W_o"],
        "L0_bq": a["L0_xattn_b_q"][order].reshape(2, P).T, "L0_bk": bkv[:D][order].reshape(2, P).T,
        "L0_bv": bkv[D:], "L0_bo": a["L0_xattn_b_o"],
        "w_gate": a["L0_ffn_w_gate"].T, "w_up": a["L0_ffn_w_up"].T, "w_down": a["L0_ffn_w_down"].T,
        "L1_wq": a["L1_xattn_W_q"].T[:, order], "L1_wk": a["L1_xattn_W_k"].T[:, order],
        "L1_wv": a["L1_xattn_W_v"].T, "L1_wo": a["L1_xattn_W_o"].T,
        "gate_w": a["L1_ffn_gate_w"], "gate_b": a["L1_ffn_gate_b"],
        "w1": a["L1_ffn_w1"], "b1": a["L1_ffn_b1"].reshape(E, FF // P, P).transpose(2, 0, 1),
        "w2": a["L1_ffn_w2"], "b2": a["L1_ffn_b2"],
    }
    arrays = {n: _np.ascontiguousarray(v) for n, v in arrays.items()}
    nc = _bacc.Bacc("TRN2", target_bir_lowering=False, num_devices=1)
    ins = {n: nc.dram_tensor(f"in_{n}", v.shape, _mybir.dt.from_np(v.dtype), kind="ExternalInput").ap()
           for n, v in arrays.items()}
    out = nc.dram_tensor("out", (B * S + P, D), F32, kind="ExternalOutput").ap()
    xattn_ffn_2(nc, ins, out)
    r = _run(nc, [{f"in_{n}": v for n, v in arrays.items()}], core_ids=[0])
    return _np.asarray(r.results[0]["out"])[:B * S].reshape(B, S, D)
```

```python
from contextlib import ExitStack

import concourse.bass as bass
from concourse import mybir

ALU = mybir.AluOpType
ACT = mybir.ActivationFunctionType
AX = mybir.AxisListType
F32 = mybir.dt.float32
BF16 = mybir.dt.bfloat16
I32 = mybir.dt.int32
U32 = mybir.dt.uint32
F32R = mybir.dt.float32r
U8 = mybir.dt.uint8

P = 128
B, S, D = 4, 512, 256
H, HD = 16, 16
KV = 1601
KVP = KV + 1
KT = -(-KV // P)
LAST = KV - (KT - 1) * P
DK = D // P
NT = B * S // P
QT = S // P
HG = 4
NG = H // HG
Q_TERMS, K_TERMS = (0, 1, 2, 0, 1, 0), (0, 0, 0, 1, 1, 2)
TERMS = len(Q_TERMS)
ROW_MASK = TERMS * HD
ROW_C = ROW_MASK + 1
ROWS = ROW_C + 2
MASKED = -1.0e30
CLAMP = -1.0e20
EPS = 1e-5
FF0 = 768
E, FF = 8, 1024
INV127 = 1.0 / 127.0
TOP = 2
SLOT_TILES = (TOP * B * S + E * (P - 1)) // P
TABLE = SLOT_TILES + SLOT_TILES % 2
ROUTE_CONST = 2 * P + 2 * NT + 1

CHUNK = 401
CHUNK_AT = [0, 400, 800, 1200]
NCHUNK = HG * QT * len(CHUNK_AT)
LEAD = 20
NS = KT * HG
KCH = [(0, 401), (401, 400), (801, 400), (1201, 400)]
VPART = [(0, 4), (4, 7), (7, 10), (10, 13)]

JOBS = [
    (0, 1, "v", (1, 0)), (0, 2, "norm", 0), (0, 3, "v", (1, 1)), (0, 4, "v", (1, 2)), (0, 5, "v", (1, 3)),
    (0, 6, "ot", 0), (0, 7, "ot", 1), (0, 8, "out", 0), (0, 9, "out", 1), (0, 10, "mx", 0), (0, 11, "xt", 0),
    (0, 12, "xt", 1),
    (1, 0, "q", 0), (1, 1, "q", 1), (1, 2, "norm", 1), (1, 3, "k", (0, 0)), (1, 5, "k", (0, 1)),
    (1, 6, "k", (0, 2)), (1, 7, "k", (0, 3)), (1, 10, "mx", 1),
    (2, 2, "norm", 2), (2, 4, "v", (0, 0)), (2, 5, "v", (0, 1)), (2, 6, "v", (0, 2)), (2, 7, "v", (0, 3)),
    (2, 10, "mx", 2),
    (3, 2, "norm", 3), (3, 4, "k", (1, 0)), (3, 5, "k", (1, 1)), (3, 6, "k", (1, 2)), (3, 7, "k", (1, 3)),
    (3, 10, "mx", 3),
]
FIRST = ([("xt", 0), ("xt", 1), ("q", 0)] + [("k", (0, c)) for c in range(4)] + [("v", (0, i)) for i in range(4)])
FIRST_LOADED = ([("k", (0, c)) for c in range(2)] + [("xt", 0), ("xt", 1), ("q", 0)] + [("k", (0, c)) for c in range(2, 4)]
                + [("v", (0, i)) for i in range(4)])
BESIDE = [("q", 1)] + [("k", (1, c)) for c in range(4)] + [("v", (1, i)) for i in range(4)]
PER_JOB = 7
PROLOGUE_JOBS = len(FIRST) + len(BESIDE) + 1
TAIL = [("norm", 4), ("ot", 0), ("ot", 1), ("out", 0), ("out", 1)]
BEHIND = ("ot", "out")
ON_ACT = ("xt", "q", "k", "ot")
AHEAD = ("xt", "q", "k")


def jobs_of(first, last):
    out = []
    for g, kt, job, arg in JOBS:
        if first and g == 0 and (job in ("norm", "v") or job in BEHIND):
            continue
        if last and (job in AHEAD or (job == "v" and arg[0] == 0) or (job == "mx" and g == 3)):
            continue
        out.append((g, kt, job, arg))
    return out


SKIPPED = len(JOBS) - len(jobs_of(True, False))


def jobs_before(b, first):
    return PROLOGUE_JOBS + (0 if first else b * len(JOBS) - SKIPPED)


def chunks_at(g, kt, last):
    lo, hi = LEAD + 5 * kt, LEAD + min(5 * kt + 5, NCHUNK)
    out = [(g + 1 + r // NCHUNK, r % NCHUNK) for r in range(lo, hi)]
    return [(t, i) for t, i in out if not (last and t >= NG)]


def load_inputs(sp, bufs, done, w_q, w_k, w_v, w_o, ctxT, between=lambda: None):
    wq, wk, wv, wo, ctx_sb = bufs
    first_in, weights_in, ctx_in = done

    def load(dst, src, sem):
        sp.dma_start(dst[:, :, :], src.rearrange("(k p) n -> p k n", p=P)).then_inc(sem, 16)

    load(wq, w_q, first_in)
    load(wk, w_k, first_in)
    load(ctx_sb, ctxT[0], ctx_in)
    between()
    load(wv, w_v, weights_in)
    load(wo, w_o, weights_in)


def attention(nc, name, x, x_in, ident, bufs, done, loaded, stats, k_rows, q_rows, ctxT, w_q, w_k, w_v, w_o, b_q, b_k, b_v,
              b_o, mask):
    with ExitStack() as ctx:
        sb = lambda n, s, d=F32: ctx.enter_context(nc.sbuf_tensor(f"{name}_{n}", s, d))
        ps = lambda n, s: ctx.enter_context(nc.psum_tensor(f"{name}_{n}", s, F32))
        sem = lambda n: nc.alloc_semaphore(f"{name}_{n}")

        sc, mxp = ps("sc", [P, 3, 512]), ps("mxp", [P, 3, 512])
        avp, misc = ps("avp", [P, 512]), ps("misc", [P, 512])

        KS = sb("KS", [ROWS, NG, HG, KVP], BF16)
        QS = sb("QS", [ROWS, NG, HG, S], BF16)
        V = sb("V", [P, NG, KT, HG, 32])
        pr = sb("pr", [P, 3, HG, S])
        wq, wk, wv, wo, ctx_sb = bufs
        first_in, weights_in, ctx_in = done
        bq, bk = sb("bq", [P, 2]), sb("bk", [P, 2])
        bv = sb("bv", [P, D])
        kf, idle = sb("kf", [P, KV]), sb("idle", [P, 5])
        kparts = sb("kparts", [P, 3, KVP], BF16)
        qf = sb("qf", [P, 2, S])
        qparts = sb("qparts", [P, 3, 2, S], BF16)
        xn, xnT = sb("xn", [P, QT, D]), sb("xnT", [P, DK, S])
        mx, mxr = sb("mx", [P, 2, NCHUNK]), sb("mxr", [P, 2, HG * QT])
        cneg, chi, clo = sb("cneg", [16, P]), sb("chi", [16, P], BF16), sb("clo", [16, P], BF16)
        osb, rden = sb("osb", [P, S]), sb("rden", [P, QT, HG])
        on = sb("on", [P, QT, D])
        oT = sb("oT", [P, DK, S])
        bo = sb("bo", [P, D])
        st, mv = sb("st", [P, NT, 6]), sb("mv", [P, NT, 2])
        ve, rs, tmp = sb("ve", [P, NT]), sb("rs", [P, NT]), sb("tmp", [P, 2, NT])
        nmask = 0
        if mask is not None:
            nmask = 16
            mrow = sb("mrow", [B, KVP], U8)
            mbias = kparts[0:B, 0, :]
            mbias_dram = nc.dram_tensor(f"{name}_mbias", [B, HG, KVP], BF16, kind="Internal").ap()

        v_clear = sem("v_clear")
        mask_in, mask_out = sem("mask_in"), sem("mask_out")
        setup_v, rows_in = sem("setup_v"), sem("rows_in")
        ln_v, ln_s = sem("ln_v"), sem("ln_s")
        xn_done = sem("xn_done")
        misc_full, misc_free = sem("misc_full"), sem("misc_free")
        split_step, gated, restack_go = sem("split_step"), sem("gated"), sem("restack_go")
        k_in = [sem(f"k_in{s}") for s in range(NG)]
        q_in = [sem(f"q_in{s}") for s in range(NG)]
        c_in = [sem(f"c_in{s}") for s in range(NG)]
        max_ready, max_done, rowmax_done, c_step = sem("max_ready"), sem("max_done"), sem("rowmax_done"), sem("c_step")
        score_ready, exp_done, av_done = sem("score_ready"), sem("exp_done"), sem("av_done")
        next_stats = sem("next_stats")
        osb_done, rden_done, bias_done = sem("osb_done"), sem("rden_done"), sem("bias_done")
        FIRST_IN, WEIGHTS_IN = (32, 32) if b_o is None else (64, 64)
        K_IN, Q_IN, C_IN = 16 * TERMS + nmask, 16 * TERMS, 32
        first_jobs = FIRST_LOADED if loaded else FIRST
        prologue = first_jobs + BESIDE + [("mx", -1)]
        SPLITS = [("q", 0), ("q", 1), ("k", 0), ("k", 1)]
        FIRST_SPLITS = [("q", 0), ("k", 0), ("q", 1), ("k", 1)]

        def split_count(n, kind, half):
            order = FIRST_SPLITS if isinstance(n, int) and n == 0 else SPLITS
            return 16 * n + 4 * (order.index((kind, half)) + 1)

        block = ctx.enter_context(nc.Block())

        @block.sync
        def _(sp):
            def load_context(n):
                sp.dma_start(ctx_sb[:, :, :], ctxT[n].rearrange("(k p) n -> p k n", p=P)
                             if isinstance(n, int) else ctxT[bass.ds(n, 1)].rearrange("o (k p) n -> p (o k) n", p=P)
                             ).then_inc(ctx_in, 16)

            if b_o is not None:
                sp.dma_start(bq[:, :], b_q).then_inc(first_in, 16)
                sp.dma_start(bk[:, :], b_k).then_inc(first_in, 16)
            if mask is not None:
                sp.dma_start(mrow[:, 0:KV], mask).then_inc(mask_in, 16)

            def rows():
                sp.dma_start(KS[ROW_MASK:ROWS, :, :, :].bitcast(U32).rearrange("r g h n -> r (g h n)"), k_rows).then_inc(rows_in, 16)
                sp.dma_start(QS[ROW_MASK:ROWS, :, :, :].bitcast(U32).rearrange("r g h n -> r (g h n)"), q_rows).then_inc(rows_in, 16)

            if loaded:
                rows()
            else:
                load_inputs(sp, bufs, done, w_q, w_k, w_v, w_o, ctxT, rows)
            if b_o is not None:
                sp.dma_start(bv[:, :], b_v.partition_broadcast(P)).then_inc(weights_in, 16)
                sp.dma_start(bo[:, :], b_o.partition_broadcast(P)).then_inc(weights_in, 16)
            if mask is not None:
                sp.wait_ge(setup_v, 2)
                for h in range(HG):
                    sp.dma_start(mbias_dram[:, h, :], mbias).then_inc(mask_out, 16)
                sp.wait_ge(mask_out, 16 * HG)

            def restack_q(s, t):
                sp.dma_start(QS[HD * t:HD * t + HD, s, :, :],
                             qparts[64 * (s % 2):64 * (s % 2) + 64, Q_TERMS[t], s // 2, :]).then_inc(q_in[s], 16)

            def restack_k(s, t):
                sp.dma_start(KS[HD * t:HD * t + HD, s, :, 0:KV],
                             kparts[64 * (s % 2):64 * (s % 2) + 64, K_TERMS[t], 0:KV]).then_inc(k_in[s], 16)

            def restack(n, s):
                sp.wait_ge(restack_go, NG * n + s + 1)
                for t in range(TERMS):
                    restack_q(s, t)
                for t in range(TERMS):
                    restack_k(s, t)
                if mask is not None:
                    src = mbias_dram[n:n + 1] if isinstance(n, int) else mbias_dram[bass.ds(n, 1)]
                    sp.dma_start(KS[ROW_MASK:ROW_MASK + 1, s, :, :], src).then_inc(k_in[s], 16)

            def shifts(G, s):
                sp.wait_ge(c_step, 2 * (G + 1))
                row = QS[ROW_C:ROW_C + 1, s, :, :].rearrange("o h (t n) -> o (h t) n", n=P)
                sp.dma_start(row, chi[:, :]).then_inc(c_in[s], 16)
                row = QS[ROW_C + 1:ROW_C + 2, s, :, :].rearrange("o h (t n) -> o (h t) n", n=P)
                sp.dma_start(row, clo[:, :]).then_inc(c_in[s], 16)

            sp.wait_ge(rows_in, 32)
            if mask is not None:
                for s in range(2):
                    sp.dma_start(KS[ROW_MASK:ROW_MASK + 1, s, :, :], mbias_dram[0:1]).then_inc(k_in[s], 16)
            sp.wait_ge(split_step, split_count(0, "q", 0))
            for t in range(TERMS):
                restack_q(0, t)
            for part in range(3):
                sp.wait_ge(split_step, split_count(0, "q", 0) + (1, 3, 4)[part])
                for t in range(TERMS):
                    if K_TERMS[t] == part:
                        restack_k(0, t)
            for t in range(TERMS):
                restack_q(1, t)
                restack_k(1, t)
            shifts(0, 0)
            restack(0, 2)

            def body(b, first, last):
                restack(b, 3)
                shifts(NG * b + 1, 1)
                if not last:
                    load_context(b + 1)
                shifts(NG * b + 2, 2)
                if not last:
                    restack(b + 1, 0)
                    restack(b + 1, 1)
                shifts(NG * b + 3, 3)
                if not last:
                    shifts(NG * b + 4, 0)
                    restack(b + 1, 2)

            body(0, True, False)
            with sp.Fori(1, B - 1) as b:
                body(b, False, False)
            body(B - 1, False, True)

        @block.gpsimd
        def _(pool):
            nc.gpsimd.memset(idle[:, :], 0.0).then_inc(gated, 1)
            nc.gpsimd.memset(V[:, :, :, :, :], 0.0).then_inc(v_clear, 1)
            pool.wait_ge(v_clear, 1)
            nc.gpsimd.memset(V[:, :, :, :, HD:HD + 1], 1.0).then_inc(v_clear, 1)

            def gate(i):
                return nc.gpsimd.tensor_tensor(idle[:, i:i + 1], idle[:, 0:1], idle[:, 0:1], ALU.mult)

            def split(n, kind, half, rest, parts):
                done = split_count(n, kind, half) - 4
                gate(1)
                nc.gpsimd.tensor_copy(parts[0], rest).then_inc(split_step, 1)
                pool.wait_ge(split_step, done + 1)
                nc.gpsimd.tensor_tensor(rest, rest, parts[0], ALU.subtract).then_inc(split_step, 1)
                pool.wait_ge(split_step, done + 2)
                gate(2)
                nc.gpsimd.tensor_copy(parts[1], rest).then_inc(split_step, 1)
                pool.wait_ge(split_step, done + 3)
                nc.gpsimd.tensor_tensor(parts[2], rest, parts[1], ALU.subtract).then_inc(split_step, 1)

            def split_q(n, half, job, fresh):
                pool.wait_ge(misc_free, job + 1)
                if not fresh:
                    for s in (2 * half, 2 * half + 1):
                        pool.wait_ge(q_in[s], Q_IN * n)
                split(n, "q", half, qf[:, half, :], [qparts[:, i, half, :] for i in range(3)])

            def split_k(n, half, job, fresh):
                pool.wait_ge(misc_free, job + 1)
                if half == 1:
                    for s in (0, 1):
                        pool.wait_ge(k_in[s], K_IN * (n + 1))
                elif not fresh:
                    for s in (2, 3):
                        pool.wait_ge(k_in[s], K_IN * n)
                split(n, "k", half, kf[:, :], [kparts[:, i, 0:KV] for i in range(3)])

            def go(n, s, fresh):
                if not fresh:
                    pool.wait_ge(score_ready, NS * (NG * n - NG + s + 1))
                pool.wait_ge(split_step, split_count(n, "k", s // 2))
                gate(4).then_inc(restack_go, 1)
                pool.wait_ge(restack_go, NG * n + s + 1)

            def add_bias(n):
                pool.wait_ge(xn_done, QT * (n + 1))
                gate(3)
                xs = x[:, QT * n:QT * n + QT, :] if isinstance(n, int) else x[:, bass.ds(QT * n, QT), :]
                nc.gpsimd.tensor_tensor(xs, xs, bo[:, :].rearrange("p (o d) -> p o d", o=1).broadcast_to([P, QT, D]),
                                        ALU.add).then_inc(bias_done, 1)

            pool.wait_ge(gated, 1)
            at = {j: i for i, j in enumerate(prologue)}
            if b_o is not None:
                pool.wait_ge(weights_in, WEIGHTS_IN)
                add_bias(0)
            pool.wait_ge(split_step, split_count(0, "k", 0))
            gate(4).then_inc(restack_go, 2)
            split_q(0, 1, at["q", 1], True)
            split_k(0, 1, at["k", (1, 3)], True)
            go(0, 2, True)
            go(0, 3, True)

            def body(b, first, last):
                before = jobs_before(b, first)
                for i, (g, kt, job, arg) in enumerate(jobs_of(first, last)):
                    if job == "q" and arg == 0 and b_o is not None:
                        add_bias(b + 1)
                    if job == "q":
                        split_q(b + 1, arg, before + i, False)
                    if job == "k" and arg[1] == 3:
                        split_k(b + 1, arg[0], before + i, False)
                        for s in (2 * arg[0], 2 * arg[0] + 1):
                            go(b + 1, s, False)

            body(0, True, False)
            with pool.Fori(1, B - 1) as b:
                body(b, False, False)
            body(B - 1, False, True)

        @block.scalar
        def _(act):
            def root(lo, hi, n):
                act.wait_ge(ln_v, n)
                nc.scalar.activation(tmp[:, 0, lo:hi], ve[:, lo:hi], ACT.Sqrt).then_inc(ln_s, 1)

            def take(n, job, kind, arg, fresh):
                act.wait_ge(misc_full, job + 1)
                if kind == "xt":
                    nc.scalar.copy(xnT[:, arg, :], misc[:, :]).then_inc(misc_free, 1)
                if kind == "ot":
                    nc.scalar.copy(oT[:, arg, :], misc[:, :]).then_inc(misc_free, 1)
                if kind == "q":
                    if not fresh:
                        act.wait_ge(split_step, split_count(n - 1, "q", arg))
                    nc.scalar.activation(qf[:, arg, :], misc[:, :], ACT.Identity, bias=bq[:, arg:arg + 1],
                                         scale=HD ** -0.5).then_inc(misc_free, 1)
                if kind == "k":
                    half, c = arg
                    if half == 1:
                        act.wait_ge(split_step, split_count(n, "k", 0))
                    elif not fresh:
                        act.wait_ge(split_step, split_count(n - 1, "k", 1))
                    o, w = KCH[c]
                    nc.scalar.activation(kf[:, o:o + w], misc[:, 0:w], ACT.Identity,
                                         bias=bk[:, half:half + 1]).then_inc(misc_free, 1)

            def take_out(G):
                act.wait_ge(av_done, KT * (G + 1))
                nc.scalar.copy(osb[:, :], avp[:, :]).then_inc(osb_done, 1)

            root(0, QT, 2)
            act.wait_ge(setup_v, 1)
            for i, (job, arg) in enumerate(prologue):
                if job == "q" and arg == 0:
                    root(QT, NT, 9)
                if job in ON_ACT:
                    take(0, i, job, arg, True)

            def body(b, first, last):
                before = jobs_before(b, first)
                jobs = {(g, kt): (i, job, arg) for i, (g, kt, job, arg) in enumerate(jobs_of(first, last))}
                for g in range(NG):
                    G = NG * b + g
                    for kt in range(KT):
                        rows = P if kt < KT - 1 else LAST
                        slot = kt % 2 if kt < KT - 1 else 2
                        if kt == 1 and not (first and g == 0):
                            take_out(G - 1)
                        if kt in (0, 1, KT - 1):
                            if not (first and g == 0):
                                act.wait_ge(av_done, KT * G - (2 - kt if kt < 2 else 0))
                        else:
                            act.wait_ge(av_done, KT * G + kt - 1)
                        for h in range(HG):
                            j = HG * kt + h
                            act.wait_ge(score_ready, NS * G + j + 1)
                            nc.scalar.activation(pr[0:rows, slot, h, :], sc[0:rows, (j + g) % 3, :],
                                                 ACT.Exp).then_inc(exp_done, 1)
                            i, job, arg = jobs.get((g, kt), (0, "", 0))
                            if h == 1 and job in ON_ACT:
                                take(b + 1, before + i, job, arg, False)

            body(0, True, False)
            with act.Fori(1, B - 1) as b:
                body(b, False, False)
            body(B - 1, False, True)
            take_out(NG * B - 1)
            tail = jobs_before(B - 1, False) + len(jobs_of(False, True))
            for i, (job, arg) in enumerate(TAIL):
                if job in ON_ACT:
                    take(B, tail + i, job, arg, False)

        @block.vector
        def _(dve):
            if b_q is None:
                nc.vector.memset(bq[:, :], 0.0)
                nc.vector.memset(bv[:, :], 0.0)
                nc.vector.memset(bk[:, :], 0.0).then_inc(setup_v, 1)
            else:
                dve.wait_ge(first_in, FIRST_IN)
                nc.vector.tensor_scalar(bq[:, :], bq[:, :], HD ** -0.5, None, ALU.mult).then_inc(setup_v, 1)
            if mask is not None:
                dve.wait_ge(mask_in, 16)
                nc.vector.memset(mbias[:, KV:KVP], 0.0)
                nc.vector.tensor_scalar(mbias[:, 0:KV], mrow[:, 0:KV], -MASKED, MASKED, ALU.mult, ALU.add).then_inc(setup_v, 1)

            def statistics(lo, hi):
                v, a = (0, 0) if lo == 0 else (7, 2)
                for t in range(lo, hi):
                    if x_in is not None and t % QT == 0:
                        dve.wait_ge(x_in[t // QT], 16)
                    last = nc.vector.bn_stats(st[:, t, :], x[:, t, :])
                last.then_inc(ln_v, 1)
                dve.wait_ge(ln_v, v + 1)
                for t in range(lo, hi):
                    last = nc.vector.bn_aggr(mv[:, t, :], st[:, t, :])
                last.then_inc(ln_s, 1)
                dve.wait_ge(ln_s, a + 1)
                nc.vector.tensor_scalar(ve[:, lo:hi], mv[:, lo:hi, 1], EPS, None, ALU.add).then_inc(ln_v, 1)
                dve.wait_ge(ln_s, a + 2)
                rsqrt_steps(nc, dve, ln_v, v + 2, ve[:, lo:hi], tmp[:, :, lo:hi], rs[:, lo:hi])

            def normalize_tokens(n, t):
                i = QT * n + t
                ds = (lambda a: a[:, i, :]) if isinstance(n, int) else (lambda a: a[:, bass.ds(i, 1), :])
                col = (lambda a: a[:, i:i + 1]) if isinstance(n, int) else (lambda a: a[:, bass.ds(i, 1)])
                mean = mv[:, i, 0:1] if isinstance(n, int) else mv[:, bass.ds(i, 1), 0]
                dst = xn[:, t, :] if isinstance(n, int) else xn[:, t:t + 1, :]
                nc.vector.tensor_scalar(dst, ds(x), mean, col(rs), ALU.subtract, ALU.mult).then_inc(xn_done, 1)

            def take(b, job, kind, arg, first):
                for _ in take_steps(b, job, kind, arg, first):
                    pass

            def take_steps(b, job, kind, arg, first):
                if kind == "mx":
                    G = NG * b + arg + 1
                    dve.wait_ge(misc_full, job + 1)
                    if not (isinstance(G, int) and G == 0):
                        dve.wait_ge(c_in[(arg) % NG], C_IN * ((b + 1) if arg >= 0 else b))
                    nc.vector.tensor_scalar(cneg[:, :], misc[0:16, 0:P], CLAMP, -1.0, ALU.max, ALU.mult).then_inc(misc_free, 1)
                    yield
                    dve.wait_ge(misc_free, job + 1)
                    nc.vector.tensor_copy(chi[:, :], cneg[:, :]).then_inc(c_step, 1)
                    yield
                    dve.wait_ge(c_step, 2 * G + 1)
                    nc.vector.tensor_tensor(clo[:, :], cneg[:, :], chi[:, :], ALU.subtract).then_inc(c_step, 1)
                    return
                dve.wait_ge(misc_full, job + 1)
                if kind == "norm":
                    g, G = (arg - 1) % NG, NG * b + arg - 1
                    src = misc[:, :].rearrange("p (t j d) -> p t j d", j=HG, d=32)
                    nc.vector.reciprocal(rden[:, :, :], src[:, :, :, HD]).then_inc(rden_done, 1)
                    yield
                    dve.wait_ge(rden_done, G + 1)
                    ont = on[:, :, 64 * g:64 * g + 64].rearrange("p t (j d) -> p t j d", j=HG)
                    ins = None
                    for t in range(QT):
                        r = rden[:, t, :].rearrange("p (j o) -> p j o", o=1).broadcast_to([P, HG, HD])
                        ins = nc.vector.tensor_tensor(ont[:, t], src[:, t, :, 0:HD], r, ALU.mult)
                    ins.then_inc(misc_free, 1)
                if kind == "out":
                    i = QT * (b - 1) + 2 * arg
                    xs = x[:, i:i + 2, :] if isinstance(b, int) else x[:, bass.ds(i, 2), :]
                    if b_o is not None:
                        dve.wait_ge(bias_done, b)
                    nc.vector.tensor_tensor(xs, misc[:, :].rearrange("p (t n) -> p t n", t=2), xs,
                                            ALU.add).then_inc(misc_free, 1)
                if kind == "v":
                    half, part = arg
                    if not (first and (b == 0 if isinstance(b, int) else False)):
                        dve.wait_ge(av_done, KT * (NG * (b - 1) + 2 * half + 2))
                    k0, k1 = VPART[part]
                    src = misc[:, :].rearrange("p (k s j d) -> p k s j d", s=2, j=HG, d=HD)
                    full = min(k1, KT - 1) - k0
                    for i in range(2):
                        s = 2 * half + i
                        bias = bv[:, 64 * s:64 * s + 64].rearrange("p (o j d) -> p o j d", o=1, d=HD)
                        ins = nc.vector.tensor_tensor(V[:, s, k0:k0 + full, :, 0:HD], src[:, 0:full, i],
                                                      bias.broadcast_to([P, full, HG, HD]), ALU.add)
                        if k1 == KT:
                            ins = nc.vector.tensor_tensor(V[0:LAST, s, KT - 1, :, 0:HD], src[0:LAST, full, i],
                                                          bias[0:LAST, 0], ALU.add)
                    ins.then_inc(misc_free, 1)

            def row_maxima(G, par):
                dve.wait_ge(max_done, NCHUNK * (G + 1))
                nc.vector.tensor_reduce(mxr[:, par, :], mx[:, par, :].rearrange("p (i c) -> p i c", c=4),
                                        AX.X, ALU.max).then_inc(rowmax_done, 1)

            def reduce_chunk(G, s, i):
                dve.wait_ge(max_ready, NCHUNK * G + i + 1)
                nc.vector.tensor_reduce(mx[:, s % 2, i:i + 1], mxp[:, (i + s) % 3, 0:CHUNK], AX.X, ALU.max).then_inc(max_done, 1)
                if i == NCHUNK - 1:
                    row_maxima(G, s % 2)

            def split_steps(n, kind, rest, parts):
                done = split_count(n, kind, 0) - 4
                nc.vector.tensor_copy(parts[0], rest).then_inc(split_step, 1)
                yield
                dve.wait_ge(split_step, done + 1)
                nc.vector.tensor_tensor(rest, rest, parts[0], ALU.subtract).then_inc(split_step, 1)
                yield
                dve.wait_ge(split_step, done + 2)
                nc.vector.tensor_copy(parts[1], rest).then_inc(split_step, 1)
                yield
                dve.wait_ge(split_step, done + 3)
                nc.vector.tensor_tensor(parts[2], rest, parts[1], ALU.subtract).then_inc(split_step, 1)
                yield

            statistics(0, QT)
            for t in range(QT):
                normalize_tokens(0, t)
            statistics(QT, NT)
            at = {j: i for i, j in enumerate(prologue)}
            dve.wait_ge(misc_free, at["q", 0] + 1)
            for _ in split_steps(0, "q", qf[:, 0, :], [qparts[:, i, 0, :] for i in range(3)]):
                pass
            if mask is not None:
                dve.wait_ge(mask_out, 16 * HG)
            dve.wait_ge(misc_free, at["k", (0, 3)] + 1)
            dve.wait_ge(v_clear, 2)
            for i, _ in enumerate(split_steps(0, "k", kf[:, :], [kparts[:, i, 0:KV] for i in range(3)])):
                if i % 2 == 1:
                    take(0, at["v", (0, i // 2)], "v", (0, i // 2), True)
            for i in (2, 3):
                take(0, at["v", (0, i)], "v", (0, i), True)
            for i in range(NCHUNK):
                reduce_chunk(0, 0, i)
                n = i // PER_JOB
                if i % PER_JOB == PER_JOB - 1 and BESIDE[n][0] == "v":
                    take(0, len(first_jobs) + n, *BESIDE[n], True)
            take(0, PROLOGUE_JOBS - 1, "mx", -1, True)
            for i in range(LEAD):
                reduce_chunk(1, 1, i)

            def body(b, first, last):
                before = jobs_before(b, first)
                jobs = {(g, kt): (i, job, arg) for i, (g, kt, job, arg) in enumerate(jobs_of(first, last))}
                for g in range(NG):
                    for kt in range(KT):
                        chunks = chunks_at(g, kt, last)
                        for tg, c in chunks[:2]:
                            reduce_chunk(NG * b + tg, tg % NG, c)
                        i, job, arg = jobs.get((g, kt), (0, "", 0))
                        steps = iter(())
                        if job and job not in ON_ACT:
                            n = b if job != "v" or arg[0] == 1 else b + 1
                            steps = take_steps(n, before + i, job, arg, first and n is b)
                        for tg, c in chunks[2:]:
                            next(steps, None)
                            reduce_chunk(NG * b + tg, tg % NG, c)
                        for _ in steps:
                            pass
                        if g == 0 and 3 <= kt < 3 + QT and not last:
                            normalize_tokens(b + 1, kt - 3)

            body(0, True, False)
            with dve.Fori(1, B - 1) as b:
                body(b, False, False)
            body(B - 1, False, True)
            tail = jobs_before(B - 1, False) + len(jobs_of(False, True))
            last_out = [i for i, j in enumerate(jobs_of(False, True)) if j[2] == "out"][-1]
            dve.wait_ge(misc_free, jobs_before(B - 1, False) + last_out + 1)
            for t in range(NT - QT):
                last = nc.vector.bn_stats(stats[0][:, t, :], x[:, t, :])
            last.then_inc(next_stats, 1)
            for i, (job, arg) in enumerate(TAIL):
                if job not in ON_ACT:
                    take(B - (job == "norm"), tail + i, job, arg, False)
                if i == 0:
                    dve.wait_ge(next_stats, 1)
                    for t in range(NT - QT):
                        nc.vector.bn_aggr(stats[1][:, t, :], stats[0][:, t, :])

        @block.tensor
        def _(pe):
            pe.wait_ge(first_in, FIRST_IN)
            if x_in is not None:
                pe.wait_ge(x_in[B], 16)

            def start(n, job, kind, arg, parts=(0, 1)):
                if 0 in parts and not (isinstance(job, int) and job == 0):
                    pe.wait_ge(misc_free, job)
                mm = None
                if kind == "xt" and 0 in parts:
                    pe.wait_ge(xn_done, QT * (n + 1))
                if kind == "k" and 0 in parts:
                    pe.wait_ge(ctx_in, 16 * (n + 1))
                if kind == "norm" and 0 in parts:
                    pe.wait_ge(osb_done, NG * n + arg)
                if kind == "mx" and 0 in parts:
                    pe.wait_ge(rowmax_done, NG * n + arg + 2)
                for part in parts:
                    if kind in ("xt", "ot", "norm"):
                        for t in (2 * part, 2 * part + 1):
                            src = {"xt": xn[:, t, P * arg:P * arg + P] if arg < DK else None,
                                   "ot": on[:, t, P * arg:P * arg + P] if arg < DK else None,
                                   "norm": osb[:, P * t:P * t + P]}[kind]
                            mm = nc.tensor.transpose(misc[:, P * t:P * t + P], src, ident[:, :])
                    if kind == "mx" and part == 0:
                        mm = nc.tensor.transpose(misc[0:16, 0:P], mxr[:, (arg + 1) % 2, :], ident[:, :])
                    if kind == "q":
                        mm = nc.tensor.matmul(misc[:, :], wq[:, part, P * arg:P * arg + P], xnT[:, part, :],
                                              start=part == 0, stop=part == DK - 1)
                    if kind == "k":
                        half, c = arg
                        o, w = KCH[c]
                        mm = nc.tensor.matmul(misc[:, 0:w], wk[:, part, P * half:P * half + P],
                                              ctx_sb[:, part, o:o + w], start=part == 0, stop=part == DK - 1)
                    if kind == "v":
                        half, i = arg
                        k0, k1 = VPART[i]
                        mid = (k0 + k1) // 2
                        for kt in (range(k0, mid) if part == 0 else range(mid, k1)):
                            rows = P if kt < KT - 1 else LAST
                            for k in range(DK):
                                mm = nc.tensor.matmul(misc[0:rows, P * (kt - k0):P * (kt - k0) + P],
                                                      ctx_sb[:, k, P * kt:P * kt + rows], wv[:, k, P * half:P * half + P],
                                                      start=k == 0, stop=k == DK - 1)
                    if kind == "out":
                        for k in range(DK):
                            a = P * (2 * arg + part)
                            mm = nc.tensor.matmul(misc[:, D * part:D * part + D], oT[:, k, a:a + P], wo[:, k, :],
                                                  start=k == 0, stop=k == DK - 1)
                if (1 if kind != "mx" else 0) in parts:
                    mm.then_inc(misc_full, 1)

            def max_chunk(G, s, i, n):
                h, t, c = i // (QT * 4), i // 4 % QT, i % 4
                if i == 0:
                    pe.wait_ge(q_in[s], Q_IN * (n + 1))
                    pe.wait_ge(k_in[s], K_IN * (n + 1))
                if i >= 3:
                    pe.wait_ge(max_done, NCHUNK * G + i - 2)
                elif not (isinstance(G, int) and G == 0):
                    pe.wait_ge(max_done, NCHUNK * G - ((0, 2, 1) if s == 0 else (2, 1, 0))[i])
                nc.tensor.matmul(mxp[:, (i + s) % 3, 0:CHUNK], QS[0:ROW_MASK + 1, s, h, P * t:P * t + P],
                                 KS[0:ROW_MASK + 1, s, h, CHUNK_AT[c]:CHUNK_AT[c] + CHUNK],
                                 start=True, stop=True).then_inc(max_ready, 1)

            def score(G, s, kt, h, first):
                j = HG * kt + h
                rows = P if kt < KT - 1 else LAST
                if j >= 3:
                    pe.wait_ge(exp_done, NS * G + j - 2)
                elif not first:
                    pe.wait_ge(exp_done, NS * G - ((0, 2, 1) if s == 0 else (2, 1, 0))[j])
                nc.tensor.matmul(sc[0:rows, (j + s) % 3, :], KS[:, s, h, P * kt:P * kt + rows], QS[:, s, h, :],
                                 start=True, stop=True).then_inc(score_ready, 1)

            def pv(G, s, kt, first):
                rows = P if kt < KT - 1 else LAST
                slot = kt % 2 if kt < KT - 1 else 2
                pe.wait_ge(exp_done, NS * G + HG * kt + HG)
                if kt == 0 and not first:
                    pe.wait_ge(osb_done, G)
                for j in range(HG):
                    mm = nc.tensor.matmul(avp[32 * j:32 * j + 32, :], V[0:rows, s, kt, j, :], pr[0:rows, slot, j, :],
                                          start=kt == 0, stop=kt == KT - 1)
                mm.then_inc(av_done, 1)

            for i, (job, arg) in enumerate(first_jobs):
                if job == "v" and arg == (0, 0):
                    pe.wait_ge(weights_in, WEIGHTS_IN)
                start(0, i, job, arg)
            pe.wait_ge(rows_in, 32)
            for i in range(NCHUNK):
                max_chunk(0, 0, i, 0)
                if i % PER_JOB == PER_JOB - 1:
                    start(0, len(first_jobs) + i // PER_JOB, *BESIDE[i // PER_JOB])
            start(0, PROLOGUE_JOBS - 1, "mx", -1)
            for i in range(LEAD):
                max_chunk(1, 1, i, 0)
            pe.wait_ge(v_clear, 2)

            def body(b, first, last):
                before = jobs_before(b, first)
                jobs = {(g, kt): (i, job, arg) for i, (g, kt, job, arg) in enumerate(jobs_of(first, last))}
                for g in range(NG):
                    G = NG * b + g
                    none_before = first and g == 0
                    for kt in range(KT):
                        if kt == 0:
                            pe.wait_ge(c_in[g], C_IN * (b + 1))
                        chunks = chunks_at(g, kt, last)
                        i, job, arg = jobs.get((g, kt), (0, "", 0))
                        n = b + 1 if job in AHEAD or (job == "v" and arg[0] == 0) else b
                        for h in range(HG):
                            score(G, g, kt, h, none_before)
                            for tg, c in (chunks[h:h + 1] if h < HG - 1 else chunks[h:]):
                                max_chunk(NG * b + tg, tg % NG, c, b + tg // NG)
                            if h < 2 and job:
                                start(n, before + i, job, arg, (h,))
                            if h == 2 and kt > 0:
                                pv(G, g, kt - 1, none_before)
                            elif h == 2 and not none_before:
                                pv(G - 1, (g - 1) % NG, KT - 1, False)

            body(0, True, False)
            with pe.Fori(1, B - 1) as b:
                body(b, False, False)
            body(B - 1, False, True)
            pv(NG * B - 1, NG - 1, KT - 1, False)
            tail = jobs_before(B - 1, False) + len(jobs_of(False, True))
            for i, (job, arg) in enumerate(TAIL):
                start(B - 1, tail + i, job, arg)


def rsqrt_steps(nc, dve, done, n, ve, tmp, rs):
    y, h = tmp[:, 0, :], tmp[:, 1, :]
    nc.vector.reciprocal(rs[:, :], y).then_inc(done, 1)
    dve.wait_ge(done, n + 1)
    nc.vector.tensor_tensor(h, rs[:, :], rs[:, :], ALU.mult).then_inc(done, 1)
    dve.wait_ge(done, n + 2)
    nc.vector.tensor_tensor(h, h, ve[:, :], ALU.mult).then_inc(done, 1)
    dve.wait_ge(done, n + 3)
    nc.vector.tensor_scalar(h, h, -0.5, 1.5, ALU.mult, ALU.add).then_inc(done, 1)
    dve.wait_ge(done, n + 4)
    nc.vector.tensor_tensor(rs[:, :], rs[:, :], h, ALU.mult).then_inc(done, 1)
    dve.wait_ge(done, n + 5)


def normalized_transposed(nc, name, ctx, x, ident, stats, kept, split=False, reuse=None):
    sb = lambda n, s, d=F32: ctx.enter_context(nc.sbuf_tensor(f"{name}_{n}", s, d))
    sem = lambda n: nc.alloc_semaphore(f"{name}_{n}")
    tp = ctx.enter_context(nc.psum_tensor(f"{name}_tp", [P, 2, 2, DK, P], F32))
    xn = sb("xn", [P, kept, D])
    xnT = sb("xnT", [P, 2, DK, B * S], F32R) if split else sb("xnT", [P, DK, B * S])
    first = xnT[:, 0] if split else xnT[:, :, :]
    st, mv = stats
    ve, rs, tmp = sb("ve", [P, NT]), sb("rs", [P, NT]), sb("tmp", [P, 2, NT])
    ln_v, ln_s, xn_done = sem("ln_v"), sem("ln_s"), sem("xn_done")
    tp_ready, xnT_done = sem("tp_ready"), sem("xnT_done")
    rest_done = sem("rest_done") if split else xnT_done
    PAIRS = NT // 2

    def pair(a, p):
        return a[:, :, 2 * P * p:2 * P * p + 2 * P].rearrange("p k (i n) -> p i k n", i=2)

    def vector(dve):
        def rest(p):
            dve.wait_ge(xnT_done, p + 1)
            nc.vector.tensor_tensor(pair(xnT[:, 1], p), tp[:, p % 2], pair(first, p).bitcast(F32),
                                    ALU.subtract).then_inc(rest_done, 1)

        for t in range(NT - QT, NT):
            last = nc.vector.bn_stats(st[:, t, :], x[:, t, :])
        last.then_inc(ln_v, 1)
        dve.wait_ge(ln_v, 1)
        for t in range(NT - QT, NT):
            last = nc.vector.bn_aggr(mv[:, t, :], st[:, t, :])
        last.then_inc(ln_s, 1)
        dve.wait_ge(ln_s, 1)
        nc.vector.tensor_scalar(ve[:, :], mv[:, :, 1], EPS, None, ALU.add).then_inc(ln_v, 1)
        dve.wait_ge(ln_s, 2)
        rsqrt_steps(nc, dve, ln_v, 2, ve, tmp, rs)
        for t in range(NT):
            if t >= kept:
                dve.wait_ge(tp_ready, (t - kept) // 2 + 1)
                if reuse is not None:
                    reuse(dve, t)
            nc.vector.tensor_scalar(xn[:, t % kept, :], x[:, t, :], mv[:, t, 0:1], rs[:, t:t + 1],
                                    ALU.subtract, ALU.mult).then_inc(xn_done, 1)
            if split and t % 2 == 1 and t >= 3:
                rest(t // 2 - 1)
        if split:
            rest(PAIRS - 1)

    def tensor(pe):
        for p in range(PAIRS):
            pe.wait_ge(xn_done, 2 * p + 2)
            if p >= 2:
                pe.wait_ge(rest_done, p - 1)
            for i in range(2):
                for k in range(DK):
                    mm = nc.tensor.transpose(tp[:, p % 2, i, k, :], xn[:, (2 * p + i) % kept, P * k:P * k + P], ident[:, :])
            mm.then_inc(tp_ready, 1)

    def scalar(act, between=lambda p: None):
        act.wait_ge(ln_v, 2)
        nc.scalar.activation(tmp[:, 0, :], ve[:, :], ACT.Sqrt).then_inc(ln_s, 1)
        for p in range(PAIRS):
            between(p)
            act.wait_ge(tp_ready, p + 1)
            nc.scalar.copy(pair(first, p), tp[:, p % 2]).then_inc(xnT_done, 1)

    return xn, xn_done, xnT, rest_done, PAIRS, vector, tensor, scalar


def swiglu(nc, x, ident, stats, w_gate, w_up, w_down, load_next):
    MT = FF0 // P
    NC = B
    with ExitStack() as ctx:
        sb = lambda n, s, d=F32: ctx.enter_context(nc.sbuf_tensor(f"ffn_{n}", s, d))
        sem = lambda n: nc.alloc_semaphore(f"ffn_{n}")
        _, _, xnT, xnT_done, PAIRS, ln_vector, ln_tensor, ln_scalar = normalized_transposed(nc, "ffn", ctx, x, ident, stats, 4, split=True)
        gp = ctx.enter_context(nc.psum_tensor("ffn_gate", [P, 2, S], F32))
        up = ctx.enter_context(nc.psum_tensor("ffn_up", [P, 2, S], F32))
        yp = ctx.enter_context(nc.psum_tensor("ffn_y", [P, QT, D], F32))
        wi = sb("wi", [P, 3, DK * FF0], I32)
        wf = sb("wf", [P, 3, DK * FF0])
        wp = sb("wp", [P, 2, 3, DK * FF0], F32R)
        wg, wu = (wp[:, :, i, :].rearrange("p a (k n) -> p a k n", k=DK) for i in range(2))
        wd = wp[:, :, 2, :].rearrange("p a (m n) -> p a m n", m=MT)
        sg, h = sb("sg", [P, 2, S]), sb("h", [P, 2, S])
        hT = sb("hT", [P, 2, MT, S], F32R)
        PRODUCTS = ((0, 0), (0, 1), (1, 0))
        w_in = [sem(f"w_in{i}") for i in range(3)]
        w_cast, w_first, w_rest = sem("w_cast"), sem("w_first"), sem("w_rest")
        h_first = sem("h_first")
        gate_ready, up_ready, silu_done = sem("gate_ready"), sem("up_ready"), sem("silu_done")
        h_done, h_rest = sem("h_done"), sem("h_rest")
        down_done, y_taken = sem("down_done"), sem("y_taken")
        block = ctx.enter_context(nc.Block())

        @block.sync
        def _(sp):
            for i, w in enumerate((w_gate, w_up)):
                sp.dma_start(wi[:, i, :].rearrange("p (k n) -> p k n", k=DK),
                             w.rearrange("(k p) n -> p k n", p=P)).then_inc(w_in[i], 16)
            sp.dma_start(wi[:, 2, :].rearrange("p (m n) -> p m n", m=MT),
                         w_down.rearrange("(m p) n -> p m n", p=P)).then_inc(w_in[2], 16)
            load_next(sp)

        @block.gpsimd
        def _(pool):
            for i in range(3):
                pool.wait_ge(w_first, i + 1)
                nc.gpsimd.tensor_tensor(wp[:, 1, i, :], wf[:, i, :], wp[:, 0, i, :].bitcast(F32),
                                        ALU.subtract).then_inc(w_rest, 1)

        def chunks(engine, body):
            body(0)
            with engine.Fori(1, NC) as c:
                body(c)

        @block.scalar
        def _(act):
            def cast(step):
                i = step // 2
                if step % 2 == 0:
                    act.wait_ge(w_in[i], 16)
                    nc.scalar.copy(wf[:, i, :], wi[:, i, :]).then_inc(w_cast, 1)
                else:
                    act.wait_ge(w_cast, i + 1)
                    nc.scalar.copy(wp[:, 0, i, :], wf[:, i, :]).then_inc(w_first, 1)

            CAST_AT = {2: 0, 3: 1, 5: 2, 6: 3}
            ln_scalar(act, lambda p: cast(CAST_AT[p]) if p in CAST_AT else None)
            for step in (4, 5):
                cast(step)

            def first_part(q, m):
                act.wait_ge(h_done, q + 1)
                if not (isinstance(q, int) and q < MT):
                    act.wait_ge(down_done, q - MT + 1)
                nc.scalar.copy(hT[:, 0, m, :], h[:, m % 2, :]).then_inc(h_first, 1)

            def body(c):
                for m in range(MT):
                    q = MT * c + m
                    if not (isinstance(q, int) and q == 0):
                        first_part(q - 1, (m - 1) % MT)
                    act.wait_ge(gate_ready, q + 1)
                    if not (isinstance(q, int) and q < 2):
                        act.wait_ge(h_done, q - 1)
                    nc.scalar.activation(sg[:, m % 2, :], gp[:, m % 2, :], ACT.Silu, scale=INV127).then_inc(silu_done, 1)

            chunks(act, body)
            first_part(MT * NC - 1, MT - 1)

        @block.vector
        def _(dve):
            ln_vector(dve)

            def take_y(c):
                dve.wait_ge(down_done, MT * (c + 1))
                for i in range(2):
                    t = QT * c + 2 * i
                    xs = x[:, t:t + 2, :] if isinstance(c, int) else x[:, bass.ds(t, 2), :]
                    ins = nc.vector.scalar_tensor_tensor(out=xs, in0=yp[:, 2 * i:2 * i + 2, :], scalar=INV127, in1=xs,
                                                         op0=ALU.mult, op1=ALU.add)
                ins.then_inc(y_taken, 1)

            def rest(q, m):
                dve.wait_ge(h_first, q + 1)
                nc.vector.tensor_tensor(hT[:, 1, m, :], h[:, m % 2, :], hT[:, 0, m, :].bitcast(F32),
                                        ALU.subtract).then_inc(h_rest, 1)

            def body(c):
                for m in range(MT):
                    if m == 1 and not (isinstance(c, int) and c == 0):
                        take_y(c - 1)
                    q = MT * c + m
                    dve.wait_ge(silu_done, q + 1)
                    dve.wait_ge(up_ready, q + 1)
                    nc.vector.scalar_tensor_tensor(out=h[:, m % 2, :], in0=up[:, m % 2, :], scalar=INV127,
                                                   in1=sg[:, m % 2, :], op0=ALU.mult, op1=ALU.mult).then_inc(h_done, 1)
                    rest(q, m)

            chunks(dve, body)
            take_y(NC - 1)

        @block.tensor
        def _(pe):
            ln_tensor(pe)
            pe.wait_ge(xnT_done, PAIRS)
            pe.wait_ge(w_rest, 2)

            def down(q, m, c):
                if isinstance(q, int) and q == 0:
                    pe.wait_ge(w_rest, 3)
                pe.wait_ge(h_rest, q + 1)
                if m == 0 and not (isinstance(c, int) and c == 0):
                    pe.wait_ge(y_taken, c)
                for t in range(QT):
                    for n, (a, b) in enumerate(PRODUCTS):
                        mm = nc.tensor.matmul(yp[:, t, :], hT[:, a, m, P * t:P * t + P], wd[:, b, m, :],
                                              start=m == 0 and t % 2 == 0 and n == 0,
                                              stop=m == MT - 1 and n == len(PRODUCTS) - 1, skip_group_check=True)
                mm.then_inc(down_done, 1)

            def body(c):
                tokens = slice(S * c, S * c + S) if isinstance(c, int) else bass.ds(S * c, S)
                for m in range(MT):
                    q = MT * c + m
                    for w, bank, ready, free in ((wg, gp, gate_ready, silu_done), (wu, up, up_ready, h_done)):
                        if not (isinstance(q, int) and q < 2):
                            pe.wait_ge(free, q - 1)
                        pairs = [(k, a, b) for k in range(DK) for a, b in PRODUCTS]
                        for k, a, b in pairs:
                            mm = nc.tensor.matmul(bank[:, m % 2, :], w[:, a, k, P * m:P * m + P], xnT[:, b, k, tokens],
                                                  start=(k, a, b) == pairs[0], stop=(k, a, b) == pairs[-1])
                        mm.then_inc(ready, 1)
                    if not (isinstance(q, int) and q == 0):
                        down(q - 1, (m - 1) % MT, c if m > 0 else c - 1)

            chunks(pe, body)
            down(MT * NC - 1, MT - 1, NC - 1)


def route(nc, ctx, sb, sem, const, xnT, gw, gb, w_in, w_in_n, plan):
    gather_row, scatter_row, weight, tile_expert = plan
    iota, before, token, slot_no = const
    PER_GROUP = 4
    lg, m8, i8 = sb("lg", [P, NT, E]), sb("m8", [P, NT, 8]), sb("i8", [P, NT, 8], U32)
    top, wt = sb("top", [P, 2, NT]), sb("wt", [P, 2, NT])
    ex, den = sb("ex", [P, NT]), sb("den", [P, NT])
    hot = sb("hot", [P, 2 * NT, E])
    chosen = sb("chosen", [P, NT * E])
    ones = sb("ones", [P, P])
    run = sb("run", [P, 2, NT, E])
    tiles_i, tiles = sb("tiles_i", [P, 2, E], I32), sb("tiles", [P, E])
    ends = sb("ends", [P, 2, E])
    slot, hi, lo = sb("slot", [P, 2 * NT]), sb("hi", [P, 2 * NT]), sb("lo", [P, 2 * NT])
    slot_i = sb("slot_i", [P, 2, 2 * NT], I32)
    at = sb("at", [P, NT, E])
    picked = sb("picked", [P, 2 * NT, E])
    at_tile = xnT[:, :, :].rearrange("p k n -> p (k n)")[:, 0:2 * NT * TABLE].rearrange("p (n w) -> p n w", n=2 * NT)
    entry = sb("entry", [P, 2 * NT, 3, TABLE], F32R)
    w_parts = sb("w_parts", [P, 2, 2 * NT])
    place = sb("place", [P, 2, PER_GROUP, P], F32R)
    rows, pad = sb("rows", [P, SLOT_TILES]), sb("pad", [P, SLOT_TILES])
    past = sb("past", [P, SLOT_TILES, E])
    past_n = sb("past_n", [P, SLOT_TILES])
    lp = ctx.enter_context(nc.psum_tensor("moe_l", [P, 512], F32))
    cp = ctx.enter_context(nc.psum_tensor("moe_c", [P, 2, NT * E], F32))
    tbl = ctx.enter_context(nc.psum_tensor("moe_tbl", [P, 3, TABLE], F32))
    lg_ready, step_v, ex_done = sem("lg_ready"), sem("step_v"), sem("ex_done")
    diff_done, chosen_done, counts_ready = sem("diff_done"), sem("chosen_done"), sem("counts_ready")
    at_tile_done, entry_done = sem("at_tile_done"), sem("entry_done")
    place_done, place_used = sem("place_done"), sem("place_used")
    GROUPS = 2 * NT // PER_GROUP

    def tensor(pe):
        pe.wait_ge(w_in, w_in_n)
        for t in range(NT):
            for k in range(DK):
                mm = nc.tensor.matmul(lp[:, E * t:E * t + E], xnT[:, k, P * t:P * t + P], gw[:, k, :],
                                      start=k == 0, stop=k == DK - 1)
        mm.then_inc(lg_ready, 1)
        pe.wait_ge(chosen_done, 1)
        nc.tensor.matmul(cp[:, 0, :], before, chosen[:, :], start=True, stop=True)
        nc.tensor.matmul(cp[:, 1, :], ones[:, :], chosen[:, :], start=True, stop=True).then_inc(counts_ready, 1)
        pe.wait_ge(entry_done, 2)
        for g in range(GROUPS):
            pe.wait_ge(place_done, g + 1)
            for i in range(PER_GROUP):
                n = PER_GROUP * g + i
                mm = nc.tensor.matmul(tbl[:, :, :], place[:, g % 2, i, :], entry[:, n, :, :],
                                      start=n == 0, stop=n == 2 * NT - 1)
            mm.then_inc(place_used, 1)

    def scalar(act):
        act.wait_ge(diff_done, 1)
        nc.scalar.activation(ex[:, :], den[:, :], ACT.Exp).then_inc(ex_done, 1)

    def vector(dve):
        n = [0]

        def step(ins):
            n[0] += 1
            ins.then_inc(step_v, 1)
            dve.wait_ge(step_v, n[0])

        def each(a, width):
            m = a.shape[-1]
            return a.rearrange("p (n o) -> p n o", o=1).broadcast_to([P, m, width])

        def over(a, count):
            return a.rearrange("p (o w) -> p o w", o=1).broadcast_to([P, count, a.shape[-1]])

        nc.vector.memset(ones[:, :], 1.0)
        dve.wait_ge(lg_ready, 1)
        dve.wait_ge(w_in, w_in_n)
        step(nc.vector.tensor_tensor(lg[:, :, :], lp[:, 0:NT * E].rearrange("p (t e) -> p t e", e=E),
                                     over(gb[:, :], NT), ALU.add))
        for t in range(NT):
            last = nc.vector.max(m8[:, t, :], lg[:, t, :])
        step(last)
        for t in range(NT):
            last = nc.vector.max_index(i8[:, t, :], m8[:, t, :], lg[:, t, :])
        step(last)
        nc.vector.tensor_tensor(den[:, :], m8[:, :, 1], m8[:, :, 0], ALU.subtract).then_inc(diff_done, 1)
        step(nc.vector.tensor_copy(top[:, :, :], i8[:, :, 0:2].rearrange("p t i -> p i t")))
        step(nc.vector.tensor_tensor(hot[:, :, :], over(iota[:, 0:E], 2 * NT),
                                     each(top[:, :, :].rearrange("p i t -> p (i t)"), E), ALU.is_equal))
        step(nc.vector.tensor_tensor(chosen[:, :], hot[:, 0:NT, :].rearrange("p t e -> p (t e)"),
                                     hot[:, NT:2 * NT, :].rearrange("p t e -> p (t e)"), ALU.add))
        nc.vector.sem_inc(chosen_done, 1)
        dve.wait_ge(ex_done, 1)
        step(nc.vector.tensor_scalar(den[:, :], ex[:, :], 1.0, None, ALU.add))
        step(nc.vector.reciprocal(wt[:, 0, :], den[:, :]))
        step(nc.vector.tensor_tensor(wt[:, 1, :], ex[:, :], wt[:, 0, :], ALU.mult))
        wts = wt[:, :, :].rearrange("p i t -> p (i t)")
        step(nc.vector.tensor_copy(w_parts[:, 0, :].bitcast(F32R), wts))
        nc.vector.tensor_tensor(w_parts[:, 1, :].bitcast(F32R), wts, w_parts[:, 0, :], ALU.subtract)
        dve.wait_ge(counts_ready, 1)
        step(nc.vector.tensor_copy(run[:, 0], cp[:, 1, :].rearrange("p (t e) -> p t e", e=E)))
        a, s = 0, 1
        while s < NT:
            nc.vector.tensor_copy(run[:, 1 - a, 0:s, :], run[:, a, 0:s, :])
            step(nc.vector.tensor_tensor(run[:, 1 - a, s:NT, :], run[:, a, s:NT, :], run[:, a, 0:NT - s, :], ALU.add))
            a, s = 1 - a, 2 * s
        step(nc.vector.tensor_scalar(tiles_i[:, 0, :], run[:, a, NT - 1, :], float(P - 1), None, ALU.add))
        step(nc.vector.tensor_scalar(tiles_i[:, 1, :], tiles_i[:, 0, :], 7, None, ALU.logical_shift_right))
        nc.vector.tensor_copy(ends[:, 0, :], tiles_i[:, 1, :])
        step(nc.vector.tensor_copy(tiles[:, :], tiles_i[:, 1, :]))
        b, s = 0, 1
        while s < E:
            nc.vector.tensor_copy(ends[:, 1 - b, 0:s], ends[:, b, 0:s])
            step(nc.vector.tensor_tensor(ends[:, 1 - b, s:E], ends[:, b, s:E], ends[:, b, 0:E - s], ALU.add))
            b, s = 1 - b, 2 * s
        step(nc.vector.tensor_tensor(tiles[:, :], ends[:, b, :], tiles[:, :], ALU.subtract))
        step(nc.vector.tensor_tensor(at[:, :, :], run[:, a], cp[:, 1, :].rearrange("p (t e) -> p t e", e=E), ALU.subtract))
        step(nc.vector.tensor_tensor(at[:, :, :], at[:, :, :], cp[:, 0, :].rearrange("p (t e) -> p t e", e=E), ALU.add))
        step(nc.vector.scalar_tensor_tensor(out=at[:, :, :], in0=over(tiles[:, :], NT), scalar=float(P), in1=at[:, :, :],
                                            op0=ALU.mult, op1=ALU.add))
        nc.vector.tensor_tensor(picked[:, 0:NT, :], hot[:, 0:NT, :], at[:, :, :], ALU.mult)
        step(nc.vector.tensor_tensor(picked[:, NT:2 * NT, :], hot[:, NT:2 * NT, :], at[:, :, :], ALU.mult))
        step(nc.vector.tensor_reduce(slot[:, :], picked[:, :, :], AX.X, ALU.add))
        step(nc.vector.tensor_copy(slot_i[:, 0, :], slot[:, :]))
        step(nc.vector.tensor_scalar(slot_i[:, 1, :], slot_i[:, 0, :], 7, None, ALU.logical_shift_right))
        step(nc.vector.tensor_copy(hi[:, :], slot_i[:, 1, :]))
        step(nc.vector.scalar_tensor_tensor(out=lo[:, :], in0=hi[:, :], scalar=-float(P), in1=slot[:, :],
                                            op0=ALU.mult, op1=ALU.add))
        step(nc.vector.tensor_tensor(at_tile, over(iota[:, 0:TABLE], 2 * NT), each(hi[:, :], TABLE), ALU.is_equal))
        nc.vector.sem_inc(at_tile_done, 1)
        for i in range(2):
            last = nc.vector.tensor_tensor(entry[:, :, 1 + i, :], at_tile, each(w_parts[:, i, :], TABLE), ALU.mult)
        last.then_inc(entry_done, 1)
        for g in range(GROUPS):
            if g >= 2:
                dve.wait_ge(place_used, g - 1)
            nc.vector.tensor_tensor(place[:, g % 2], over(iota, PER_GROUP), each(lo[:, PER_GROUP * g:PER_GROUP * (g + 1)], P),
                                    ALU.is_equal).then_inc(place_done, 1)
        step(nc.vector.tensor_tensor(past[:, :, :], each(iota[:, 0:SLOT_TILES], E), over(ends[:, b, :], SLOT_TILES),
                                     ALU.is_ge))
        step(nc.vector.tensor_reduce(past_n[:, :], past[:, :, :], AX.X, ALU.add))
        step(nc.vector.tensor_scalar(tile_expert, past_n[:, :], float(E - 1), None, ALU.min))
        dve.wait_ge(place_used, GROUPS)
        nc.vector.tensor_copy(weight, tbl[:, 1, 0:SLOT_TILES])
        step(nc.vector.tensor_scalar(rows[:, :], tbl[:, 0, 0:SLOT_TILES], float(B * S), None, ALU.add))
        nc.vector.tensor_tensor(weight, tbl[:, 2, 0:SLOT_TILES], weight, ALU.add)
        step(nc.vector.tensor_scalar(pad[:, :], rows[:, :], float(B * S), slot_no, ALU.is_equal, ALU.mult))
        step(nc.vector.tensor_tensor(pad[:, :], pad[:, :], rows[:, :], ALU.add))
        nc.vector.tensor_copy(scatter_row, pad[:, :])
        step(nc.vector.tensor_scalar(gather_row, pad[:, :], float(B * S - 1), None, ALU.min))

    def gpsimd(pool):
        pool.wait_ge(at_tile_done, 1)
        nc.gpsimd.tensor_tensor(entry[:, :, 0, :], at_tile,
                                token.rearrange("p (n o) -> p n o", o=1).broadcast_to([P, 2 * NT, TABLE]),
                                ALU.mult).then_inc(entry_done, 1)

    return vector, tensor, scalar, gpsimd


def experts(nc, x, ident, stats, route_const, gate_w, gate_b, w1, b1, w2, b2, out):
    MT = FF // P
    HALF = FF // 2
    sem = lambda n: nc.alloc_semaphore(f"moe_{n}")
    xn_rows = nc.dram_tensor("moe_xn_rows", (B * S, D), F32).ap()
    xn_out, x_out = [sem(f"xn_out{i}") for i in range(4)], sem("x_out")
    w_in = sem("w_in")
    e_in = [sem(f"e_in{e}") for e in range(E)]
    XN_KEPT = 8
    HELD_BACK = 3
    with ExitStack() as outer:
        keep = lambda n, s, d=F32: outer.enter_context(nc.sbuf_tensor(f"moe_{n}", s, d))
        w1s, w2s = keep("w1", [P, E, DK, FF]), keep("w2", [P, E, MT, D])
        b1c, b2b = keep("b1", [P, E, MT]), keep("b2", [P, E, D])
        gather_row, scatter_row = keep("gather_row", [P, SLOT_TILES], U32), keep("scatter_row", [P, SLOT_TILES], U32)
        weight, tile_expert = keep("weight", [P, SLOT_TILES]), keep("tile_expert", [P, SLOT_TILES], I32)

        def load_expert(sp, e):
            sp.dma_start(w1s[:, e], w1[e].rearrange("(k p) n -> p k n", p=P)).then_inc(e_in[e], 16)
            sp.dma_start(w2s[:, e], w2[e].rearrange("(k p) n -> p k n", p=P)).then_inc(e_in[e], 16)

        with ExitStack() as ctx:
            sb = lambda n, s, d=F32: ctx.enter_context(nc.sbuf_tensor(f"route_{n}", s, d))
            xn, xn_done, xnT, xnT_done, PAIRS, ln_vector, ln_tensor, ln_scalar = normalized_transposed(
                nc, "moe", ctx, x, ident, stats, XN_KEPT,
                reuse=lambda dve, t: dve.wait_ge(xn_out[(t - XN_KEPT) // 4], 16))
            gw, gb = sb("gw", [P, DK, E]), sb("gb", [P, E])
            rc = sb("const", [P, ROUTE_CONST])
            const = rc[:, 0:P], rc[:, P:2 * P], rc[:, 2 * P:2 * P + 2 * NT], rc[:, 2 * P + 2 * NT:]
            plan = gather_row[:, :], scatter_row[:, :], weight[:, :], tile_expert[:, :]
            route_vector, route_tensor, route_scalar, route_gpsimd = route(nc, ctx, sb, sem, const, xnT, gw, gb, w_in, 80, plan)
            block = ctx.enter_context(nc.Block())

            @block.sync
            def _(sp):
                sp.dma_start(gw[:, :, :], gate_w.rearrange("(k p) n -> p k n", p=P)).then_inc(w_in, 16)
                sp.dma_start(gb[:, :], gate_b.partition_broadcast(P)).then_inc(w_in, 16)
                sp.dma_start(rc[:, :], route_const).then_inc(w_in, 16)
                sp.dma_start(b1c[:, :, :], b1).then_inc(w_in, 16)
                sp.dma_start(b2b[:, :, :], b2.partition_broadcast(P)).then_inc(w_in, 16)
                for e in range(E - HELD_BACK):
                    if e == 0:
                        for stored in xn_out:
                            sp.wait_ge(stored, 16)
                        sp.dma_start(out[0:B * S, :].rearrange("(t p) d -> p t d", p=P), x[:, :, :]).then_inc(x_out, 16)
                        sp.dma_start(out[B * S:, :], x[:, 0, :]).then_inc(x_out, 16)
                    load_expert(sp, e)

            @block.gpsimd
            def _(pool):
                pool.wait_ge(w_in, 80)
                route_gpsimd(pool)

            @block.scalar
            def _(act):
                def store(p):
                    if p in (2, 4, 6, PAIRS):
                        t = 2 * p - 4
                        act.wait_ge(xn_done, t + 4)
                        act.dma_start(xn_rows[P * t:P * t + 4 * P, :].rearrange("(t p) d -> p t d", p=P),
                                      xn[:, t % XN_KEPT:t % XN_KEPT + 4, :]).then_inc(xn_out[t // 4], 16)

                ln_scalar(act, store)
                store(PAIRS)
                route_scalar(act)

            @block.vector
            def _(dve):
                ln_vector(dve)
                route_vector(dve)

            @block.tensor
            def _(pe):
                ln_tensor(pe)
                pe.wait_ge(xnT_done, PAIRS)
                route_tensor(pe)

        with ExitStack() as ctx:
            sb = lambda n, s, d=F32: ctx.enter_context(nc.sbuf_tensor(f"moe_{n}", s, d))
            ps = lambda n, s: ctx.enter_context(nc.psum_tensor(f"tile_{n}", s, F32))
            xg, xT = sb("xg", [P, 2, D]), sb("xT", [P, DK, P])
            g_row, s_row = [sb(f"g_row{i}", [P, 1], U32) for i in range(2)], sb("s_row", [P, 1], U32)
            idle = sb("idle", [P, 8])
            h_in, hT = sb("h_in", [P, FF]), sb("hT", [P, MT, P])
            b1e = sb("b1e", [P, 2, MT])
            y_sum, y_out = sb("y_sum", [P, 2, D]), sb("y_out", [P, 2, D])
            xp, hp, tp, yp = ps("xp", [P, 4, P]), ps("hp", [P, 2, HALF]), ps("tp", [P, MT, P]), ps("yp", [P, D])
            g_in = [sem("g_in0"), sem("g_in1")]
            loaded = sem("loaded")
            added = [sem("added0"), sem("added1")]
            row_step, idle_done = sem("row_step"), sem("idle_done")
            xT_ready, xT_done, h_ready, h_taken = sem("xT_ready"), sem("xT_done"), sem("h_ready"), sem("h_taken")
            hT_ready, hT_done, b1_done = sem("hT_ready"), sem("hT_done"), sem("b1_done")
            y_ready, y_step, y_done = sem("y_ready"), sem("y_step"), sem("y_done")
            block = ctx.enter_context(nc.Block())
            LAST_TILE = SLOT_TILES - 1

            def tiles(engine, body):
                for j in range(3):
                    body(j, j % 2, j // 2)
                with engine.Fori(1, (SLOT_TILES - 5) // 2) as i:
                    body(2 * i + 1, 1, i)
                    body(2 * i + 2, 0, i + 1)
                for j in range(SLOT_TILES - 4, SLOT_TILES):
                    body(j, j % 2, j // 2)

            def col(a, j):
                return a[:, j:j + 1] if isinstance(j, int) else a[:, bass.ds(j, 1)]

            def expert_of(engine, j):
                at = slice(j, j + 1) if isinstance(j, int) else bass.ds(j, 1)
                return engine.value_load(tile_expert[0:1, at], min_val=0, max_val=E - 1)

            @block.sync
            def _(sp):
                for e in range(E):
                    if e == E - HELD_BACK:
                        for i in range(2):
                            sp.wait_ge(g_in[i], 16)
                    if e >= E - HELD_BACK:
                        load_expert(sp, e)
                    sp.wait_ge(e_in[e], 32)
                    sp.sem_inc(loaded, 1)

            @block.gpsimd
            def _(pool):
                def gate(i):
                    return nc.gpsimd.tensor_tensor(idle[:, i:i + 1], idle[:, 0:1], idle[:, 0:1], ALU.mult)

                def gather(j, par):
                    nc.gpsimd.tensor_copy(g_row[par][:, :], col(gather_row, j)).then_inc(row_step, 1)
                    pool.wait_ge(row_step, j + 1 if isinstance(j, int) and j <= 3 else 2 * j - 2)
                    gate(2)
                    nc.gpsimd.indirect_dma_start(xg[:, par, :], None, xn_rows,
                                                 bass.IndirectOffsetOnAxis(ap=g_row[par][:, :], axis=0)).then_inc(g_in[par], 16)

                nc.gpsimd.memset(idle[:, :], 0.0).then_inc(idle_done, 1)
                pool.wait_ge(idle_done, 1)
                for j in range(3):
                    if j == 2:
                        pool.wait_ge(xT_ready, 1)
                        gate(5)
                    gather(j, j % 2)
                pool.wait_ge(x_out, 32)

                def body(j, par, pair):
                    if not isinstance(j, int) or j + 3 < SLOT_TILES:
                        pool.wait_ge(xT_ready, j + 2)
                        gate(1)
                        gather(j + 3, 1 - par)
                    pool.wait_ge(y_done, j + 1)
                    if not isinstance(j, int) or j > 0:
                        pool.wait_ge(added[1 - par], 16 * (pair + par))
                    gate(3)
                    nc.gpsimd.tensor_copy(s_row[:, :], col(scatter_row, j)).then_inc(row_step, 1)
                    pool.wait_ge(row_step, j + 1 + (j + 4 if not isinstance(j, int) or j + 3 < SLOT_TILES else SLOT_TILES))
                    gate(4)
                    nc.gpsimd.indirect_dma_start(out, bass.IndirectOffsetOnAxis(ap=s_row[:, :], axis=0), y_out[:, par, :], None,
                                                 compute_op=ALU.add).then_inc(added[par], 16)

                tiles(pool, body)
                pool.wait_ge(added[0], 16 * ((SLOT_TILES + 1) // 2))
                pool.wait_ge(added[1], 16 * (SLOT_TILES // 2))

            @block.scalar
            def _(act):
                def take_xT(j):
                    act.wait_ge(xT_ready, j + 1)
                    if not (isinstance(j, int) and j == 0):
                        act.wait_ge(h_ready, 2 * j)
                    nc.scalar.copy(xT[:, :, :], xp[:, 0:DK, :]).then_inc(xT_done, 1)

                take_xT(0)

                def body(j, par, pair):
                    e = expert_of(act, j)
                    nc.scalar.copy(b1e[:, par, :], b1c[:, bass.ds(e, 1), :]).then_inc(b1_done, 1)
                    if not isinstance(j, int) or j < LAST_TILE:
                        take_xT(j + 1)
                    act.wait_ge(b1_done, j + 1)
                    if not (isinstance(j, int) and j == 0):
                        act.wait_ge(y_ready, j)
                    for m in range(MT):
                        if m % (MT // 2) == 0:
                            act.wait_ge(hT_ready, 2 * j + 1 + m // (MT // 2))
                        last = nc.scalar.activation(hT[:, m, :], tp[:, m, :], ACT.Gelu, bias=b1e[:, par, m:m + 1])
                        if m % (MT // 2) == MT // 2 - 1:
                            last.then_inc(hT_done, 1)

                tiles(act, body)

            @block.vector
            def _(dve):
                def take_y(j, par, pair):
                    e = expert_of(dve, j)
                    if not (isinstance(j, int) and j < 2):
                        dve.wait_ge(added[par], 16 * pair)
                    dve.wait_ge(y_ready, j + 1)
                    nc.vector.tensor_tensor(y_sum[:, par, :], yp[:, :], b2b[:, bass.ds(e, 1), :].rearrange("p o d -> p (o d)"),
                                            ALU.add).then_inc(y_step, 1)
                    dve.wait_ge(y_step, j + 1)
                    nc.vector.tensor_scalar(y_out[:, par, :], y_sum[:, par, :], col(weight, j), None, ALU.mult).then_inc(y_done, 1)

                def body(j, par, pair):
                    for h in range(2):
                        dve.wait_ge(h_ready, 2 * j + h + 1)
                        if not (isinstance(j, int) and j == 0):
                            dve.wait_ge(hT_ready, 2 * j + h - 1)
                        nc.vector.tensor_copy(h_in[:, HALF * h:HALF * h + HALF], hp[:, h, :]).then_inc(h_taken, 1)
                    if not (isinstance(j, int) and j == 0):
                        take_y(j - 1, 1 - par, pair + par - 1)

                tiles(dve, body)
                take_y(LAST_TILE, LAST_TILE % 2, LAST_TILE // 2)

            @block.tensor
            def _(pe):
                def transpose_x(j, par, pair):
                    pe.wait_ge(g_in[par], 16 * (pair + 1))
                    if not (isinstance(j, int) and j == 0):
                        pe.wait_ge(xT_done, j)
                    for k in range(DK):
                        mm = nc.tensor.transpose(xp[:, k, :], xg[:, par, P * k:P * k + P], ident[:, :])
                    mm.then_inc(xT_ready, 1)

                def down(j, e):
                    pe.wait_ge(hT_done, 2 * j + 2)
                    if not (isinstance(j, int) and j == 0):
                        pe.wait_ge(y_done, j)
                    for m in range(MT):
                        mm = nc.tensor.matmul(yp[:, :], hT[:, m, :], w2s[:, bass.ds(e, 1), m, :],
                                              start=m == 0, stop=m == MT - 1)
                    mm.then_inc(y_ready, 1)

                transpose_x(0, 0, 0)

                def body(j, par, pair):
                    e = expert_of(pe, j)
                    pe.wait_ge(loaded, e + 1)
                    pe.wait_ge(xT_done, j + 1)
                    for h in range(2):
                        if not (isinstance(j, int) and j == 0):
                            pe.wait_ge(h_taken, 2 * j + h - 1)
                        for k in range(DK):
                            mm = nc.tensor.matmul(hp[:, h, :], xT[:, k, :], w1s[:, bass.ds(e, 1), k, HALF * h:HALF * h + HALF],
                                                  start=k == 0, stop=k == DK - 1)
                        mm.then_inc(h_ready, 1)
                    if not isinstance(j, int) or j < LAST_TILE:
                        transpose_x(j + 1, 1 - par, pair + par)
                    if not (isinstance(j, int) and j == 0):
                        down(j - 1, expert_of(pe, j - 1))
                    for h in range(2):
                        pe.wait_ge(h_taken, 2 * j + h + 1)
                        if not (isinstance(j, int) and j == 0):
                            pe.wait_ge(hT_done, 2 * j + h - 1)
                        for m in range(MT // 2 * h, MT // 2 * (h + 1)):
                            mm = nc.tensor.transpose(tp[:, m, :], h_in[:, P * m:P * m + P], ident[:, :])
                        mm.then_inc(hT_ready, 1)

                tiles(pe, body)
                down(LAST_TILE, expert_of(pe, LAST_TILE))


def xattn_ffn_2(nc, ins, out):
    with ExitStack() as ctx:
        sb = lambda n, s: ctx.enter_context(nc.sbuf_tensor(n, s, F32))
        x, ident = sb("x_sb", [P, NT, D]), sb("ident_sb", [P, P])
        stats = sb("stats", [P, NT, 6]), sb("mean_var", [P, NT, 2])
        x_in = [nc.alloc_semaphore(f"x_in{b}") for b in range(B)] + [nc.alloc_semaphore("ident_in")]
        with nc.Block() as block:
            @block.scalar
            def _(act):
                for b in range(B):
                    act.dma_start(x[:, QT * b:QT * b + QT, :],
                                  ins["x"][S * b:S * b + S, :].rearrange("(t p) d -> p t d", p=P)).then_inc(x_in[b], 16)
                    if b == 0:
                        act.dma_start(ident[:, :], ins["ident"]).then_inc(x_in[B], 16)
        stacks = ins["k_rows"], ins["q_rows"], ins["ctxT"]
        weights = [[ins[f"L{i}_{w}"] for w in ("wq", "wk", "wv", "wo")] for i in range(2)]
        arrived = [[nc.alloc_semaphore(f"L{i}_{n}") for n in ("first_in", "weights_in", "ctx_in")] for i in range(2)]
        with ExitStack() as both:
            bufs = [both.enter_context(nc.sbuf_tensor(f"{w}_sb", [P, DK, D], F32)) for w in ("wq", "wk", "wv", "wo")]
            bufs.append(both.enter_context(nc.sbuf_tensor("ctx_sb", [P, DK, KV], F32)))
            attention(nc, "L0", x, x_in, ident, bufs, arrived[0], False, stats, *stacks, *weights[0],
                      ins["L0_bq"], ins["L0_bk"], ins["L0_bv"], ins["L0_bo"], ins["mask"])
            swiglu(nc, x, ident, stats, ins["w_gate"], ins["w_up"], ins["w_down"],
                   lambda sp: load_inputs(sp, bufs, arrived[1], *weights[1], ins["ctxT"]))
            attention(nc, "L1", x, None, ident, bufs, arrived[1], True, stats, *stacks, *weights[1],
                      None, None, None, None, None)
        experts(nc, x, ident, stats, ins["route_const"], ins["gate_w"], ins["gate_b"], ins["w1"], ins["b1"], ins["w2"],
                ins["b2"], out)




def route_constants(np):
    p = np.arange(P, dtype=np.float32)
    rows = p[:, None] + P * np.tile(np.arange(NT, dtype=np.float32), TOP) - B * S
    return np.concatenate([np.tile(p, (P, 1)), np.triu(np.ones((P, P), np.float32), 1), rows, p[:, None]], axis=1)


def kernel(**inputs):
    import numpy as _np
    import concourse.bacc as _bacc
    from concourse import mybir as _mybir
    from concourse.bass_utils import run_bass_kernel_spmd as _run

    a = {n: _np.asarray(v) for n, v in inputs.items()}
    order = _np.array([HD * (HG * g + j) + d for g in range(NG) for d in range(HD) for j in range(HG)])
    wkv, bkv = a["L0_xattn_W_kv"], a["L0_xattn_b_kv"]
    ones = 0x3F803F80
    k_rows = _np.full((3, NG * HG * KVP // 2), ones, _np.uint32)
    k_rows[0] = 0
    arrays = {
        "x": a["x"].reshape(B * S, D),
        "ident": _np.eye(P, dtype=_np.float32),
        "route_const": route_constants(_np),
        "k_rows": k_rows,
        "q_rows": _np.full((3, NG * HG * S // 2), ones, _np.uint32),
        "ctxT": a["ctx_1024"].transpose(0, 2, 1),
        "mask": a["mask_BxS2_bf1"].view(_np.uint8),
        "L0_wq": a["L0_xattn_W_q"][:, order], "L0_wk": wkv[:, :D][:, order], "L0_wv": wkv[:, D:],
        "L0_wo": a["L0_xattn_W_o"],
        "L0_bq": a["L0_xattn_b_q"][order].reshape(2, P).T, "L0_bk": bkv[:D][order].reshape(2, P).T,
        "L0_bv": bkv[D:], "L0_bo": a["L0_xattn_b_o"],
        "w_gate": a["L0_ffn_w_gate"].T, "w_up": a["L0_ffn_w_up"].T, "w_down": a["L0_ffn_w_down"].T,
        "L1_wq": a["L1_xattn_W_q"].T[:, order], "L1_wk": a["L1_xattn_W_k"].T[:, order],
        "L1_wv": a["L1_xattn_W_v"].T, "L1_wo": a["L1_xattn_W_o"].T,
        "gate_w": a["L1_ffn_gate_w"], "gate_b": a["L1_ffn_gate_b"],
        "w1": a["L1_ffn_w1"], "b1": a["L1_ffn_b1"].reshape(E, FF // P, P).transpose(2, 0, 1),
        "w2": a["L1_ffn_w2"], "b2": a["L1_ffn_b2"],
    }
    arrays = {n: _np.ascontiguousarray(v) for n, v in arrays.items()}
    nc = _bacc.Bacc("TRN2", target_bir_lowering=False, num_devices=1)
    ins = {n: nc.dram_tensor(f"in_{n}", v.shape, _mybir.dt.from_np(v.dtype), kind="ExternalInput").ap()
           for n, v in arrays.items()}
    out = nc.dram_tensor("out", (B * S + P, D), F32, kind="ExternalOutput").ap()
    xattn_ffn_2(nc, ins, out)
    r = _run(nc, [{f"in_{n}": v for n, v in arrays.items()}], core_ids=[0])
    return _np.asarray(r.results[0]["out"])[:B * S].reshape(B, S, D)
```
